# Optimizing a Trainium2 kernel written in Bass

```python
import numpy as np
import jax
import jax.numpy as jnp

def _softmax(x, axis=-1):
    return jax.nn.softmax(x, axis=axis)

def _gelu(x):
    return jax.nn.gelu(x, approximate=True)

def _silu(x):
    return jax.nn.silu(x)

def _sigmoid(x):
    return jax.nn.sigmoid(x)

def _layernorm(x, axis=-1, eps=1e-05):
    m = jnp.mean(x, axis=axis, keepdims=True)
    v = jnp.var(x, axis=axis, keepdims=True)
    return (x - m) / jnp.sqrt(v + eps)

def _scatter_add(tgt, idx, src, axis=0):
    return tgt.at[idx].add(src)

def _segment_sum(src, seg, n):
    return jax.ops.segment_sum(src, seg, n)
kernel_name = 'mk_sandwich_d2_jaxref_r8_e1aa6a'

def setup_inputs(seed: int=0):
    np.random.seed(seed)
    _w = jnp.asarray

    def _L0_attn_setup():
        import jax, jax.numpy as jnp
        import numpy as np
        HIDDEN = 512
        HEADS = 32
        D_K = HIDDEN // HEADS
        key = jax.random.key(seed)
        ks = jax.random.split(key, 5)
        scale = 1.0 / np.sqrt(HIDDEN)
        x = jax.random.normal(ks[0], (2, 256, HIDDEN), dtype=jnp.float32)
        w_q = jax.random.uniform(ks[1], (HIDDEN, HIDDEN), jnp.float32, -scale, scale)
        w_k = jax.random.uniform(ks[2], (HIDDEN, HIDDEN), jnp.float32, -scale, scale)
        w_v = jax.random.uniform(ks[3], (HIDDEN, HIDDEN), jnp.float32, -scale, scale)
        w_o = jax.random.uniform(ks[4], (HIDDEN, HIDDEN), jnp.float32, -scale, scale)
        return {'x': x, 'w_q': w_q, 'w_k': w_k, 'w_v': w_v, 'w_o': w_o}
    _L0_attn_in = _L0_attn_setup()

    def _L0_ffn_setup():
        import jax, jax.numpy as jnp
        import numpy as np
        D_MODEL = 512
        D_FF = 1376

        def _dequant_matmul(x, w_int, s):
            w = w_int.astype(jnp.float32) * s
            return x @ w.T
        key = jax.random.key(seed)
        ks = jax.random.split(key, 7)
        x = jax.random.normal(ks[0], (4, 256, D_MODEL), dtype=jnp.float32)
        gate_w = jax.random.randint(ks[1], (D_FF, D_MODEL), -128, 128, dtype=jnp.int32)
        up_w = jax.random.randint(ks[2], (D_FF, D_MODEL), -128, 128, dtype=jnp.int32)
        down_w = jax.random.randint(ks[3], (D_MODEL, D_FF), -128, 128, dtype=jnp.int32)
        gate_s = jax.random.uniform(ks[4], (D_FF, 1), dtype=jnp.float32) * 0.01
        up_s = jax.random.uniform(ks[5], (D_FF, 1), dtype=jnp.float32) * 0.01
        down_s = jax.random.uniform(ks[6], (D_MODEL, 1), dtype=jnp.float32) * 0.01
        return {'x': x, 'gate_w': gate_w, 'gate_s': gate_s, 'up_w': up_w, 'up_s': up_s, 'down_w': down_w, 'down_s': down_s}
    _L0_ffn_in = _L0_ffn_setup()

    def _L1_attn_setup():
        import math
        import jax, jax.numpy as jnp
        import numpy as np
        NUM_HEADS = 32
        HIDDEN = 512
        HEAD_DIM = HIDDEN // NUM_HEADS
        NEG_INF = -1e+30

        def _alibi_slopes(n: int) -> jnp.ndarray:
            cp2 = 2 ** math.floor(math.log2(n))
            base = 2.0 ** (-2.0 ** (-(math.log2(cp2) - 3)))
            slopes = base ** np.arange(1, cp2 + 1, dtype=np.float64)
            if cp2 != n:
                extra_base = 2.0 ** (-2.0 ** (-(math.log2(2 * cp2) - 3)))
                rem = min(cp2, n - cp2)
                extra = extra_base ** np.arange(1, 1 + 2 * rem, 2, dtype=np.float64)
                slopes = np.concatenate([slopes, extra])
            return jnp.asarray(slopes, dtype=jnp.float32)
        key = jax.random.key(seed)
        k1, k2, k3 = jax.random.split(key, 3)
        B, S = (2, 256)
        hidden_states = jax.random.normal(k1, (B, S, HIDDEN), dtype=jnp.float32)
        Wqkv = jax.random.normal(k2, (HIDDEN, NUM_HEADS * HEAD_DIM + 2 * HEAD_DIM), dtype=jnp.float32) * 0.02
        Wo = jax.random.normal(k3, (HIDDEN, HIDDEN), dtype=jnp.float32) * 0.02
        return {'hidden_states': hidden_states, 'Wqkv': Wqkv, 'Wo': Wo}
    _L1_attn_in = _L1_attn_setup()

    def _L1_ffn_setup():
        import jax, jax.numpy as jnp
        import numpy as np
        C_CLAMP = 0.5
        EPS = 1e-06
        key = jax.random.key(seed)
        ks = jax.random.split(key, 6)
        B_, S, D, O, R, E = (4, 256, 512, 512, 16, 8)
        x = jax.random.normal(ks[0], (B_, S, D), dtype=jnp.float32)
        W = jax.random.normal(ks[1], (O, D), dtype=jnp.float32) * (1.0 / np.sqrt(D))
        b = jax.random.normal(ks[2], (O,), dtype=jnp.float32) * 0.01
        A = jax.random.normal(ks[3], (E, D, R), dtype=jnp.float32) * (1.0 / np.sqrt(D))
        Bm = jax.random.normal(ks[4], (E, R, O), dtype=jnp.float32) * (1.0 / np.sqrt(R))
        p_scores = jax.random.uniform(ks[5], (E,), dtype=jnp.float32)
        return {'x': x, 'W': W, 'b': b, 'A': A, 'B': Bm, 'p_scores': p_scores}
    _L1_ffn_in = _L1_ffn_setup()
    _d = {'L0_attn_x': _L0_attn_in['x'], 'L0_attn_w_q': _L0_attn_in['w_q'], 'L0_attn_w_k': _L0_attn_in['w_k'], 'L0_attn_w_v': _L0_attn_in['w_v'], 'L0_attn_w_o': _L0_attn_in['w_o'], 'L0_ffn_gate_w': _L0_ffn_in['gate_w'], 'L0_ffn_gate_s': _L0_ffn_in['gate_s'], 'L0_ffn_up_w': _L0_ffn_in['up_w'], 'L0_ffn_up_s': _L0_ffn_in['up_s'], 'L0_ffn_down_w': _L0_ffn_in['down_w'], 'L0_ffn_down_s': _L0_ffn_in['down_s'], 'L1_attn_Wqkv': _L1_attn_in['Wqkv'], 'L1_attn_Wo': _L1_attn_in['Wo'], 'L1_ffn_W': _L1_ffn_in['W'], 'L1_ffn_b': _L1_ffn_in['b'], 'L1_ffn_A': _L1_ffn_in['A'], 'L1_ffn_B': _L1_ffn_in['B'], 'L1_ffn_p_scores': _L1_ffn_in['p_scores']}
    _x0 = _d['L0_attn_x']
    _d['L0_attn_x'] = jax.random.normal(jax.random.fold_in(jax.random.key(seed), 1), (2, 1024, 512), dtype=_x0.dtype)
    del _x0
    return _d

def reference(L0_attn_x, L0_attn_w_q, L0_attn_w_k, L0_attn_w_v, L0_attn_w_o, L0_ffn_gate_w, L0_ffn_gate_s, L0_ffn_up_w, L0_ffn_up_s, L0_ffn_down_w, L0_ffn_down_s, L1_attn_Wqkv, L1_attn_Wo, L1_ffn_W, L1_ffn_b, L1_ffn_A, L1_ffn_B, L1_ffn_p_scores):

    def _L0_attn_ref(x, w_q, w_k, w_v, w_o):
        import jax, jax.numpy as jnp
        import numpy as np
        HIDDEN = 512
        HEADS = 32
        D_K = HIDDEN // HEADS
        B, S, _ = x.shape

        def proj(w):
            y = jnp.einsum('bsd,ed->bse', x, w)
            return y.reshape(B, S, HEADS, D_K).transpose(0, 2, 1, 3)
        q, k, v = (proj(w_q), proj(w_k), proj(w_v))
        scores = jnp.einsum('bhqd,bhkd->bhqk', q, k) / jnp.sqrt(jnp.float32(D_K))
        attn = jax.nn.softmax(scores, axis=-1)
        out = jnp.einsum('bhqk,bhkd->bhqd', attn, v)
        out = out.transpose(0, 2, 1, 3).reshape(B, S, HIDDEN)
        return jnp.einsum('bse,oe->bso', out, w_o)

    def _L0_ffn_ref(x, gate_w, gate_s, up_w, up_s, down_w, down_s):
        import jax, jax.numpy as jnp
        import numpy as np
        D_MODEL = 512
        D_FF = 1376

        def _dequant_matmul(x, w_int, s):
            w = w_int.astype(jnp.float32) * s
            return x @ w.T
        batch, seq_len, hidden = x.shape
        x_flat = x.reshape(-1, hidden).astype(jnp.float32)
        gate = _dequant_matmul(x_flat, gate_w, gate_s)
        up = _dequant_matmul(x_flat, up_w, up_s)
        h = jax.nn.silu(gate) * up
        out = _dequant_matmul(h, down_w, down_s)
        return out.astype(x.dtype).reshape(batch, seq_len, hidden)

    def _L1_attn_ref(hidden_states, Wqkv, Wo):
        import math
        import jax, jax.numpy as jnp
        import numpy as np
        NUM_HEADS = 32
        HIDDEN = 512
        HEAD_DIM = HIDDEN // NUM_HEADS
        NEG_INF = -1e+30

        def _alibi_slopes(n: int) -> jnp.ndarray:
            cp2 = 2 ** math.floor(math.log2(n))
            base = 2.0 ** (-2.0 ** (-(math.log2(cp2) - 3)))
            slopes = base ** np.arange(1, cp2 + 1, dtype=np.float64)
            if cp2 != n:
                extra_base = 2.0 ** (-2.0 ** (-(math.log2(2 * cp2) - 3)))
                rem = min(cp2, n - cp2)
                extra = extra_base ** np.arange(1, 1 + 2 * rem, 2, dtype=np.float64)
                slopes = np.concatenate([slopes, extra])
            return jnp.asarray(slopes, dtype=jnp.float32)
        B, S, H = hidden_states.shape
        nH, d = (NUM_HEADS, HEAD_DIM)
        scale = d ** (-0.5)
        qkv = hidden_states @ Wqkv
        q = qkv[..., :nH * d].reshape(B, S, nH, d)
        k = qkv[..., nH * d:nH * d + d]
        v = qkv[..., nH * d + d:]
        scores = jnp.einsum('bqhd,bkd->bhqk', q, k) * scale
        pos_q = jnp.arange(S)[:, None]
        pos_k = jnp.arange(S)[None, :]
        slopes = _alibi_slopes(nH)
        alibi = slopes[:, None, None] * (pos_k - pos_q).astype(jnp.float32)
        causal = pos_k <= pos_q
        scores = jnp.where(causal[None, None], scores + alibi[None], NEG_INF)
        probs = jax.nn.softmax(scores, axis=-1)
        attn = jnp.einsum('bhqk,bkd->bqhd', probs, v).reshape(B, S, H)
        return attn @ Wo

    def _L1_ffn_ref(x, W, b, A, B, p_scores):
        import jax, jax.numpy as jnp
        import numpy as np
        C_CLAMP = 0.5
        EPS = 1e-06
        z = jnp.einsum('bsd,od->bso', x, W) + b
        u = jnp.einsum('bsd,edr->ebsr', x, A)
        m = jnp.einsum('ebsr,ero,e->bso', u, B, p_scores)
        norm_z = jnp.linalg.norm(z, axis=-1, keepdims=True)
        norm_m = jnp.linalg.norm(m, axis=-1, keepdims=True)
        gamma = jnp.minimum(C_CLAMP * norm_z / (norm_m + EPS), 1.0)
        return z + gamma * m
    x = L0_attn_x
    x = x + _layernorm(_L0_attn_ref(_layernorm(x, axis=-1), L0_attn_w_q, L0_attn_w_k, L0_attn_w_v, L0_attn_w_o), axis=-1)
    x = x + _layernorm(_L0_ffn_ref(_layernorm(x, axis=-1), L0_ffn_gate_w, L0_ffn_gate_s, L0_ffn_up_w, L0_ffn_up_s, L0_ffn_down_w, L0_ffn_down_s), axis=-1)
    x = x + _layernorm(_L1_attn_ref(_layernorm(x, axis=-1), L1_attn_Wqkv, L1_attn_Wo), axis=-1)
    x = x + _layernorm(_L1_ffn_ref(_layernorm(x, axis=-1), L1_ffn_W, L1_ffn_b, L1_ffn_A, L1_ffn_B, L1_ffn_p_scores), axis=-1)
    return x

_drawn_inputs = setup_inputs


def setup_inputs(seed=0):
    import zlib

    import numpy as np

    out = dict(_drawn_inputs(seed))
    spreads = {}
    factors = {'L1_ffn_b': 8.0}
    for name, (base, spread) in spreads.items():
        noise = np.random.default_rng([zlib.crc32(name.encode()), seed]).standard_normal(out[name].shape)
        drawn = base * np.exp(spread * noise) if base else spread * noise
        out[name] = jnp.asarray(drawn.astype(out[name].dtype))
    for name, factor in factors.items():
        out[name] = (out[name] * factor).astype(out[name].dtype)
    return out
```

```python
from contextlib import ExitStack

import numpy as np

import concourse.bass as bass
from concourse import mybir

F32 = mybir.dt.float32
BF16 = mybir.dt.bfloat16
I32 = mybir.dt.int32
ALU = mybir.AluOpType
ACT = mybir.ActivationFunctionType
AX = mybir.AxisListType

P = 128
BATCH, SEQ, D = 2, 1024, 512
TOK = BATCH * SEQ
NT = TOK // P
DC = D // P
BLK = 512
NB = TOK // BLK
TB = BLK // P
HEADS, HD = 32, 16
GH = 4
NG = HEADS // GH
ITS = BATCH * NG
HALF = 512
KT = SEQ // P
QT = HALF // P
SCALE = HD ** -0.5
FF = 1376
FT = -(-FF // P)
FLAST = FF - (FT - 1) * P
LN_EPS = 1e-5
ER = 128
CLAMP, NORM_EPS = 0.5, 1e-6

Q_PARTS = (0, 0, 0, 1, 1, 2)
K_PARTS = (0, 1, 2, 0, 1, 0)
MAIN = HD * len(Q_PARTS)
ALIBI = 9
SHIFT = 3


def widths(causal, half):
    out = []
    for kt in range(KT):
        first = kt * P - half * HALF
        if causal and first >= HALF:
            break
        diagonal = causal and first >= 0
        out.append((first if diagonal else 0, diagonal))
    return out


class Norm:

    def __init__(self, sb, ps, sems, tag):
        self.xn = sb(f"xn{tag}", [P, TB, D], F32)
        self.xnT = sb(f"xnT{tag}", [P, 2, DC, BLK], F32)
        self.stats = sb(f"stats{tag}", [P, TB, 6], F32)
        self.mv = sb(f"mv{tag}", [P, TB, 2], F32)
        self.rstd = sb(f"rstd{tag}", [P, TB], F32)
        self.tp = ps(f"tp_ps{tag}", [P, 2, DC, P], F32)
        self.summed, self.meaned, self.padded, self.rooted, self.inverted, self.normed = (
            sems(n) for n in ("ln_stats", "ln_mean", "ln_var_eps", "ln_root", "ln_rstd", "ln_out"))
        self.turned, self.ready, self.passed = sems("xn_turned"), sems("xnT_ready"), sems("ln_passed")


def settle(engine, passed):
    engine.sem_inc(passed, 1)


def x_tile(x_sb, t):
    if isinstance(t, int):
        return x_sb[:, t, :]
    return x_sb[:, bass.ds(t, 1), :].rearrange("p a d -> p (a d)")


def norm_vector(dve, n, x_sb, nb, first):
    for i in range(TB):
        dve.bn_stats(n.stats[:, i, :], x_tile(x_sb, TB * nb + i)).then_inc(n.summed, 1)
    dve.wait_ge(n.summed, TB * (nb + 1))
    settle(dve, n.passed)
    for i in range(TB):
        dve.bn_aggr(n.mv[:, i, :], n.stats[:, i, :]).then_inc(n.meaned, 1)
    dve.wait_ge(n.meaned, TB * (nb + 1))
    dve.tensor_scalar(n.mv[:, :, 1], n.mv[:, :, 1], LN_EPS, None, ALU.add).then_inc(n.padded, 1)
    dve.wait_ge(n.rooted, nb + 1)
    dve.reciprocal(n.rstd[:, :], n.rstd[:, :]).then_inc(n.inverted, 1)
    dve.wait_ge(n.inverted, nb + 1)
    if not first:
        dve.wait_ge(n.turned, TB * nb)
    for i in range(TB):
        dve.tensor_scalar(n.xn[:, i, :], x_tile(x_sb, TB * nb + i), n.mv[:, i, 0:1], n.rstd[:, i:i + 1],
                          ALU.subtract, ALU.mult).then_inc(n.normed, 1)


def norm_root(act, n, nb):
    act.wait_ge(n.padded, nb + 1)
    act.activation(n.rstd[:, :], n.mv[:, :, 1], ACT.Sqrt).then_inc(n.rooted, 1)


def norm_turn(pe, n, ident, nb):
    for i in range(TB):
        pe.wait_ge(n.normed, TB * nb + i + 1)
        if not (isinstance(nb, int) and nb == 0 and i < 2):
            pe.wait_ge(n.ready, TB * nb + i - 1)
        for c in range(DC):
            ins = pe.transpose(n.tp[:, i % 2, c, :], n.xn[:, i, c * P:(c + 1) * P], ident[:, :])
        ins.then_inc(n.turned, 1)


def norm_copy(act, n, nb, par):
    for i in range(TB):
        act.wait_ge(n.turned, TB * nb + i + 1)
        act.activation(n.xnT[:, par, :, i * P:(i + 1) * P], n.tp[:, i % 2, :, :],
                       ACT.Copy).then_inc(n.ready, 1)


class Residual:

    def __init__(self, sb, sems, tag):
        self.stats = sb(f"ystats{tag}", [P, 6], F32)
        self.mv = sb(f"ymv{tag}", [P, 2], F32)
        self.rstd = sb(f"yrstd{tag}", [P, 1], F32)
        self.yn = sb(f"yn{tag}", [P, 2, D], F32)
        self.summed, self.meaned, self.padded, self.rooted, self.inverted, self.normed, self.added = (
            sems(n) for n in ("y_stats", "y_mean", "y_var_eps", "y_root", "y_rstd", "y_normed", "x_added"))


def residual_vector(dve, r, y, t, par, first):
    dve.bn_stats(r.stats[:, :], y).then_inc(r.summed, 1)
    dve.wait_ge(r.summed, t + 1)
    dve.bn_aggr(r.mv[:, :], r.stats[:, :]).then_inc(r.meaned, 1)
    dve.wait_ge(r.meaned, t + 1)
    dve.tensor_scalar(r.mv[:, 1:2], r.mv[:, 1:2], LN_EPS, None, ALU.add).then_inc(r.padded, 1)
    dve.wait_ge(r.rooted, t + 1)
    dve.reciprocal(r.rstd[:, :], r.rstd[:, :]).then_inc(r.inverted, 1)
    dve.wait_ge(r.inverted, t + 1)
    if not first:
        dve.wait_ge(r.added, t - 1)
    dve.tensor_scalar(r.yn[:, par, :], y, r.mv[:, 0:1], r.rstd[:, :], ALU.subtract,
                      ALU.mult).then_inc(r.normed, 1)


def residual_root(act, r, t):
    act.wait_ge(r.padded, t + 1)
    act.activation(r.rstd[:, :], r.mv[:, 1:2], ACT.Sqrt).then_inc(r.rooted, 1)


def residual_add(pool, r, x_sb, t, par):
    pool.wait_ge(r.normed, t + 1)
    pool.tensor_tensor(x_tile(x_sb, t), x_tile(x_sb, t), r.yn[:, par, :], ALU.add).then_inc(r.added, 1)


def project(nc, sb, ps, sems, tag, x_sb, ident, w_aps, outputs, first_loads=None, constants=()):
    n_out = len(outputs)
    splits = [u for u, o in enumerate(outputs) if o[0] == "split"]
    vs = [u for u, o in enumerate(outputs) if o[0] == "v"]
    ns, nv = len(splits), len(vs)
    n = Norm(sb, ps, sems, tag)
    parts = sb(f"parts{tag}", [P, ns, 3, BLK], BF16)
    rest = sb(f"rest{tag}", [P, ns, BLK], F32)
    vout = sb(f"vout{tag}", [P, TB, D if nv == TB else outputs[vs[0]][3]], F32)
    w = {k: sb(f"w_{k}{tag}", [P, DC, ap.shape[1]], F32) for k, ap in w_aps.items()}
    acc = ps(f"acc_ps{tag}", [P, 6, BLK], F32)
    x_loaded, w_loaded, made = sems("x_loaded"), sems("w_loaded"), sems("product_made")
    passed = sems("pool_passed")
    hi_out, rest_out, mid_out, low_out = (sems(k) for k in (
        "part0_ready", "rest_ready", "part1_ready", "parts_ready"))
    v_out, stored, const_loaded = sems("v_ready"), sems("stored"), sems("constants_loaded")

    def bank_free(u, nb, first):
        if u < 6 and first:
            return None
        q, b = (u - 6, nb) if u >= 6 else (n_out + u - 6, nb - 1)
        return (rest_out, b * ns + splits.index(q) + 1) if q in splits else (v_out, b * nv + vs.index(q) + 1)

    with nc.Block() as block:
        @block.sync
        def _(sp):
            for dst, src in constants:
                sp.dma_start(dst, src).then_inc(const_loaded, 16)
            for c in range(NB if first_loads else 0):
                dst, src = first_loads(c)
                if c:
                    sp.wait_ge(x_loaded, 16 * c)
                sp.dma_start(dst, src).then_inc(x_loaded, 16)
                if c == 0:
                    for k, ap in w_aps.items():
                        sp.dma_start(w[k][:, :, :], ap.rearrange("(c p) e -> p c e", p=P)).then_inc(w_loaded, 16)
            if not first_loads:
                for k, ap in w_aps.items():
                    sp.dma_start(w[k][:, :, :], ap.rearrange("(c p) e -> p c e", p=P)).then_inc(w_loaded, 16)

            def store(nb, first):
                for u, o in enumerate(outputs):
                    if u in splits:
                        s = splits.index(u)
                        sp.wait_ge(low_out, nb * ns + s + 1)
                        src = parts[o[3]:o[3] + o[4], s, :, :]
                    else:
                        s = vs.index(u)
                        sp.wait_ge(v_out, nb * nv + s + 1)
                        src = vout[:, :, :] if o[4] else vout[:, s, :].rearrange("p (g c) -> p g c", g=NG)
                    if not (first and u == 0):
                        sp.wait_ge(stored, 16 * (nb * n_out + u))
                    sp.dma_start(o[-1](nb, s), src).then_inc(stored, 16)

            store(0, True)
            with sp.Fori(1, NB) as nb:
                store(nb, False)
            sp.wait_ge(stored, 16 * NB * n_out)

        @block.vector
        def _(dve):
            def rests(nb, first):
                for s, u in enumerate(splits):
                    o = outputs[u]
                    rows = slice(o[3], o[3] + o[4])
                    dve.wait_ge(hi_out, nb * ns + s + 1)
                    if not first:
                        dve.wait_ge(low_out, (nb - 1) * ns + s + 1)
                    dve.scalar_tensor_tensor(out=rest[rows, s, :], in0=acc[rows, u % 6, :], scalar=o[5],
                                             in1=parts[rows, s, 0, :], op0=ALU.mult, op1=ALU.subtract
                                             ).then_inc(rest_out, 1)

            def step(nb, first, last):
                if not last:
                    if first_loads:
                        dve.wait_ge(x_loaded, 16 * (nb + 2))
                    norm_vector(dve, n, x_sb, nb + 1, False)
                rests(nb, first)

            if first_loads:
                dve.wait_ge(x_loaded, 16)
            norm_vector(dve, n, x_sb, 0, True)
            step(0, True, False)
            with dve.Fori(1, NB - 1) as nb:
                step(nb, False, False)
            step(NB - 1, False, True)

        @block.gpsimd
        def _(pool):
            with pool.Fori(0, NB) as nb:
                for s, u in enumerate(splits):
                    o = outputs[u]
                    rows = slice(o[3], o[3] + o[4])
                    if o[4] < P:
                        pool.wait_ge(low_out, nb * ns + s)
                    pool.wait_ge(rest_out, nb * ns + s + 1)
                    settle(pool, passed)
                    pool.tensor_copy(parts[rows, s, 1, :], rest[rows, s, :]).then_inc(mid_out, 1)
                    pool.wait_ge(mid_out, nb * ns + s + 1)
                    pool.tensor_tensor(parts[rows, s, 2, :], rest[rows, s, :], parts[rows, s, 1, :],
                                       ALU.subtract).then_inc(low_out, 1)
                    if o[4] < P:
                        pool.wait_ge(low_out, nb * ns + s + 1)
                        settle(pool, passed)

        @block.scalar
        def _(act):
            def copies(nb, us, first):
                for u in us:
                    o = outputs[u]
                    act.wait_ge(made, nb * n_out + u + 1)
                    if not first:
                        act.wait_ge(stored, 16 * ((nb - 1) * n_out + u + 1))
                    if u in splits:
                        rows = slice(o[3], o[3] + o[4])
                        act.activation(parts[rows, splits.index(u), 0, :], acc[rows, u % 6, :], ACT.Copy,
                                       scale=o[5]).then_inc(hi_out, 1)
                    elif o[4]:
                        act.activation(vout[:, :, :], acc[:, u % 6, 0:TB * o[3]].rearrange(
                            "p (t c) -> p t c", t=TB), ACT.Copy).then_inc(v_out, 1)
                    else:
                        act.activation(vout[:, vs.index(u), :], acc[:, u % 6, :], ACT.Copy).then_inc(v_out, 1)

            norm_root(act, n, 0)
            norm_copy(act, n, 0, 0)
            for nb in range(NB):
                if nb < NB - 1:
                    norm_root(act, n, nb + 1)
                copies(nb, range(0, 4), nb == 0)
                if nb < NB - 1:
                    norm_copy(act, n, nb + 1, (nb + 1) % 2)
                copies(nb, range(4, n_out), nb == 0)

        @block.tensor
        def _(pe):
            def products(nb, par, us, first):
                for u in us:
                    o = outputs[u]
                    old = bank_free(u, nb, first)
                    if old:
                        pe.wait_ge(*old)
                    bank = acc[:, u % 6, :]
                    if u in splits:
                        for c in range(DC):
                            ins = pe.matmul(bank, w[o[1]][:, c, o[2]:o[2] + P], n.xnT[:, par, c, :],
                                            start=c == 0, stop=c == DC - 1)
                    else:
                        for k, t in enumerate(range(TB) if o[4] else [vs.index(u)]):
                            for c in range(DC):
                                ins = pe.matmul(bank[:, k * o[3]:(k + 1) * o[3]],
                                                n.xnT[:, par, c, t * P:(t + 1) * P],
                                                w[o[1]][:, c, o[2]:o[2] + o[3]],
                                                start=c == 0, stop=c == DC - 1)
                    ins.then_inc(made, 1)

            if constants:
                pe.wait_ge(const_loaded, 16 * len(constants))
            norm_turn(pe, n, ident, 0)
            pe.wait_ge(w_loaded, 16 * len(w_aps))
            for nb in range(NB):
                pe.wait_ge(n.ready, TB * (nb + 1))
                products(nb, nb % 2, range(0, 4), nb == 0)
                if nb < NB - 1:
                    norm_turn(pe, n, ident, nb + 1)
                products(nb, nb % 2, range(4, n_out), nb == 0)


def attention(nc, sb, ps, sems, tag, causal, qparts, kparts, vrows, ot, ident, ident_bf, mask_q, mask_k, fixed_k, bias_q):
    bias_rows = ALIBI if causal else 0
    top = MAIN + bias_rows
    rows = top + SHIFT
    kh = 1 if causal else GH
    qst = sb(f"q_stack{tag}", [rows, 3, 2, GH, HALF], BF16)
    kst = sb(f"k_stack{tag}", [rows, 3, kh, SEQ], BF16)
    vload = sb(f"v_load{tag}", [P, KT, kh, HD], F32)
    vone = sb(f"v_ones{tag}", [P, KT, kh, 2 * HD], F32)
    probs = sb(f"probs{tag}", [P, 16, HALF], F32)
    maxes = sb(f"maxes{tag}", [P, 2, GH * QT], F32)
    mrow = sb(f"mrow{tag}", [GH * QT, P], F32)
    mneg = sb(f"mneg{tag}", [GH * QT, P], F32)
    mrest = sb(f"mrest{tag}", [GH * QT, P], F32)
    mparts = sb(f"mparts{tag}", [GH * QT, 3, P], BF16)
    s_ps = ps(f"s_ps{tag}", [P, 2, SEQ], F32)
    st_ps = ps(f"st_ps{tag}", [P, 3, HALF], F32)
    o_ps = ps(f"o_ps{tag}", [P, HALF], F32)

    stacks, v_in, v_set, fixed = sems("stacks_loaded"), sems("v_loaded"), sems("v_spread"), sems("fixed_rows")
    scored, maxed = sems("row_scores_ready"), sems("row_max_ready")
    st_made, st_used = sems("key_scores_ready"), sems("key_scores_used")
    m_neg, m_part0, m_rest, m_part1, m_parts, m_rows = (sems(n) for n in (
        "max_negated", "max_part0", "max_rest", "max_part1", "max_parts_ready", "max_rows_ready"))
    pv_done, o_out = sems("probs_used"), sems("o_copied")
    passed, sp_passed = sems("pool_passed"), sems("sp_passed")

    steps = [(half, kt, *w) for half in range(2) for kt, w in enumerate(widths(causal, half))]
    n_steps = len(steps)
    first_of = [next(i for i, s in enumerate(steps) if s[0] == half) for half in range(2)]
    row_units = [[(half, qt, h) for qt in range(QT) for h in range(GH)] for half in range(2)]
    units_at = [[] for _ in steps]
    for half in range(2):
        mine = [i for i, s in enumerate(steps) if s[0] == half]
        for n, unit in enumerate(row_units[half]):
            units_at[mine[n * len(mine) // len(row_units[half])]].append((half * GH * QT + n, *unit))
    takes = []
    for i, s in enumerate(steps):
        takes += [("exp", i, h) for h in range(GH)]
        if i == first_of[s[0]] + 1:
            takes.append(("max", s[0], 0))
    where = {t: n for n, t in enumerate(takes)}
    n_takes = len(takes)

    def is_last(it, k=1):
        return isinstance(it, int) and it >= ITS - k

    def bank_of(n):
        return n % 3

    skipped = where[("max", 1, 0)]

    def taken(it, n):
        return 1 + n_takes * it + n + 1 - (1 if is_last(it) and n >= skipped else 0)

    def used_before(it, n):
        m = max(x for x in range(-n_takes, n) if bank_of(x % n_takes) == bank_of(n)
                and not (is_last(it) and x == skipped))
        if m < 0:
            return max(1 + n_takes * it + m + 1, 1) if isinstance(it, int) else 1 + n_takes * it + m + 1
        return taken(it, m)

    def max_take(n):
        group, half = n
        if half == 1:
            return taken(group, where[("max", 0, 0)])
        if isinstance(group, int) and group == 0:
            return 1
        return taken(group - 1, where[("max", 1, 0)])

    ring = 4
    n_loads = 16 * (3 * len(Q_PARTS) + (2 if causal else 0))
    loop = range(1, ITS - 3)
    assert len(loop) % 3 == 0 and n_steps % ring == 0

    def run(engine, body):
        body(0, 0, False)
        with engine.Fori(0, len(loop) // 3) as i:
            for r in range(3):
                body(3 * i + 1 + r, (1 + r) % 3, True)
        for it in range(ITS - 3, ITS):
            body(it, it % 3, True)

    def key_width(half, qt):
        return (half * QT + qt + 1) * P if causal else SEQ

    with nc.Block() as block:
        @block.sync
        def _(sp):
            def load_stacks(it, buf):
                for r, (a, b) in enumerate(zip(Q_PARTS, K_PARTS)):
                    dst = slice(HD * r, HD * r + HD)
                    for half in range(2):
                        sp.dma_start(qst[dst, buf, half, :, :], qparts(a, it, half)).then_inc(stacks, 16)
                    sp.dma_start(kst[dst, buf, :, :], kparts(b, it)).then_inc(stacks, 16)
                if causal:
                    for half in range(2):
                        sp.dma_start(qst[MAIN:top, buf, half, :, :], bias_q(it, half)).then_inc(stacks, 16)

            def load_v(it):
                sp.dma_start(vload[:, :, :, :].rearrange("p k h d -> p k (h d)"), vrows(it)).then_inc(v_in, 16)

            def max_rows(n, half, buf):
                sp.wait_ge(m_parts, n + 1)
                for p in range(SHIFT):
                    sp.dma_start(qst[top + p:top + p + 1, buf, half, :, :].rearrange(
                        "r h (q c) -> r (h q) c", c=P), mparts[:, p, :]).then_inc(m_rows, 16)

            def body(it, buf, before):
                if before:
                    sp.wait_ge(st_made, 1 + n_takes * it)
                if not is_last(it, 2):
                    sp.wait_ge(stacks, n_loads * (it + 2))
                    settle(sp, sp_passed)
                    load_stacks(it + 2, (buf + 2) % 3)
                if not is_last(it):
                    sp.wait_ge(v_set, it + 2)
                    settle(sp, sp_passed)
                    load_v(it + 1)
                max_rows(2 * it + 1, 1, buf)
                if not is_last(it):
                    max_rows(2 * it + 2, 0, (buf + 1) % 3)

            for buf in range(3):
                for h in range(kh):
                    sp.dma_start(kst[MAIN:rows, buf, h, :], fixed_k[ALIBI - bias_rows:, :]).then_inc(fixed, 16)
            load_stacks(0, 0)
            load_v(0)
            sp.wait_ge(stacks, n_loads)
            load_stacks(1, 1)
            max_rows(0, 0, 0)
            run(sp, body)
            sp.wait_ge(m_rows, 16 * SHIFT * 2 * ITS)

        @block.gpsimd
        def _(pool):
            def spread(it, before):
                pool.wait_ge(v_in, 16 * (it + 1))
                if before:
                    pool.wait_ge(pv_done, n_steps * it)
                    settle(pool, passed)
                pool.tensor_copy(vone[:, :, :, 0:HD], vload[:, :, :, :]).then_inc(v_set, 1)

            def split_max(n, turned, before):
                pool.wait_ge(st_used, max_take(turned))
                settle(pool, passed)
                pool.tensor_scalar(mneg[:, :], mrow[:, :], -1.0, None, ALU.mult).then_inc(m_neg, 1)
                pool.wait_ge(m_neg, n + 1)
                if before:
                    pool.wait_ge(m_rows, 16 * SHIFT * n)
                    settle(pool, passed)
                pool.tensor_copy(mparts[:, 0, :], mneg[:, :]).then_inc(m_part0, 1)
                pool.wait_ge(m_part0, n + 1)
                pool.tensor_tensor(mrest[:, :], mneg[:, :], mparts[:, 0, :], ALU.subtract).then_inc(m_rest, 1)
                pool.wait_ge(m_rest, n + 1)
                settle(pool, passed)
                pool.tensor_copy(mparts[:, 1, :], mrest[:, :]).then_inc(m_part1, 1)
                pool.wait_ge(m_part1, n + 1)
                pool.tensor_tensor(mparts[:, 2, :], mrest[:, :], mparts[:, 1, :], ALU.subtract).then_inc(m_parts, 1)

            def body(it, before, last):
                spread(it, before)
                split_max(2 * it + 1, (it, 1), True)
                if not last:
                    split_max(2 * it + 2, (it + 1, 0), True)

            pool.memset(vone[:, :, :, :], 1.0).then_inc(v_set, 1)
            pool.wait_ge(v_set, 1)
            split_max(0, (0, 0), False)
            body(0, False, False)
            with pool.Fori(1, ITS - 1) as it:
                body(it, True, False)
            body(ITS - 1, True, True)

        @block.scalar
        def _(act):
            def body(it, before, last):
                for n, (kind, i, h) in enumerate(takes):
                    if kind == "max" and last and i == 1:
                        continue
                    act.wait_ge(st_made, taken(it, n))
                    if kind == "max":
                        act.wait_ge(m_neg, 2 * it + 1 + i)
                        act.activation(mrow[:, :], st_ps[0:GH * QT, bank_of(n), 0:P],
                                       ACT.Copy).then_inc(st_used, 1)
                        continue
                    first = steps[i][2]
                    if h == 0 and (before or i >= ring):
                        act.wait_ge(pv_done, n_steps * it + i - ring + 1)
                    act.activation(probs[:, (i % ring) * GH + h, first:HALF], st_ps[:, bank_of(n), first:HALF],
                                   ACT.Exp).then_inc(st_used, 1)

            act.wait_ge(st_made, 1)
            act.activation(mrow[:, :], st_ps[0:GH * QT, 2, 0:P], ACT.Copy).then_inc(st_used, 1)
            body(0, False, False)
            with act.Fori(1, ITS - 1) as it:
                body(it, True, False)
            body(ITS - 1, True, True)

        @block.vector
        def _(dve):
            def maximum(group, n, half, qt, h):
                dve.wait_ge(scored, 2 * GH * QT * group + n + 1)
                dve.reduce_max(maxes[:, half, h * QT + qt:h * QT + qt + 1],
                               s_ps[:, n % 2, 0:key_width(half, qt)], AX.X).then_inc(maxed, 1)

            def copy_o(it, half):
                dve.wait_ge(pv_done, n_steps * it + (first_of[1] if half == 0 else n_steps))
                dve.tensor_copy(ot(it, half), o_ps[:, :]).then_inc(o_out, 1)

            def body(it, before, last):
                for i in range(n_steps):
                    for n, half, qt, h in units_at[i] if not last else ():
                        if n == half * GH * QT:
                            dve.wait_ge(st_made, max_take((it, half)))
                        maximum(it + 1, n, half, qt, h)
                    if i == 0 and before:
                        copy_o(it - 1, 1)
                    if i == first_of[1]:
                        copy_o(it, 0)

            for half in range(2):
                for n, (_, qt, h) in enumerate(row_units[half]):
                    maximum(0, half * GH * QT + n, half, qt, h)
            body(0, False, False)
            with dve.Fori(1, ITS - 1) as it:
                body(it, True, False)
            body(ITS - 1, True, True)
            copy_o(ITS - 1, 1)

        @block.tensor
        def _(pe):
            def row_scores(group, buf, n, half, qt, h):
                if not (isinstance(group, int) and group == 0 and n < 2):
                    pe.wait_ge(maxed, 2 * GH * QT * group + n - 1)
                q = qst[0:top, buf, half, h, qt * P:(qt + 1) * P]
                width = key_width(half, qt)
                for a in range(0, width, HALF):
                    b = min(a + HALF, width)
                    masked = causal and b == width
                    ins = pe.matmul(s_ps[:, n % 2, a:b], q, kst[0:top, buf, h % kh, a:b],
                                    start=True, stop=not masked)
                    if masked:
                        ins = pe.matmul(s_ps[:, n % 2, width - P:width], ident_bf[:, :], mask_q[:, :],
                                        start=False, stop=True)
                ins.then_inc(scored, 1)

            def turn_max(group, half, bank):
                pe.wait_ge(maxed, 2 * GH * QT * group + (half + 1) * GH * QT)
                pe.matmul(st_ps[0:GH * QT, bank, 0:P], maxes[:, half, :], ident[:, :],
                          start=True, stop=True).then_inc(st_made, 1)

            def values(it, i):
                half, kt, first, _ = steps[i]
                if i == 0:
                    pe.wait_ge(v_set, it + 2)
                if kt == 0 and not (isinstance(it, int) and it == 0 and half == 0):
                    pe.wait_ge(o_out, 2 * it + half)
                last = i == n_steps - 1 or steps[i + 1][0] != half
                pe.wait_ge(st_used, taken(it, where[("exp", i, GH - 1)]))
                for h in range(GH):
                    ins = pe.matmul(o_ps[32 * h:32 * h + 32, first:HALF], vone[:, kt, h % kh, :],
                                    probs[:, (i % ring) * GH + h, first:HALF], start=kt == 0, stop=last)
                ins.then_inc(pv_done, 1)

            def body(it, buf, before):
                last = is_last(it)
                if not last:
                    pe.wait_ge(stacks, n_loads * (it + 2))
                for i, (half, kt, first, diagonal) in enumerate(steps):
                    if i == first_of[half]:
                        pe.wait_ge(m_rows, 16 * SHIFT * (2 * it + half + 1))
                    units = [] if last else list(units_at[i])
                    spacing = -(-len(units) // 2)
                    for h in range(GH):
                        n = where[("exp", i, h)]
                        pe.wait_ge(st_used, used_before(it, n))
                        bank = st_ps[:, bank_of(n), :]
                        ins = pe.matmul(bank[:, first:HALF], kst[0:rows, buf, h % kh, kt * P:(kt + 1) * P],
                                        qst[0:rows, buf, half, h, first:HALF], start=True, stop=not diagonal)
                        if diagonal:
                            ins = pe.matmul(bank[:, first:first + P], ident_bf[:, :], mask_k[:, :],
                                            start=False, stop=True)
                        ins.then_inc(st_made, 1)
                        if h % 2:
                            for unit in units[:spacing]:
                                row_scores(it + 1, (buf + 1) % 3, *unit)
                            units = units[spacing:]
                    if i == 0 and before:
                        values(it - 1, n_steps - 1)
                    if i > 0:
                        values(it, i - 1)
                    if i == first_of[half] + 1 and not (last and half == 1):
                        n = where[("max", half, 0)]
                        pe.wait_ge(st_used, used_before(it, n))
                        turn_max(it + half, 1 - half, bank_of(n))

            pe.wait_ge(stacks, n_loads)
            pe.wait_ge(v_set, 1)
            pe.wait_ge(fixed, 16 * 3 * kh)
            for half in range(2):
                for n, (_, qt, h) in enumerate(row_units[half]):
                    row_scores(0, 0, half * GH * QT + n, half, qt, h)
                if half == 0:
                    turn_max(0, 0, 2)
            run(pe, body)
            values(ITS - 1, n_steps - 1)


def output(nc, sb, ps, sems, tag, x_sb, ident, ot, wo_ap):
    wo = sb(f"wo{tag}", [P, DC, D], F32)
    recip = sb(f"recip{tag}", [P, HEADS], F32)
    on = sb(f"on{tag}", [P, D], F32)
    onT = sb(f"onT{tag}", [P, DC, P], F32)
    r = Residual(sb, sems, tag)
    a_ps = ps(f"a_ps{tag}", [P, 2, NG, P], F32)
    b_ps = ps(f"b_ps{tag}", [P, 2, DC, P], F32)
    y_ps = ps(f"y_ps{tag}", [P, 2, D], F32)
    w_loaded, turned, inverted, scaled = sems("w_loaded"), sems("o_turned"), sems("sums_inverted"), sems("o_scaled")
    back, back_out, made = sems("o_turned_back"), sems("oT_ready"), sems("y_made")

    with nc.Block() as block:
        @block.sync
        def _(sp):
            sp.dma_start(wo[:, :, :], wo_ap.rearrange("(c p) e -> p c e", p=P)).then_inc(w_loaded, 16)

        @block.tensor
        def _(pe):
            def turn(t, par, first):
                b, q = (t // (SEQ // P), t % (SEQ // P))
                if not first:
                    pe.wait_ge(scaled, t - 1)
                for g in range(NG):
                    ins = pe.transpose(a_ps[:, par, g, :], ot(b, g, q), ident[:, :])
                ins.then_inc(turned, 1)

            def turn_back(t, par, first):
                pe.wait_ge(scaled, t + 1)
                if not first:
                    pe.wait_ge(back_out, t - 1)
                for c in range(DC):
                    ins = pe.transpose(b_ps[:, par, c, :], on[:, c * P:(c + 1) * P], ident[:, :])
                ins.then_inc(back, 1)

            def product(t, par, first):
                pe.wait_ge(back_out, t + 1)
                if not first:
                    pe.wait_ge(r.normed, t - 1)
                for c in range(DC):
                    ins = pe.matmul(y_ps[:, par, :], onT[:, c, :], wo[:, c, :], start=c == 0, stop=c == DC - 1)
                ins.then_inc(made, 1)

            def body(t, par, first, last):
                turn_back(t, par, first)
                if not last:
                    turn(t + 1, 1 - par, first)
                product(t, par, first)

            turn(0, 0, True)
            pe.wait_ge(w_loaded, 16)
            body(0, 0, True, False)
            for t in range(1, NT):
                body(t, t % 2, t < 2, t == NT - 1)

        @block.vector
        def _(dve):
            def scale(t, par, first):
                dve.wait_ge(turned, t + 1)
                sums = a_ps[:, par, :, :].rearrange("p g (h c) -> p (g h) c", h=GH)
                dve.reciprocal(recip[:, :], sums[:, :, HD]).then_inc(inverted, 1)
                dve.wait_ge(inverted, t + 1)
                if not first:
                    dve.wait_ge(back, t)
                dve.tensor_tensor(on[:, :].rearrange("p (h c) -> p h c", c=HD), sums[:, :, 0:HD],
                                  recip[:, :].rearrange("p (h a) -> p h a", a=1).broadcast_to([P, HEADS, HD]),
                                  ALU.mult).then_inc(scaled, 1)

            scale(0, 0, True)
            for t in range(NT):
                if t < NT - 1:
                    scale(t + 1, (t + 1) % 2, False)
                dve.wait_ge(made, t + 1)
                residual_vector(dve, r, y_ps[:, t % 2, :], t, t % 2, t < 2)

        @block.scalar
        def _(act):
            for t in range(NT):
                act.wait_ge(back, t + 1)
                if t:
                    act.wait_ge(made, t)
                act.activation(onT[:, :, :], b_ps[:, t % 2, :, :], ACT.Copy).then_inc(back_out, 1)
                residual_root(act, r, t)

        @block.gpsimd
        def _(pool):
            for t in range(NT):
                residual_add(pool, r, x_sb, t, t % 2)


def gated_ffn(nc, sb, ps, sems, tag, x_sb, ident, gate_w, gate_s, up_w, up_s, down_w, down_s):
    n, r = Norm(sb, ps, sems, tag), Residual(sb, sems, tag)
    wg = sb(f"wg{tag}", [P, DC, FF], F32)
    wu = sb(f"wu{tag}", [P, DC, FF], F32)
    wd = sb(f"wd{tag}", [P, FT, D], F32)
    sg = sb(f"sg{tag}", [P, FT], F32)
    su = sb(f"su{tag}", [P, FT], F32)
    ds = sb(f"ds{tag}", [P, D], F32)
    silu = sb(f"silu{tag}", [P, 2, BLK], F32)
    hT = sb(f"hT{tag}", [P, FT, BLK], F32)
    g_ps = ps(f"g_ps{tag}", [P, 2, BLK], F32)
    u_ps = ps(f"u_ps{tag}", [P, 2, BLK], F32)
    y_ps = ps(f"y_ps{tag}", [P, 2, D], F32)
    s_loaded = sems("scales_loaded")
    g_made, u_made, silu_out, h_out, y_made = (sems(k) for k in ("gate", "up", "silu_ready", "h_ready", "y_made"))
    frows = [P] * (FT - 1) + [FLAST]
    gu_pieces = [(f"{k}{c}", w, w_ap, c) for c in range(DC) for k, w, w_ap in (("g", wg, gate_w), ("u", wu, up_w))]
    gu_loaded = [sems(f"w_{k}_loaded") for k, *_ in gu_pieces]
    wd_loaded = sems("w_down_loaded")
    wd_float, wd_scaled, gu_float = sems("w_down_float"), sems("w_down_scaled"), sems("w_gate_up_float")

    with nc.Block() as block:
        @block.sync
        def _(sp):
            for (k, w, w_ap, c), loaded in zip(gu_pieces, gu_loaded):
                sp.dma_start(w[:, c, :].bitcast(I32), w_ap[c * P:(c + 1) * P, :]).then_inc(loaded, 16)
            for dst, src in ((sg, gate_s), (su, up_s), (ds, down_s)):
                sp.dma_start(dst[:, :], src).then_inc(s_loaded, 16)
            sp.dma_start(wd[:, 0:FT - 1, :].bitcast(I32), down_w[0:(FT - 1) * P, :].rearrange(
                "(j p) d -> p j d", p=P)).then_inc(wd_loaded, 16)
            sp.dma_start(wd[0:FLAST, FT - 1, :].bitcast(I32), down_w[(FT - 1) * P:FF, :]).then_inc(wd_loaded, 16)

        @block.gpsimd
        def _(pool):
            pool.wait_ge(wd_loaded, 16 * 2)
            pool.wait_ge(s_loaded, 16 * 3)
            for j, k in enumerate(frows):
                pool.tensor_copy(wd[0:k, j, :], wd[0:k, j, :].bitcast(I32)).then_inc(wd_float, 1)
                pool.wait_ge(wd_float, j + 1)
                pool.tensor_tensor(wd[0:k, j, :], wd[0:k, j, :], ds[0:k, :], ALU.mult).then_inc(wd_scaled, 1)
            with pool.Fori(0, NT // 2) as i:
                for par in range(2):
                    residual_add(pool, r, x_sb, 2 * i + par, par)

        @block.scalar
        def _(act):
            norm_root(act, n, 0)
            for (k, w, _, c), loaded in zip(gu_pieces, gu_loaded):
                act.wait_ge(loaded, 16)
                act.activation(w[:, c, :], w[:, c, :].bitcast(I32), ACT.Copy).then_inc(gu_float, 1)
            norm_copy(act, n, 0, 0)
            act.wait_ge(s_loaded, 16 * 3)
            for nb in range(NB):
                for j in range(FT):
                    k, c = frows[j], nb * FT + j
                    act.wait_ge(g_made, c + 1)
                    if c >= 2:
                        act.wait_ge(h_out, c - 1)
                    act.activation(silu[0:k, c % 2, :], g_ps[0:k, c % 2, :], ACT.Silu,
                                   scale=sg[0:k, j:j + 1]).then_inc(silu_out, 1)
                if nb < NB - 1:
                    norm_root(act, n, nb + 1)
                    norm_copy(act, n, nb + 1, (nb + 1) % 2)
                for i in range(TB):
                    residual_root(act, r, TB * nb + i)

        @block.vector
        def _(dve):
            norm_vector(dve, n, x_sb, 0, True)
            dve.wait_ge(s_loaded, 16 * 3)
            for nb in range(NB):
                for j in range(FT):
                    k, c = frows[j], nb * FT + j
                    dve.wait_ge(u_made, c + 1)
                    dve.wait_ge(silu_out, c + 1)
                    if nb:
                        dve.wait_ge(y_made, TB * nb)
                    dve.scalar_tensor_tensor(out=hT[0:k, j, :], in0=u_ps[0:k, c % 2, :], scalar=su[0:k, j:j + 1],
                                             in1=silu[0:k, c % 2, :], op0=ALU.mult, op1=ALU.mult).then_inc(h_out, 1)
                if nb < NB - 1:
                    norm_vector(dve, n, x_sb, nb + 1, False)
                for i in range(TB):
                    t = TB * nb + i
                    dve.wait_ge(y_made, t + 1)
                    residual_vector(dve, r, y_ps[:, t % 2, :], t, t % 2, t < 2)

        @block.tensor
        def _(pe):
            norm_turn(pe, n, ident, 0)
            pe.wait_ge(gu_float, 2 * DC)
            for nb in range(NB):
                pe.wait_ge(n.ready, TB * (nb + 1))
                for j in range(FT):
                    k, c = frows[j], nb * FT + j
                    if c >= 2:
                        pe.wait_ge(silu_out, c - 1)
                    for d in range(DC):
                        ins = pe.matmul(g_ps[0:k, c % 2, :], wg[:, d, j * P:j * P + k], n.xnT[:, nb % 2, d, :],
                                        start=d == 0, stop=d == DC - 1)
                    ins.then_inc(g_made, 1)
                    if c >= 2:
                        pe.wait_ge(h_out, c - 1)
                    for d in range(DC):
                        ins = pe.matmul(u_ps[0:k, c % 2, :], wu[:, d, j * P:j * P + k], n.xnT[:, nb % 2, d, :],
                                        start=d == 0, stop=d == DC - 1)
                    ins.then_inc(u_made, 1)
                if nb < NB - 1:
                    norm_turn(pe, n, ident, nb + 1)
                if nb == 0:
                    pe.wait_ge(wd_scaled, FT)
                pe.wait_ge(h_out, FT * (nb + 1))
                for i in range(TB):
                    t = TB * nb + i
                    if t >= 2:
                        pe.wait_ge(r.normed, t - 1)
                    for j in range(FT):
                        ins = pe.matmul(y_ps[:, t % 2, :], hT[0:frows[j], j, i * P:(i + 1) * P],
                                        wd[0:frows[j], j, :], start=j == 0, stop=j == FT - 1)
                    ins.then_inc(y_made, 1)


def adapter_ffn(nc, sb, ps, sems, tag, x_sb, ident, w_ap, b_ap, a_ap, bm_ap, p_ap, out):
    n, r = Norm(sb, ps, sems, tag), Residual(sb, sems, tag)
    w = sb(f"w{tag}", [P, DC, D], F32)
    a = sb(f"a{tag}", [P, DC, ER], F32)
    bm = sb(f"bm{tag}", [ER, D], F32)
    bias = sb(f"bias{tag}", [P, D], F32)
    scores = sb(f"scores{tag}", [ER, 1], F32)
    uT = sb(f"uT{tag}", [ER, 2, BLK], F32)
    z = sb(f"z{tag}", [P, 2, D], F32)
    y = sb(f"y{tag}", [P, 2, D], F32)
    square = sb(f"square{tag}", [P, 2, D], F32)
    norms = sb(f"norms{tag}", [P, 2, 2], F32)
    gamma = sb(f"gamma{tag}", [P, 3], F32)
    u_ps = ps(f"u_ps{tag}", [ER, BLK], F32)
    z_ps = ps(f"z_ps{tag}", [P, 2, D], F32)
    m_ps = ps(f"m_ps{tag}", [P, 2, D], F32)
    w_loaded, u_made, u_out, z_made, m_made, z_out = (sems(k) for k in (
        "w_loaded", "u_made", "uT_ready", "z_made", "m_made", "z_ready"))
    z_squared, m_squared, roots, g_steps, y_out, stored = (sems(k) for k in (
        "z_squared", "m_squared", "norms_ready", "gamma_steps", "y_ready", "stored"))

    with nc.Block() as block:
        @block.sync
        def _(sp):
            sp.dma_start(w[:, :, :], w_ap.rearrange("(c p) e -> p c e", p=P)).then_inc(w_loaded, 16)
            sp.dma_start(a[:, :, :], a_ap.rearrange("(c p) e -> p c e", p=P)).then_inc(w_loaded, 16)
            sp.dma_start(bm[:, :], bm_ap).then_inc(w_loaded, 16)
            sp.dma_start(bias[:, :], b_ap).then_inc(w_loaded, 16)
            sp.dma_start(scores[:, :], p_ap).then_inc(w_loaded, 16)
            for t in range(NT):
                sp.wait_ge(r.added, t + 1)
                sp.dma_start(out[t * P:(t + 1) * P, :], x_sb[:, t, :]).then_inc(stored, 16)
            sp.wait_ge(stored, 16 * NT)

        @block.gpsimd
        def _(pool):
            for t in range(NT):
                residual_add(pool, r, x_sb, t, t % 2)

        @block.scalar
        def _(act):
            norm_root(act, n, 0)
            norm_copy(act, n, 0, 0)
            act.wait_ge(w_loaded, 16 * 5)
            for nb in range(NB):
                if nb < NB - 1:
                    norm_root(act, n, nb + 1)
                act.wait_ge(u_made, nb + 1)
                act.activation(uT[:, nb % 2, :], u_ps[:, :], ACT.Copy, scale=scores[:, 0:1]).then_inc(u_out, 1)
                for i in range(TB):
                    t = TB * nb + i
                    par = t % 2
                    act.wait_ge(z_out, t + 1)
                    if t >= 2:
                        act.wait_ge(g_steps, 5 * (t - 1))
                    if t:
                        act.wait_ge(roots, t)
                    act.activation(square[:, 0, :], z[:, par, :], ACT.Square,
                                   accum_out=norms[:, par, 0:1]).then_inc(z_squared, 1)
                    act.wait_ge(m_made, t + 1)
                    act.activation(square[:, 1, :], m_ps[:, par, :], ACT.Square,
                                   accum_out=norms[:, par, 1:2]).then_inc(m_squared, 1)
                    act.wait_ge(z_squared, t + 1)
                    act.wait_ge(m_squared, t + 1)
                    act.activation(norms[:, par, :], norms[:, par, :], ACT.Sqrt).then_inc(roots, 1)
                    residual_root(act, r, t)
                    if i == 1 and nb < NB - 1:
                        norm_copy(act, n, nb + 1, (nb + 1) % 2)

        @block.vector
        def _(dve):
            norm_vector(dve, n, x_sb, 0, True)
            dve.wait_ge(w_loaded, 16 * 5)
            for nb in range(NB):
                if nb < NB - 1:
                    norm_vector(dve, n, x_sb, nb + 1, False)
                for i in range(TB):
                    t = TB * nb + i
                    par = t % 2
                    dve.wait_ge(z_made, t + 1)
                    dve.tensor_tensor(z[:, par, :], z_ps[:, par, :], bias[:, :], ALU.add).then_inc(z_out, 1)
                    dve.wait_ge(roots, t + 1)
                    dve.tensor_scalar(gamma[:, 0:1], norms[:, par, 1:2], NORM_EPS, None, ALU.add).then_inc(g_steps, 1)
                    dve.wait_ge(g_steps, 5 * t + 1)
                    dve.reciprocal(gamma[:, 1:2], gamma[:, 0:1]).then_inc(g_steps, 1)
                    dve.wait_ge(g_steps, 5 * t + 2)
                    dve.scalar_tensor_tensor(out=gamma[:, 2:3], in0=norms[:, par, 0:1], scalar=CLAMP,
                                             in1=gamma[:, 1:2], op0=ALU.mult, op1=ALU.mult).then_inc(g_steps, 1)
                    dve.wait_ge(g_steps, 5 * t + 3)
                    dve.tensor_scalar(gamma[:, 2:3], gamma[:, 2:3], 1.0, None, ALU.min).then_inc(g_steps, 1)
                    dve.wait_ge(g_steps, 5 * t + 4)
                    dve.wait_ge(m_squared, t + 1)
                    dve.scalar_tensor_tensor(out=y[:, par, :], in0=m_ps[:, par, :], scalar=gamma[:, 2:3],
                                             in1=z[:, par, :], op0=ALU.mult, op1=ALU.add).then_inc(g_steps, 1)
                    dve.wait_ge(g_steps, 5 * t + 5)
                    residual_vector(dve, r, y[:, par, :], t, par, t < 2)

        @block.tensor
        def _(pe):
            norm_turn(pe, n, ident, 0)
            pe.wait_ge(w_loaded, 16 * 5)
            for nb in range(NB):
                par = nb % 2
                pe.wait_ge(n.ready, TB * (nb + 1))
                if nb:
                    pe.wait_ge(u_out, nb)
                for c in range(DC):
                    ins = pe.matmul(u_ps[:, :], a[:, c, :], n.xnT[:, par, c, :], start=c == 0, stop=c == DC - 1)
                ins.then_inc(u_made, 1)
                for i in range(TB):
                    t = TB * nb + i
                    if t >= 2:
                        pe.wait_ge(z_out, t - 1)
                    for c in range(DC):
                        ins = pe.matmul(z_ps[:, t % 2, :], n.xnT[:, par, c, i * P:(i + 1) * P], w[:, c, :],
                                        start=c == 0, stop=c == DC - 1)
                    ins.then_inc(z_made, 1)
                    pe.wait_ge(u_out, nb + 1)
                    if t >= 2:
                        pe.wait_ge(g_steps, 5 * (t - 1))
                    pe.matmul(m_ps[:, t % 2, :], uT[:, par, i * P:(i + 1) * P], bm[:, :],
                              start=True, stop=True).then_inc(m_made, 1)
                    if i == 1 and nb < NB - 1:
                        norm_turn(pe, n, ident, nb + 1)


def build(nc, x, w_q, w_k, w_v, w_o, gate_w, gate_s, up_w, up_s, down_w, down_s, wqkv, wo1, w1, b1, a1, bm1,
          p1, ident_in, ident_bf_in, mask_q_in, mask_k_in, fixed_k, bias_q_in, out, stop=99):
    with ExitStack() as whole:
        x_sb = whole.enter_context(nc.sbuf_tensor("x_sb", [P, NT, D], F32))
        ident = whole.enter_context(nc.sbuf_tensor("ident", [P, P], F32))
        ident_bf = whole.enter_context(nc.sbuf_tensor("ident_bf", [P, P], BF16))
        mask_q = whole.enter_context(nc.sbuf_tensor("mask_q", [P, P], BF16))
        mask_k = whole.enter_context(nc.sbuf_tensor("mask_k", [P, P], BF16))
        q_parts = [nc.dram_tensor(f"q_parts{l}", (3, ITS, GH * HD, SEQ), BF16, kind="Internal").ap() for l in range(2)]
        k_parts = [nc.dram_tensor("k_parts0", (3, ITS, GH * HD, SEQ), BF16, kind="Internal").ap(),
                   nc.dram_tensor("k_parts1", (3, BATCH, HD, SEQ), BF16, kind="Internal").ap()]
        v_rows = [nc.dram_tensor("v_rows0", (ITS, P, KT, GH * HD), F32, kind="Internal").ap(),
                  nc.dram_tensor("v_rows1", (BATCH, P, KT, HD), F32, kind="Internal").ap()]

        def one(i):
            return slice(i, i + 1) if isinstance(i, int) else bass.ds(i, 1)

        def store_parts(scratch, j):
            def to(nb, s):
                b, th = nb // 2, nb % 2
                v = scratch.rearrange("c (b i) e (h t) -> c b (i e) h t", b=BATCH, h=2)
                return v[:, one(b), j * P:(j + 1) * P, one(th), :].rearrange("c b e h t -> (b e h) c t")
            return to

        def store_k1(nb, s):
            v = k_parts[1].rearrange("c b e (h t) -> c b e h t", h=2)
            return v[:, one(nb // 2), :, one(nb % 2), :].rearrange("c b e h t -> (b e h) c t")

        def store_v0(nb, s):
            v = v_rows[0].rearrange("(b g) p (h k) c -> b h k p g c", b=BATCH, h=2)
            return v[one(nb // 2), one(nb % 2), s].rearrange("b h p g c -> (b h p) g c")

        def store_v1(nb, s):
            v = v_rows[1].rearrange("b p (h k) c -> b h p k c", h=2)
            return v[one(nb // 2), one(nb % 2)].rearrange("b h p k c -> (b h p) k c")

        phases = [0]

        def phase():
            ctx, mine = ExitStack(), []
            phases[0] += 1
            number = phases[0]

            def sb(name, shape, dt):
                return ctx.enter_context(nc.sbuf_tensor(name, shape, dt))

            def ps(name, shape, dt):
                return ctx.enter_context(nc.psum_tensor(name, shape, dt))

            def sems(name):
                mine.append(nc.alloc_semaphore(f"{name}_{number}"))
                return mine[-1]

            def give_back():
                nc.clear_and_free_semaphores(mine)
                nc.all_engine_barrier()

            ctx.callback(give_back)
            return ctx, sb, ps, sems

        out0 = [("split", "q", j * P, 0, P, SCALE, store_parts(q_parts[0], j)) for j in range(DC)]
        out0 += [("split", "k", j * P, 0, P, 1.0, store_parts(k_parts[0], j)) for j in range(DC)]
        out0 += [("v", "v", 0, D, False, store_v0)] * TB
        out0 = out0[:8] + [("v", "v", 0, D, False, store_v0) for _ in range(TB)]
        kv = HEADS * HD + 2 * HD - P
        out1 = [("split", "qkv", j * P, 0, P, SCALE, store_parts(q_parts[1], j)) for j in range(DC)]
        out1 += [("split", "qkv", kv, P - 2 * HD, HD, 1.0, store_k1),
                 ("v", "qkv", HEADS * HD + HD, HD, True, store_v1)]
        consts = [(ident[:, :], ident_in), (ident_bf[:, :], ident_bf_in), (mask_q[:, :], mask_q_in),
                  (mask_k[:, :], mask_k_in)]

        def load_x(c):
            return x_sb[:, TB * c:TB * c + TB, :], x[BLK * c:BLK * (c + 1), :].rearrange("(t p) d -> p t d", p=P)

        for layer in range(2):
            ctx, sb, ps, sems = phase()
            with ctx:
                if layer == 0:
                    project(nc, sb, ps, sems, "A", x_sb, ident, {"q": w_q, "k": w_k, "v": w_v}, out0, load_x, consts)
                else:
                    project(nc, sb, ps, sems, "F", x_sb, ident, {"qkv": wqkv}, out1)
            if stop <= 4 * layer + 1:
                break
            with ExitStack() as kept:
                tag = "BG"[layer]
                oT = kept.enter_context(nc.sbuf_tensor(f"oT{tag}", [P, ITS, 2, HALF], F32))

                def ot(it, half):
                    if isinstance(it, int):
                        return oT[:, it, half, :]
                    return oT[:, bass.ds(it, 1), half, :].rearrange("p a t -> p (a t)")

                def heads_q(c, it, half):
                    v = q_parts[layer].rearrange("c i (h d) (f t) -> c i f d h t", d=HD, f=2)
                    return v[c, one(it), half].rearrange("i d h t -> (i d) h t")

                def heads_k(c, it):
                    if layer:
                        return k_parts[1][c, one(it // NG)].rearrange("b d (h t) -> (b d) h t", h=1)
                    v = k_parts[0].rearrange("c i (h d) t -> c i d h t", d=HD)
                    return v[c, one(it)].rearrange("i d h t -> (i d) h t")

                def v_of(it):
                    return v_rows[layer][one(it // NG if layer else it)].rearrange("i p k c -> (i p) k c")

                def bias_q(it, half):
                    return bias_q_in[one(it % NG), :, half].rearrange("i r h t -> (i r) h t")

                ctx, sb, ps, sems = phase()
                with ctx:
                    attention(nc, sb, ps, sems, tag, layer == 1, heads_q, heads_k, v_of, ot, ident, ident_bf,
                              mask_q, mask_k, fixed_k, bias_q)
                ctx, sb, ps, sems = phase()

                def o_tile(b, g, q):
                    return oT[:, b * NG + g, q // QT, (q % QT) * P:(q % QT + 1) * P]

                with ctx:
                    output(nc, sb, ps, sems, "CH"[layer], x_sb, ident, o_tile, (w_o, wo1)[layer])
            if stop <= 4 * layer + 2:
                break
            ctx, sb, ps, sems = phase()
            with ctx:
                if layer == 0:
                    gated_ffn(nc, sb, ps, sems, "D", x_sb, ident, gate_w, gate_s, up_w, up_s, down_w, down_s)
                else:
                    adapter_ffn(nc, sb, ps, sems, "I", x_sb, ident, w1, b1, a1, bm1, p1, out)
            if stop <= 4 * layer + 3:
                break
        if stop < 99:
            dump = whole.enter_context(nc.semaphore("dump"))
            with nc.Block() as block:
                @block.sync
                def _(sp):
                    sp.dma_start(out.rearrange("(t p) d -> p t d", p=P), x_sb[:, :, :]).then_inc(dump, 16)
                    sp.wait_ge(dump, 16)


def shape_constants():

    bf = np.dtype("bfloat16")

    def parts(a, n):
        a, out = a.astype(np.float32), []
        for _ in range(n):
            out.append(a.astype(bf))
            a = a - out[-1].astype(np.float32)
        return out

    later = np.arange(P)[None, :] > np.arange(P)[:, None]
    mask_q = np.where(later, np.float32(-1e30), np.float32(0)).astype(bf)
    pos = np.arange(SEQ, dtype=np.float32)
    slopes = (2.0 ** (-0.25 * np.arange(1, HEADS + 1, dtype=np.float64))).astype(np.float32)
    ones = np.ones((HEADS, SEQ), np.float32)
    slope_parts, pos_parts = parts(slopes[:, None] * ones, 3), parts(pos, 2)
    query_parts = parts(-slopes[:, None] * pos[None, :], 3)
    q_rows = np.stack([s for s in slope_parts for _ in pos_parts] + query_parts)
    k_rows = np.stack([p for _ in slope_parts for p in pos_parts] + [np.ones(SEQ, bf)] * (3 + SHIFT))
    bias_q = q_rows.reshape(ALIBI, NG, GH, 2, HALF).transpose(1, 0, 3, 2, 4)
    return {
        "ident": np.eye(P, dtype=np.float32), "ident_bf": np.eye(P).astype(bf), "mask_q": mask_q,
        "mask_k": np.ascontiguousarray(mask_q.T), "fixed_k": k_rows, "bias_q": np.ascontiguousarray(bias_q),
    }


def kernel(**inputs):
    import concourse.bacc as _bacc
    from concourse.bass_utils import run_bass_kernel_spmd as _run

    a = {k: np.asarray(v) for k, v in inputs.items()}

    def columns(v):
        return np.pad(v.reshape(FF), (0, FT * P - FF)).reshape(FT, P).T

    arrays = {
        "x": a["L0_attn_x"].reshape(TOK, D),
        "w_q": a["L0_attn_w_q"].T, "w_k": a["L0_attn_w_k"].T, "w_v": a["L0_attn_w_v"].T, "w_o": a["L0_attn_w_o"].T,
        "gate_w": a["L0_ffn_gate_w"].T, "gate_s": columns(a["L0_ffn_gate_s"]), "up_w": a["L0_ffn_up_w"].T,
        "up_s": columns(a["L0_ffn_up_s"]), "down_w": a["L0_ffn_down_w"].T,
        "down_s": np.broadcast_to(a["L0_ffn_down_s"].reshape(1, D), (P, D)),
        "wqkv": a["L1_attn_Wqkv"], "wo1": a["L1_attn_Wo"], "w1": a["L1_ffn_W"].T,
        "b1": np.broadcast_to(a["L1_ffn_b"].reshape(1, D), (P, D)),
        "a1": a["L1_ffn_A"].transpose(1, 0, 2).reshape(D, ER), "bm1": a["L1_ffn_B"].reshape(ER, D),
        "p1": np.repeat(a["L1_ffn_p_scores"], ER // 8).reshape(ER, 1),
    }
    arrays.update(shape_constants())
    nc = _bacc.Bacc("TRN2", target_bir_lowering=False, num_devices=1)
    in_map, args = {}, []
    for name, v in arrays.items():
        v = np.ascontiguousarray(v)
        in_map[f"in_{name}"] = v
        args.append(nc.dram_tensor(f"in_{name}", v.shape, mybir.dt.from_np(v.dtype), kind="ExternalInput").ap())
    args.append(nc.dram_tensor("out_0", (TOK, D), F32, kind="ExternalOutput").ap())
    build(nc, *args)
    r = _run(nc, [in_map], core_ids=[0])
    return r.results[0]["out_0"].reshape(BATCH, SEQ, D)
```

```python
from contextlib import ExitStack

import numpy as np

import concourse.bass as bass
from concourse import mybir

F32 = mybir.dt.float32
F32R = mybir.dt.float32r
BF16 = mybir.dt.bfloat16
I32 = mybir.dt.int32
ALU = mybir.AluOpType
ACT = mybir.ActivationFunctionType
AX = mybir.AxisListType

P = 128
BATCH, SEQ, D = 2, 1024, 512
TOK = BATCH * SEQ
NT = TOK // P
DC = D // P
BLK = 512
NB = TOK // BLK
TB = BLK // P
HEADS, HD = 32, 16
GH = 4
NG = HEADS // GH
ITS = BATCH * NG
HALF = 512
KT = SEQ // P
QT = HALF // P
SCALE = HD ** -0.5
FF = 1376
FT = -(-FF // P)
FLAST = FF - (FT - 1) * P
LN_EPS = 1e-5
ER = 128
CLAMP, NORM_EPS = 0.5, 1e-6

Q_PARTS = (0, 0, 0, 1, 1, 2)
K_PARTS = (0, 1, 2, 0, 1, 0)
MAIN = HD * len(Q_PARTS)
ALIBI = 9
SHIFT = 3


def widths(causal, half):
    out = []
    for kt in range(KT):
        first = kt * P - half * HALF
        if causal and first >= HALF:
            break
        diagonal = causal and first >= 0
        out.append((first if diagonal else 0, diagonal))
    return out


def settle(engine, passed):
    engine.sem_inc(passed, 1)


def split_product(pe, out, left, right, start, stop):
    pe.matmul(out, left[0], right[0], start=start, stop=False)
    pe.matmul(out, left[0], right[1], start=False, stop=False)
    return pe.matmul(out, left[1], right[0], start=False, stop=stop)


class Norm:

    def __init__(self, sb, ps, sems, tag, buffers=2):
        self.x = sb(f"x{tag}", [P, 2, TB, D], F32)
        self.xn = sb(f"xn{tag}", [P, TB, D], F32)
        self.high = sb(f"xhT{tag}", [P, buffers, DC, BLK], F32R)
        self.low = sb(f"xlT{tag}", [P, buffers, DC, BLK], F32R)
        self.buffers = buffers
        self.stats = sb(f"stats{tag}", [P, TB, 6], F32)
        self.mv = sb(f"mv{tag}", [P, TB, 2], F32)
        self.rstd = sb(f"rstd{tag}", [P, TB], F32)
        self.tp = ps(f"tp{tag}", [P, 2, DC, P], F32)
        self.loaded = sems("x_loaded")
        self.summed, self.meaned, self.padded, self.rooted, self.inverted, self.normed = (
            sems(n) for n in ("ln_stats", "ln_mean", "ln_var_eps", "ln_root", "ln_rstd", "ln_out"))
        self.turned, self.high_out, self.ready = sems("xn_turned"), sems("xhT_ready"), sems("xT_ready")

    def parts(self, nb, c, cols=slice(0, BLK)):
        b = nb % self.buffers
        return self.high[:, b, c, cols], self.low[:, b, c, cols]


def load_block(sp, n, x, nb, free=None):
    if nb:
        sp.wait_ge(n.loaded, 16 * nb)
    if free:
        sp.wait_ge(*free)
    sp.dma_start(n.x[:, nb % 2, :, :], x[BLK * nb:BLK * (nb + 1), :].rearrange("(t p) d -> p t d", p=P)
                 ).then_inc(n.loaded, 16)


def norm_stats(dve, n, nb):
    dve.wait_ge(n.loaded, 16 * (nb + 1))
    for i in range(TB):
        dve.bn_stats(n.stats[:, i, :], n.x[:, nb % 2, i, :]).then_inc(n.summed, 1)
    dve.wait_ge(n.summed, TB * (nb + 1))
    for i in range(TB):
        dve.bn_aggr(n.mv[:, i, :], n.stats[:, i, :]).then_inc(n.meaned, 1)
    dve.wait_ge(n.meaned, TB * (nb + 1))
    dve.tensor_scalar(n.mv[:, :, 1], n.mv[:, :, 1], LN_EPS, None, ALU.add).then_inc(n.padded, 1)


def norm_apply(dve, n, nb):
    dve.wait_ge(n.rooted, nb + 1)
    dve.reciprocal(n.rstd[:, :], n.rstd[:, :]).then_inc(n.inverted, 1)
    dve.wait_ge(n.inverted, nb + 1)
    if nb:
        dve.wait_ge(n.turned, TB * nb)
    for i in range(TB):
        dve.tensor_scalar(n.xn[:, i, :], n.x[:, nb % 2, i, :], n.mv[:, i, 0:1], n.rstd[:, i:i + 1],
                          ALU.subtract, ALU.mult).then_inc(n.normed, 1)


def norm_vector(dve, n, nb):
    norm_stats(dve, n, nb)
    norm_apply(dve, n, nb)


def norm_root(act, n, nb):
    act.wait_ge(n.padded, nb + 1)
    act.activation(n.rstd[:, :], n.mv[:, :, 1], ACT.Sqrt).then_inc(n.rooted, 1)


def norm_turn(pe, n, ident, nb, tiles=range(TB)):
    for i in tiles:
        t = TB * nb + i
        pe.wait_ge(n.normed, t + 1)
        if t >= 2:
            pe.wait_ge(n.ready, t - 1)
        for c in range(DC):
            ins = pe.transpose(n.tp[:, i % 2, c, :], n.xn[:, i, c * P:(c + 1) * P], ident[:, :])
        ins.then_inc(n.turned, 1)


def norm_high(act, n, nb):
    for i in range(TB):
        t = TB * nb + i
        act.wait_ge(n.turned, t + 1)
        act.activation(n.high[:, nb % n.buffers, :, i * P:(i + 1) * P], n.tp[:, i % 2, :, :],
                       ACT.Copy).then_inc(n.high_out, 1)


def norm_low(dve, n, nb):
    for i in range(TB):
        t = TB * nb + i
        dve.wait_ge(n.high_out, t + 1)
        cols = slice(i * P, (i + 1) * P)
        dve.tensor_tensor(n.low[:, nb % n.buffers, :, cols], n.tp[:, i % 2, :, :],
                          n.high[:, nb % n.buffers, :, cols].bitcast(F32), ALU.subtract).then_inc(n.ready, 1)


class Weights:

    def __init__(self, sb, sems, tag, aps):
        self.raw, self.high, self.low, self.order = {}, {}, {}, list(aps)
        self.aps = aps
        self.loaded = {k: sems(f"{k}_loaded") for k in aps}
        self.high_out, self.ready = sems("weights_high"), sems("weights_ready")
        for k, ap in aps.items():
            shape = [P, ap.shape[0] // P, ap.shape[1]]
            self.raw[k] = sb(f"{k}_raw{tag}", shape, F32)
            self.high[k], self.low[k] = (sb(f"{k}_{x}{tag}", shape, F32R) for x in ("high", "low"))

    def load(self, sp):
        for k, ap in self.aps.items():
            sp.dma_start(self.raw[k][:, :, :], ap.rearrange("(c p) e -> p c e", p=P)).then_inc(self.loaded[k], 16)

    def split_high(self, act, keys):
        for k in keys:
            act.wait_ge(self.loaded[k], 16)
            act.activation(self.high[k][:, :, :], self.raw[k][:, :, :], ACT.Copy).then_inc(self.high_out, 1)

    def split_low(self, dve, keys):
        for k in keys:
            dve.wait_ge(self.high_out, self.order.index(k) + 1)
            dve.tensor_tensor(self.low[k][:, :, :], self.raw[k][:, :, :], self.high[k][:, :, :].bitcast(F32),
                              ALU.subtract).then_inc(self.ready, 1)

    def count(self, k):
        return self.order.index(k) + 1

    def parts(self, k, c, cols):
        return self.high[k][:, c, cols], self.low[k][:, c, cols]


class Residual:

    def __init__(self, sb, sems, tag):
        self.stats = sb(f"ystats{tag}", [P, 6], F32)
        self.mv = sb(f"ymv{tag}", [P, 2], F32)
        self.rstd = sb(f"yrstd{tag}", [P, 1], F32)
        self.yn = sb(f"yn{tag}", [P, 2, D], F32)
        self.summed, self.meaned, self.padded, self.rooted, self.inverted, self.normed, self.added = (
            sems(n) for n in ("y_stats", "y_mean", "y_var_eps", "y_root", "y_rstd", "y_normed", "x_added"))
        self.stored = sems("x_stored")


def residual_vector(dve, r, y, t):
    dve.bn_stats(r.stats[:, :], y).then_inc(r.summed, 1)
    dve.wait_ge(r.summed, t + 1)
    dve.bn_aggr(r.mv[:, :], r.stats[:, :]).then_inc(r.meaned, 1)
    dve.wait_ge(r.meaned, t + 1)
    dve.tensor_scalar(r.mv[:, 1:2], r.mv[:, 1:2], LN_EPS, None, ALU.add).then_inc(r.padded, 1)
    dve.wait_ge(r.rooted, t + 1)
    dve.reciprocal(r.rstd[:, :], r.rstd[:, :]).then_inc(r.inverted, 1)
    dve.wait_ge(r.inverted, t + 1)
    if t >= 2:
        dve.wait_ge(r.added, t - 1)
    dve.tensor_scalar(r.yn[:, t % 2, :], y, r.mv[:, 0:1], r.rstd[:, :], ALU.subtract,
                      ALU.mult).then_inc(r.normed, 1)


def residual_root(act, r, t):
    act.wait_ge(r.padded, t + 1)
    act.activation(r.rstd[:, :], r.mv[:, 1:2], ACT.Sqrt).then_inc(r.rooted, 1)


def residual_add(pool, r, x, t):
    pool.wait_ge(r.normed, t + 1)
    pool.tensor_tensor(x, x, r.yn[:, t % 2, :], ALU.add).then_inc(r.added, 1)


def store_block(sp, r, n, out, nb):
    sp.wait_ge(r.added, TB * (nb + 1))
    if nb:
        sp.wait_ge(r.stored, 16 * nb)
    sp.dma_start(out[BLK * nb:BLK * (nb + 1), :].rearrange("(t p) d -> p t d", p=P), n.x[:, nb % 2, :, :]
                 ).then_inc(r.stored, 16)


def store_last(sp, r, n, out):
    nb = NB - 1
    sp.wait_ge(r.stored, 16 * nb)
    for i in range(TB):
        sp.wait_ge(r.added, TB * nb + i + 1)
        sp.dma_start(out[BLK * nb + P * i:BLK * nb + P * (i + 1), :], n.x[:, nb % 2, i, :]).then_inc(r.stored, 16)
    sp.wait_ge(r.stored, 16 * (nb + TB))


class BlockResidual:

    def __init__(self, sb, sems, tag, buffers=1):
        self.y = sb(f"y{tag}", [P, buffers, TB, D], F32)
        self.stats = sb(f"ystats{tag}", [P, TB, 6], F32)
        self.mv = sb(f"ymv{tag}", [P, TB, 2], F32)
        self.rstd = sb(f"yrstd{tag}", [P, TB], F32)
        self.buffers = buffers
        self.summed, self.meaned, self.padded, self.rooted, self.inverted, self.normed, self.added = (
            sems(n) for n in ("y_stats", "y_mean", "y_var_eps", "y_root", "y_rstd", "y_normed", "x_added"))
        self.stored = sems("x_stored")

    def tile(self, nb, i):
        return self.y[:, nb % self.buffers, i, :]


def block_residual_stats(dve, r, nb, y_ready):
    for i in range(TB):
        y_ready(i)
        dve.bn_stats(r.stats[:, i, :], r.tile(nb, i)).then_inc(r.summed, 1)
    dve.wait_ge(r.summed, TB * (nb + 1))
    for i in range(TB):
        dve.bn_aggr(r.mv[:, i, :], r.stats[:, i, :]).then_inc(r.meaned, 1)
    dve.wait_ge(r.meaned, TB * (nb + 1))
    dve.tensor_scalar(r.mv[:, :, 1], r.mv[:, :, 1], LN_EPS, None, ALU.add).then_inc(r.padded, 1)


def block_residual_root(act, r, nb):
    act.wait_ge(r.padded, nb + 1)
    act.activation(r.rstd[:, :], r.mv[:, :, 1], ACT.Sqrt).then_inc(r.rooted, 1)


def block_residual_apply(dve, r, nb):
    dve.wait_ge(r.rooted, nb + 1)
    dve.reciprocal(r.rstd[:, :], r.rstd[:, :]).then_inc(r.inverted, 1)
    dve.wait_ge(r.inverted, nb + 1)
    for i in range(TB):
        dve.tensor_scalar(r.tile(nb, i), r.tile(nb, i), r.mv[:, i, 0:1], r.rstd[:, i:i + 1],
                          ALU.subtract, ALU.mult).then_inc(r.normed, 1)


def block_residual_add(pool, r, n, nb):
    for i in range(TB):
        pool.wait_ge(r.normed, TB * nb + i + 1)
        x = n.x[:, nb % 2, i, :]
        pool.tensor_tensor(x, x, r.tile(nb, i), ALU.add).then_inc(r.added, 1)


def project(nc, sb, ps, sems, tag, x, ident, w_aps, outputs, constants=()):
    n_out = len(outputs)
    splits = [u for u, o in enumerate(outputs) if o[0] == "split"]
    vs = [u for u, o in enumerate(outputs) if o[0] == "v"]
    ns, nv = len(splits), len(vs)
    n = Norm(sb, ps, sems, tag)
    parts = sb(f"parts{tag}", [P, ns, 3, BLK], BF16)
    rest = sb(f"rest{tag}", [P, ns, BLK], F32)
    vout = sb(f"vout{tag}", [P, TB, D if nv == TB else outputs[vs[0]][3]], F32)
    w = Weights(sb, sems, tag, w_aps)
    acc = ps(f"acc_ps{tag}", [P, 6, BLK], F32)
    made = sems("product_made")
    passed = sems("pool_passed")
    hi_out, rest_out, mid_out, low_out = (sems(k) for k in (
        "part0_ready", "rest_ready", "part1_ready", "parts_ready"))
    v_out, const_loaded = sems("v_ready"), sems("constants_loaded")
    stored = [sems(f"stored{i}") for i in range(3)]
    assert n_out % 3 == 0

    def stores(u, nb):
        return stored[u % 3], 16 * (nb * (n_out // 3) + u // 3 + 1)

    def bank_free(u, nb, first):
        if u < 6 and first:
            return None
        q, b = (u - 6, nb) if u >= 6 else (n_out + u - 6, nb - 1)
        return (rest_out, b * ns + splits.index(q) + 1) if q in splits else (v_out, b * nv + vs.index(q) + 1)

    with nc.Block() as block:
        @block.sync
        def _(sp):
            for dst, src in constants:
                sp.dma_start(dst, src).then_inc(const_loaded, 16)
            load_block(sp, n, x, 0)
            w.load(sp)
            load_block(sp, n, x, 1)

            def store(nb, first):
                for u, o in enumerate(outputs):
                    if u in splits:
                        s = splits.index(u)
                        sp.wait_ge(low_out, nb * ns + s + 1)
                        src = parts[o[3]:o[3] + o[4], s, :, :]
                    else:
                        s = vs.index(u)
                        sp.wait_ge(v_out, nb * nv + s + 1)
                        src = vout[:, :, :] if o[4] else vout[:, s, :].rearrange("p (g c) -> p g c", g=NG)
                    if not (first and u < 3):
                        sp.wait_ge(*(stores(u - 3, nb) if u >= 3 else stores(n_out + u - 3, nb - 1)))
                    sp.dma_start(o[-1](nb, s), src).then_inc(stored[u % 3], 16)

            for nb in range(NB):
                if nb + 2 < NB:
                    load_block(sp, n, x, nb + 2, (n.normed, TB * (nb + 1)))
                store(nb, nb == 0)
            for u in range(n_out - 3, n_out):
                sp.wait_ge(*stores(u, NB - 1))

        @block.vector
        def _(dve):
            def rests(nb, which):
                for s in which:
                    u = splits[s]
                    o = outputs[u]
                    rows = slice(o[3], o[3] + o[4])
                    dve.wait_ge(hi_out, nb * ns + s + 1)
                    if nb:
                        dve.wait_ge(low_out, (nb - 1) * ns + s + 1)
                    dve.scalar_tensor_tensor(out=rest[rows, s, :], in0=acc[rows, u % 6, :], scalar=o[5],
                                             in1=parts[rows, s, 0, :], op0=ALU.mult, op1=ALU.subtract
                                             ).then_inc(rest_out, 1)

            norm_vector(dve, n, 0)
            w.split_low(dve, w.order[:1])
            norm_low(dve, n, 0)
            w.split_low(dve, w.order[1:])
            for nb in range(NB):
                if nb < NB - 1:
                    norm_vector(dve, n, nb + 1)
                rests(nb, range(0, 4))
                if nb < NB - 1:
                    norm_low(dve, n, nb + 1)
                rests(nb, range(4, ns))

        @block.gpsimd
        def _(pool):
            with pool.Fori(0, NB) as nb:
                for s, u in enumerate(splits):
                    o = outputs[u]
                    rows = slice(o[3], o[3] + o[4])
                    if o[4] < P:
                        pool.wait_ge(low_out, nb * ns + s)
                    pool.wait_ge(rest_out, nb * ns + s + 1)
                    settle(pool, passed)
                    pool.tensor_copy(parts[rows, s, 1, :], rest[rows, s, :]).then_inc(mid_out, 1)
                    pool.wait_ge(mid_out, nb * ns + s + 1)
                    pool.tensor_tensor(parts[rows, s, 2, :], rest[rows, s, :], parts[rows, s, 1, :],
                                       ALU.subtract).then_inc(low_out, 1)
                    if o[4] < P:
                        pool.wait_ge(low_out, nb * ns + s + 1)
                        settle(pool, passed)

        @block.scalar
        def _(act):
            def copies(nb, us, first):
                for u in us:
                    o = outputs[u]
                    act.wait_ge(made, nb * n_out + u + 1)
                    if not first:
                        act.wait_ge(*stores(u, nb - 1))
                    if u in splits:
                        rows = slice(o[3], o[3] + o[4])
                        act.activation(parts[rows, splits.index(u), 0, :], acc[rows, u % 6, :], ACT.Copy,
                                       scale=o[5]).then_inc(hi_out, 1)
                    elif o[4]:
                        act.activation(vout[:, :, :], acc[:, u % 6, 0:TB * o[3]].rearrange(
                            "p (t c) -> p t c", t=TB), ACT.Copy).then_inc(v_out, 1)
                    else:
                        act.activation(vout[:, vs.index(u), :], acc[:, u % 6, :], ACT.Copy).then_inc(v_out, 1)

            norm_root(act, n, 0)
            w.split_high(act, w.order[:1])
            norm_high(act, n, 0)
            w.split_high(act, w.order[1:])
            for nb in range(NB):
                if nb < NB - 1:
                    norm_root(act, n, nb + 1)
                copies(nb, range(0, 4), nb == 0)
                if nb < NB - 1:
                    norm_high(act, n, nb + 1)
                copies(nb, range(4, n_out), nb == 0)

        @block.tensor
        def _(pe):
            def products(nb, us, first):
                for u in us:
                    o = outputs[u]
                    if first:
                        pe.wait_ge(w.ready, w.count(o[1]))
                    old = bank_free(u, nb, first)
                    if old:
                        pe.wait_ge(*old)
                    bank = acc[:, u % 6, :]
                    if u in splits:
                        for c in range(DC):
                            ins = split_product(pe, bank, w.parts(o[1], c, slice(o[2], o[2] + P)), n.parts(nb, c),
                                                c == 0, c == DC - 1)
                    else:
                        for k, t in enumerate(range(TB) if o[4] else [vs.index(u)]):
                            for c in range(DC):
                                ins = split_product(pe, bank[:, k * o[3]:(k + 1) * o[3]],
                                                    n.parts(nb, c, slice(t * P, (t + 1) * P)),
                                                    w.parts(o[1], c, slice(o[2], o[2] + o[3])),
                                                    c == 0, c == DC - 1)
                    ins.then_inc(made, 1)

            if constants:
                pe.wait_ge(const_loaded, 16 * len(constants))
            norm_turn(pe, n, ident, 0)
            for nb in range(NB):
                pe.wait_ge(n.ready, TB * (nb + 1))
                products(nb, range(0, 4), nb == 0)
                if nb < NB - 1:
                    norm_turn(pe, n, ident, nb + 1)
                products(nb, range(4, n_out), nb == 0)


def attention(nc, sb, ps, sems, tag, causal, qparts, kparts, vrows, ot, ident, ident_bf, mask_q, mask_k, fixed_k, bias_q):
    bias_rows = ALIBI if causal else 0
    top = MAIN + bias_rows
    rows = top + SHIFT
    kh = 1 if causal else GH
    qst = sb(f"q_stack{tag}", [rows, 3, 2, GH, HALF], BF16)
    kst = sb(f"k_stack{tag}", [rows, 3, kh, SEQ], BF16)
    vload = sb(f"v_load{tag}", [P, KT, kh, HD], F32)
    vone = sb(f"v_ones{tag}", [P, KT, kh, 2 * HD], F32)
    probs = sb(f"probs{tag}", [P, 16, HALF], F32)
    maxes = sb(f"maxes{tag}", [P, 2, GH * QT], F32)
    mrow = sb(f"mrow{tag}", [GH * QT, P], F32)
    mneg = sb(f"mneg{tag}", [GH * QT, P], F32)
    mrest = sb(f"mrest{tag}", [GH * QT, P], F32)
    mparts = sb(f"mparts{tag}", [GH * QT, 3, P], BF16)
    s_ps = ps(f"s_ps{tag}", [P, 2, SEQ], F32)
    st_ps = ps(f"st_ps{tag}", [P, 3, HALF], F32)
    o_ps = ps(f"o_ps{tag}", [P, HALF], F32)

    stacks, v_in, v_set, fixed = sems("stacks_loaded"), sems("v_loaded"), sems("v_spread"), sems("fixed_rows")
    scored, maxed = sems("row_scores_ready"), sems("row_max_ready")
    st_made, st_used = sems("key_scores_ready"), sems("key_scores_used")
    m_neg, m_part0, m_rest, m_part1, m_parts, m_rows = (sems(n) for n in (
        "max_negated", "max_part0", "max_rest", "max_part1", "max_parts_ready", "max_rows_ready"))
    pv_done, o_out = sems("probs_used"), sems("o_copied")
    passed, sp_passed = sems("pool_passed"), sems("sp_passed")

    steps = [(half, kt, *w) for half in range(2) for kt, w in enumerate(widths(causal, half))]
    n_steps = len(steps)
    first_of = [next(i for i, s in enumerate(steps) if s[0] == half) for half in range(2)]
    row_units = [[(half, qt, h) for qt in range(QT) for h in range(GH)] for half in range(2)]
    units_at = [[] for _ in steps]
    for half in range(2):
        mine = [i for i, s in enumerate(steps) if s[0] == half]
        mine = mine[:-1] if causal and half else mine
        for n, unit in enumerate(row_units[half]):
            units_at[mine[n * len(mine) // len(row_units[half])]].append((half * GH * QT + n, *unit))
    turn_at = [f + (0 if causal else 1) for f in first_of]
    takes = []
    for i, s in enumerate(steps):
        takes += [("exp", i, h) for h in range(GH)]
        if i == turn_at[s[0]]:
            takes.append(("max", s[0], 0))
    where = {t: n for n, t in enumerate(takes)}
    n_takes = len(takes)

    def is_last(it, k=1):
        return isinstance(it, int) and it >= ITS - k

    def bank_of(n):
        return n % 3

    skipped = where[("max", 1, 0)]

    def taken(it, n):
        return 1 + n_takes * it + n + 1 - (1 if is_last(it) and n >= skipped else 0)

    def used_before(it, n):
        m = max(x for x in range(-n_takes, n) if bank_of(x % n_takes) == bank_of(n)
                and not (is_last(it) and x == skipped))
        if m < 0:
            return max(1 + n_takes * it + m + 1, 1) if isinstance(it, int) else 1 + n_takes * it + m + 1
        return taken(it, m)

    def max_take(n):
        group, half = n
        if half == 1:
            return taken(group, where[("max", 0, 0)])
        if isinstance(group, int) and group == 0:
            return 1
        return taken(group - 1, where[("max", 1, 0)])

    ring = 4
    n_loads = 16 * (3 * len(Q_PARTS) + (2 if causal else 0))
    loop = range(1, ITS - 3)
    assert len(loop) % 3 == 0 and n_steps % ring == 0

    def run(engine, body):
        body(0, 0, False)
        with engine.Fori(0, len(loop) // 3) as i:
            for r in range(3):
                body(3 * i + 1 + r, (1 + r) % 3, True)
        for it in range(ITS - 3, ITS):
            body(it, it % 3, True)

    def key_width(half, qt):
        return (half * QT + qt + 1) * P if causal else SEQ

    with nc.Block() as block:
        @block.sync
        def _(sp):
            def load_stacks(it, buf):
                for r, (a, b) in enumerate(zip(Q_PARTS, K_PARTS)):
                    dst = slice(HD * r, HD * r + HD)
                    for half in range(2):
                        sp.dma_start(qst[dst, buf, half, :, :], qparts(a, it, half)).then_inc(stacks, 16)
                    sp.dma_start(kst[dst, buf, :, :], kparts(b, it)).then_inc(stacks, 16)
                if causal:
                    for half in range(2):
                        sp.dma_start(qst[MAIN:top, buf, half, :, :], bias_q(it, half)).then_inc(stacks, 16)

            def load_v(it):
                sp.dma_start(vload[:, :, :, :].rearrange("p k h d -> p k (h d)"), vrows(it)).then_inc(v_in, 16)

            def max_rows(n, half, buf):
                sp.wait_ge(m_parts, n + 1)
                for p in range(SHIFT):
                    sp.dma_start(qst[top + p:top + p + 1, buf, half, :, :].rearrange(
                        "r h (q c) -> r (h q) c", c=P), mparts[:, p, :]).then_inc(m_rows, 16)

            def body(it, buf, before):
                if before:
                    sp.wait_ge(st_made, 1 + n_takes * it)
                max_rows(2 * it + 1, 1, buf)
                if not is_last(it, 2):
                    sp.wait_ge(stacks, n_loads * (it + 2))
                    settle(sp, sp_passed)
                    load_stacks(it + 2, (buf + 2) % 3)
                if not is_last(it):
                    sp.wait_ge(v_set, it + 2)
                    settle(sp, sp_passed)
                    load_v(it + 1)
                if not is_last(it):
                    max_rows(2 * it + 2, 0, (buf + 1) % 3)

            for buf in range(3):
                for h in range(kh):
                    sp.dma_start(kst[MAIN:rows, buf, h, :], fixed_k[ALIBI - bias_rows:, :]).then_inc(fixed, 16)
            load_stacks(0, 0)
            load_v(0)
            sp.wait_ge(stacks, n_loads)
            load_stacks(1, 1)
            max_rows(0, 0, 0)
            run(sp, body)
            sp.wait_ge(m_rows, 16 * SHIFT * 2 * ITS)

        @block.gpsimd
        def _(pool):
            def spread(it, before):
                pool.wait_ge(v_in, 16 * (it + 1))
                if before:
                    pool.wait_ge(pv_done, n_steps * it)
                    settle(pool, passed)
                pool.tensor_copy(vone[:, :, :, 0:HD], vload[:, :, :, :]).then_inc(v_set, 1)

            def split_max(n, turned, before):
                pool.wait_ge(st_used, max_take(turned))
                settle(pool, passed)
                pool.tensor_scalar(mneg[:, :], mrow[:, :], -1.0, None, ALU.mult).then_inc(m_neg, 1)
                pool.wait_ge(m_neg, n + 1)
                if before:
                    pool.wait_ge(m_rows, 16 * SHIFT * n)
                    settle(pool, passed)
                pool.tensor_copy(mparts[:, 0, :], mneg[:, :]).then_inc(m_part0, 1)
                pool.wait_ge(m_part0, n + 1)
                pool.tensor_tensor(mrest[:, :], mneg[:, :], mparts[:, 0, :], ALU.subtract).then_inc(m_rest, 1)
                pool.wait_ge(m_rest, n + 1)
                settle(pool, passed)
                pool.tensor_copy(mparts[:, 1, :], mrest[:, :]).then_inc(m_part1, 1)
                pool.wait_ge(m_part1, n + 1)
                pool.tensor_tensor(mparts[:, 2, :], mrest[:, :], mparts[:, 1, :], ALU.subtract).then_inc(m_parts, 1)

            def body(it, before, last):
                spread(it, before)
                split_max(2 * it + 1, (it, 1), True)
                if not last:
                    split_max(2 * it + 2, (it + 1, 0), True)

            pool.memset(vone[:, :, :, :], 1.0).then_inc(v_set, 1)
            pool.wait_ge(v_set, 1)
            split_max(0, (0, 0), False)
            body(0, False, False)
            with pool.Fori(1, ITS - 1) as it:
                body(it, True, False)
            body(ITS - 1, True, True)

        @block.scalar
        def _(act):
            def body(it, before, last):
                for n, (kind, i, h) in enumerate(takes):
                    if kind == "max" and last and i == 1:
                        continue
                    act.wait_ge(st_made, taken(it, n))
                    if kind == "max":
                        act.wait_ge(m_neg, 2 * it + 1 + i)
                        act.activation(mrow[:, :], st_ps[0:GH * QT, bank_of(n), 0:P],
                                       ACT.Copy).then_inc(st_used, 1)
                        continue
                    first = steps[i][2]
                    if h == 0 and (before or i >= ring):
                        act.wait_ge(pv_done, n_steps * it + i - ring + 1)
                    act.activation(probs[:, (i % ring) * GH + h, first:HALF], st_ps[:, bank_of(n), first:HALF],
                                   ACT.Exp).then_inc(st_used, 1)

            act.wait_ge(st_made, 1)
            act.activation(mrow[:, :], st_ps[0:GH * QT, 2, 0:P], ACT.Copy).then_inc(st_used, 1)
            body(0, False, False)
            with act.Fori(1, ITS - 1) as it:
                body(it, True, False)
            body(ITS - 1, True, True)

        @block.vector
        def _(dve):
            def maximum(group, n, half, qt, h):
                dve.wait_ge(scored, 2 * GH * QT * group + n + 1)
                dve.reduce_max(maxes[:, half, h * QT + qt:h * QT + qt + 1],
                               s_ps[:, n % 2, 0:key_width(half, qt)], AX.X).then_inc(maxed, 1)

            def copy_o(it, half):
                dve.wait_ge(pv_done, n_steps * it + (first_of[1] if half == 0 else n_steps))
                dve.tensor_copy(ot(it, half), o_ps[:, :]).then_inc(o_out, 1)

            def body(it, before, last):
                for i in range(n_steps):
                    for n, half, qt, h in units_at[i] if not last else ():
                        if n == half * GH * QT:
                            dve.wait_ge(st_made, max_take((it, half)))
                        maximum(it + 1, n, half, qt, h)
                    if i == 0 and before:
                        copy_o(it - 1, 1)
                    if i == first_of[1]:
                        copy_o(it, 0)

            for half in range(2):
                for n, (_, qt, h) in enumerate(row_units[half]):
                    maximum(0, half * GH * QT + n, half, qt, h)
            body(0, False, False)
            with dve.Fori(1, ITS - 1) as it:
                body(it, True, False)
            body(ITS - 1, True, True)
            copy_o(ITS - 1, 1)

        @block.tensor
        def _(pe):
            def row_scores(group, buf, n, half, qt, h):
                if not (isinstance(group, int) and group == 0 and n < 2):
                    pe.wait_ge(maxed, 2 * GH * QT * group + n - 1)
                q = qst[0:top, buf, half, h, qt * P:(qt + 1) * P]
                width = key_width(half, qt)
                for a in range(0, width, HALF):
                    b = min(a + HALF, width)
                    masked = causal and b == width
                    ins = pe.matmul(s_ps[:, n % 2, a:b], q, kst[0:top, buf, h % kh, a:b],
                                    start=True, stop=not masked)
                    if masked:
                        ins = pe.matmul(s_ps[:, n % 2, width - P:width], ident_bf[:, :], mask_q[:, :],
                                        start=False, stop=True)
                ins.then_inc(scored, 1)

            def turn_max(group, half, bank):
                pe.wait_ge(maxed, 2 * GH * QT * group + (half + 1) * GH * QT)
                pe.matmul(st_ps[0:GH * QT, bank, 0:P], maxes[:, half, :], ident[:, :],
                          start=True, stop=True).then_inc(st_made, 1)

            def values(it, i):
                half, kt, first, _ = steps[i]
                if i == 0:
                    pe.wait_ge(v_set, it + 2)
                if kt == 0 and not (isinstance(it, int) and it == 0 and half == 0):
                    pe.wait_ge(o_out, 2 * it + half)
                last = i == n_steps - 1 or steps[i + 1][0] != half
                pe.wait_ge(st_used, taken(it, where[("exp", i, GH - 1)]))
                for h in range(GH):
                    ins = pe.matmul(o_ps[32 * h:32 * h + 32, first:HALF], vone[:, kt, h % kh, :],
                                    probs[:, (i % ring) * GH + h, first:HALF], start=kt == 0, stop=last)
                ins.then_inc(pv_done, 1)

            def body(it, buf, before):
                last = is_last(it)
                if not last:
                    pe.wait_ge(stacks, n_loads * (it + 2))
                for i, (half, kt, first, diagonal) in enumerate(steps):
                    if i == first_of[half]:
                        pe.wait_ge(m_rows, 16 * SHIFT * (2 * it + half + 1))
                    units = [] if last else list(units_at[i])
                    spacing = -(-len(units) // 2)
                    for h in range(GH):
                        n = where[("exp", i, h)]
                        pe.wait_ge(st_used, used_before(it, n))
                        bank = st_ps[:, bank_of(n), :]
                        ins = pe.matmul(bank[:, first:HALF], kst[0:rows, buf, h % kh, kt * P:(kt + 1) * P],
                                        qst[0:rows, buf, half, h, first:HALF], start=True, stop=not diagonal)
                        if diagonal:
                            ins = pe.matmul(bank[:, first:first + P], ident_bf[:, :], mask_k[:, :],
                                            start=False, stop=True)
                        ins.then_inc(st_made, 1)
                        if h % 2:
                            for unit in units[:spacing]:
                                row_scores(it + 1, (buf + 1) % 3, *unit)
                            units = units[spacing:]
                    if i == 0 and before:
                        values(it - 1, n_steps - 1)
                    if i > 0:
                        values(it, i - 1)
                    if i == turn_at[half] and not (last and half == 1):
                        n = where[("max", half, 0)]
                        pe.wait_ge(st_used, used_before(it, n))
                        turn_max(it + half, 1 - half, bank_of(n))

            pe.wait_ge(stacks, n_loads)
            pe.wait_ge(v_set, 1)
            pe.wait_ge(fixed, 16 * 3 * kh)
            for half in range(2):
                for n, (_, qt, h) in enumerate(row_units[half]):
                    row_scores(0, 0, half * GH * QT + n, half, qt, h)
                if half == 0:
                    turn_max(0, 0, 2)
            run(pe, body)
            values(ITS - 1, n_steps - 1)


def output(nc, sb, ps, sems, tag, x, x_out, ident, ot, wo_ap):
    w = Weights(sb, sems, tag, {"wo": wo_ap})
    xt = sb(f"xt{tag}", [P, 2, TB, D], F32)
    recip = sb(f"recip{tag}", [P, HEADS], F32)
    on = sb(f"on{tag}", [P, D], F32)
    onh = sb(f"onhT{tag}", [P, DC, P], F32R)
    onl = sb(f"onlT{tag}", [P, DC, P], F32R)
    r = Residual(sb, sems, tag)
    a_ps = ps(f"a_ps{tag}", [P, 2, NG, P], F32)
    b_ps = ps(f"b_ps{tag}", [P, 2, DC, P], F32)
    y_ps = ps(f"y_ps{tag}", [P, 2, D], F32)
    x_loaded, turned, inverted, scaled = sems("x_loaded"), sems("o_turned"), sems("sums_inverted"), sems("o_scaled")
    back, high_out, ready, made = sems("o_turned_back"), sems("ohT_ready"), sems("oT_ready"), sems("y_made")

    with nc.Block() as block:
        @block.sync
        def _(sp):
            w.load(sp)
            for nb in range(NB + 1):
                if nb < NB:
                    if nb:
                        sp.wait_ge(x_loaded, 16 * nb)
                    if nb >= 2:
                        sp.wait_ge(r.stored, 16 * (nb - 1))
                    sp.dma_start(xt[:, nb % 2, :, :], x[BLK * nb:BLK * (nb + 1), :].rearrange(
                        "(t p) d -> p t d", p=P)).then_inc(x_loaded, 16)
                if nb:
                    sp.wait_ge(r.added, TB * nb)
                    if nb > 1:
                        sp.wait_ge(r.stored, 16 * (nb - 1))
                    sp.dma_start(x_out[BLK * (nb - 1):BLK * nb, :].rearrange("(t p) d -> p t d", p=P),
                                 xt[:, (nb - 1) % 2, :, :]).then_inc(r.stored, 16)
            sp.wait_ge(r.stored, 16 * NB)

        @block.tensor
        def _(pe):
            def turn(t):
                if t >= 2:
                    pe.wait_ge(scaled, t - 1)
                for g in range(NG):
                    ins = pe.transpose(a_ps[:, t % 2, g, :], ot(t // (SEQ // P), g, t % (SEQ // P)), ident[:, :])
                ins.then_inc(turned, 1)

            turn(0)
            for t in range(NT):
                pe.wait_ge(scaled, t + 1)
                if t >= 2:
                    pe.wait_ge(ready, t - 1)
                for c in range(DC):
                    ins = pe.transpose(b_ps[:, t % 2, c, :], on[:, c * P:(c + 1) * P], ident[:, :])
                ins.then_inc(back, 1)
                if t < NT - 1:
                    turn(t + 1)
                if t == 0:
                    pe.wait_ge(w.ready, 1)
                pe.wait_ge(ready, t + 1)
                if t >= 2:
                    pe.wait_ge(r.normed, t - 1)
                for c in range(DC):
                    ins = split_product(pe, y_ps[:, t % 2, :], (onh[:, c, :], onl[:, c, :]),
                                        w.parts("wo", c, slice(0, D)), c == 0, c == DC - 1)
                ins.then_inc(made, 1)

        @block.vector
        def _(dve):
            def scale(t):
                dve.wait_ge(turned, t + 1)
                sums = a_ps[:, t % 2, :, :].rearrange("p g (h c) -> p (g h) c", h=GH)
                dve.reciprocal(recip[:, :], sums[:, :, HD]).then_inc(inverted, 1)
                dve.wait_ge(inverted, t + 1)
                if t:
                    dve.wait_ge(back, t)
                dve.tensor_tensor(on[:, :].rearrange("p (h c) -> p h c", c=HD), sums[:, :, 0:HD],
                                  recip[:, :].rearrange("p (h a) -> p h a", a=1).broadcast_to([P, HEADS, HD]),
                                  ALU.mult).then_inc(scaled, 1)

            scale(0)
            w.split_low(dve, w.order)
            for t in range(NT):
                dve.wait_ge(high_out, t + 1)
                if t:
                    dve.wait_ge(made, t)
                dve.tensor_tensor(onl[:, :, :], b_ps[:, t % 2, :, :], onh[:, :, :].bitcast(F32),
                                  ALU.subtract).then_inc(ready, 1)
                if t < NT - 1:
                    scale(t + 1)
                if t:
                    residual_vector(dve, r, y_ps[:, (t - 1) % 2, :], t - 1)
            dve.wait_ge(made, NT)
            residual_vector(dve, r, y_ps[:, (NT - 1) % 2, :], NT - 1)

        @block.scalar
        def _(act):
            w.split_high(act, w.order)
            for t in range(NT):
                act.wait_ge(back, t + 1)
                if t:
                    act.wait_ge(made, t)
                act.activation(onh[:, :, :], b_ps[:, t % 2, :, :], ACT.Copy).then_inc(high_out, 1)
                if t:
                    residual_root(act, r, t - 1)
            residual_root(act, r, NT - 1)

        @block.gpsimd
        def _(pool):
            for t in range(NT):
                if t % TB == 0:
                    pool.wait_ge(x_loaded, 16 * (t // TB + 1))
                residual_add(pool, r, xt[:, t // TB % 2, t % TB, :], t)


def gated_ffn(nc, sb, ps, sems, tag, x, x_out, ident, gate_w, gate_s, up_w, up_s, down_w, down_s):
    n, r = Norm(sb, ps, sems, tag, buffers=1), BlockResidual(sb, sems, tag)
    wg, wu = ([sb(f"w{k}_{x_}{tag}", [P, DC, FF], F32R) for x_ in ("high", "low")] for k in "gu")
    wd = [sb(f"wd_{x_}{tag}", [P, FT, D], F32R) for x_ in ("high", "low")]
    sg = sb(f"sg{tag}", [P, FT], F32)
    su = sb(f"su{tag}", [P, FT], F32)
    ds = sb(f"ds{tag}", [P, D], F32)
    silu = sb(f"silu{tag}", [P, BLK], F32)
    h = sb(f"h{tag}", [P, BLK], F32)
    hh = sb(f"hh{tag}", [P, 2, BLK], F32R)
    hl = sb(f"hl{tag}", [P, 2, BLK], F32R)
    g_ps = ps(f"g_ps{tag}", [P, BLK], F32)
    u_ps = ps(f"u_ps{tag}", [P, BLK], F32)
    y_ps = ps(f"y_ps{tag}", [P, TB, D], F32)
    s_loaded, w_high, w_low = sems("scales_loaded"), sems("w_high"), sems("w_low")
    g_made, u_made, silu_out, h_out, hh_out, hl_out, y_made, y_scaled = (sems(k) for k in (
        "gate", "up", "silu_ready", "h_ready", "h_high", "h_low", "y_made", "y_scaled"))
    tile_made = sems("y_tile_made")
    frows = [P] * (FT - 1) + [FLAST]

    pieces, piece_of = [], {}

    def gate_up_piece(j0, j1):
        cols = slice(j0 * P, min(j1 * P, FF))
        for k, w_ap in ((wg, gate_w), (wu, up_w)):
            pieces.append((w_ap.rearrange("(c p) f -> p c f", p=P)[:, :, cols], k[0][:, :, cols], k[1][:, :, cols]))
        piece_of.update({("gu", j): len(pieces) for j in range(j0, j1)})

    def down_piece(j0, j1):
        k = frows[j0]
        src = down_w[j0 * P:min(j1 * P, FF), :].rearrange("(j p) d -> p j d", p=k)
        pieces.append((src, wd[0][0:k, j0:j1, :], wd[1][0:k, j0:j1, :]))
        piece_of.update({("d", j): len(pieces) for j in range(j0, j1)})

    gate_up_piece(0, 1)
    gate_up_piece(1, 3)
    down_piece(0, 1)
    for j in range(1, 9, 2):
        down_piece(j, j + 2)
        gate_up_piece(j + 2, j + 4)
    down_piece(9, 10)
    down_piece(10, FT)
    first, second = (0, 1), (2, 3)
    later = {0: (4, 5), 1: (6, 7), 2: (8,), 3: (9, 10), 4: (11,), 5: (12, 13), 6: (14,), 7: (15, 16), 8: (17,), 9: (18,)}
    assert len(pieces) == 19
    land = sb(f"land{tag}", [P, 2, 2 * D], I32)
    landed = [sems(f"w_landed{i}") for i in range(4)]

    def landing(i):
        rows, middle, cols = pieces[i][1].shape
        slot = i % 4
        room = land[0:rows, slot, :] if slot < 2 else r.y[0:rows, 0, 2 * slot - 4:2 * slot - 2, :].rearrange(
            "p a c -> p (a c)").bitcast(I32)
        return room[:, 0:middle * cols].rearrange("p (m c) -> p m c", m=middle)

    with nc.Block() as block:
        @block.sync
        def _(sp):
            load_block(sp, n, x, 0)
            for i, piece in enumerate(pieces):
                if i >= 4:
                    sp.wait_ge(w_low, i - 3)
                sp.dma_start(landing(i), piece[0]).then_inc(landed[i % 4], 16)
                if i == 1:
                    for dst, src in ((sg, gate_s), (su, up_s), (ds, down_s)):
                        sp.dma_start(dst[:, :], src).then_inc(s_loaded, 16)
                if i == 3:
                    load_block(sp, n, x, 1)
            for nb in range(NB - 1):
                store_block(sp, r, n, x_out, nb)
                if nb + 2 < NB:
                    load_block(sp, n, x, nb + 2, (r.stored, 16 * (nb + 1)))
            store_last(sp, r, n, x_out)

        @block.gpsimd
        def _(pool):
            for nb in range(NB):
                block_residual_add(pool, r, n, nb)

        @block.scalar
        def _(act):
            def high(which):
                for i in which:
                    act.wait_ge(landed[i % 4], 16 * (i // 4 + 1))
                    act.activation(pieces[i][1], landing(i), ACT.Copy).then_inc(w_high, 1)

            norm_root(act, n, 0)
            high(first)
            norm_high(act, n, 0)
            high(second)
            act.wait_ge(s_loaded, 16 * 3)
            for nb in range(NB):
                for j, k in enumerate(frows):
                    c = nb * FT + j
                    act.wait_ge(g_made, c + 1)
                    if c:
                        act.wait_ge(h_out, c)
                    act.activation(silu[0:k, :], g_ps[0:k, :], ACT.Silu, scale=sg[0:k, j:j + 1]).then_inc(silu_out, 1)
                    act.wait_ge(h_out, c + 1)
                    if c >= 2:
                        old_nb, old_j = divmod(c - 2, FT)
                        if old_j == FT - 1:
                            act.wait_ge(tile_made, TB * (old_nb + 1))
                        else:
                            act.wait_ge(y_made, (FT - 1) * old_nb + old_j + 1)
                    act.activation(hh[0:k, c % 2, :], h[0:k, :], ACT.Copy).then_inc(hh_out, 1)
                    if nb == 0:
                        high(later.get(j, ()))
                    if nb and j == 1:
                        block_residual_root(act, r, nb - 1)
                    if nb < NB - 1 and j == 6:
                        norm_root(act, n, nb + 1)
                if nb < NB - 1:
                    norm_high(act, n, nb + 1)
            block_residual_root(act, r, NB - 1)

        @block.vector
        def _(dve):
            def low(which):
                for i in which:
                    dve.wait_ge(w_high, i + 1)
                    dve.tensor_tensor(pieces[i][2], landing(i), pieces[i][1].bitcast(F32),
                                      ALU.subtract).then_inc(w_low, 1)

            norm_stats(dve, n, 0)
            norm_apply(dve, n, 0)
            low(first)
            norm_low(dve, n, 0)
            low(second)
            dve.wait_ge(s_loaded, 16 * 3)
            for nb in range(NB):
                for j, k in enumerate(frows):
                    c = nb * FT + j
                    dve.wait_ge(u_made, c + 1)
                    dve.wait_ge(silu_out, c + 1)
                    if c:
                        dve.wait_ge(hl_out, c)
                    dve.scalar_tensor_tensor(out=h[0:k, :], in0=u_ps[0:k, :], scalar=su[0:k, j:j + 1],
                                             in1=silu[0:k, :], op0=ALU.mult, op1=ALU.mult).then_inc(h_out, 1)
                    dve.wait_ge(hh_out, c + 1)
                    dve.tensor_tensor(hl[0:k, c % 2, :], h[0:k, :], hh[0:k, c % 2, :].bitcast(F32),
                                      ALU.subtract).then_inc(hl_out, 1)
                    if nb == 0:
                        low(later.get(j, ()))
                    if nb and j == 1:
                        block_residual_stats(dve, r, nb - 1, lambda i: None)
                    if nb and j == 2:
                        block_residual_apply(dve, r, nb - 1)
                    if nb < NB - 1 and j == 6:
                        norm_stats(dve, n, nb + 1)
                    if nb < NB - 1 and j == 8:
                        norm_apply(dve, n, nb + 1)
                if nb < NB - 1:
                    norm_low(dve, n, nb + 1)
                if nb:
                    dve.wait_ge(r.added, TB * nb)
                for i in range(TB):
                    dve.wait_ge(tile_made, TB * nb + i + 1)
                    dve.tensor_tensor(r.tile(nb, i), y_ps[:, i, :], ds[:, :], ALU.mult).then_inc(y_scaled, 1)
                dve.wait_ge(y_scaled, TB * (nb + 1))
            block_residual_stats(dve, r, NB - 1, lambda i: None)
            block_residual_apply(dve, r, NB - 1)

        @block.tensor
        def _(pe):
            def down(nb, j):
                k, c = frows[j], nb * FT + j
                if nb == 0:
                    pe.wait_ge(w_low, piece_of["d", j])
                pe.wait_ge(hl_out, c + 1)
                if nb and j == 0:
                    pe.wait_ge(y_scaled, TB * nb)
                for i in range(TB):
                    cols = slice(i * P, (i + 1) * P)
                    ins = split_product(pe, y_ps[:, i, :], (hh[0:k, c % 2, cols], hl[0:k, c % 2, cols]),
                                        (wd[0][0:k, j, :], wd[1][0:k, j, :]), j == 0, j == FT - 1)
                    if j == FT - 1:
                        ins.then_inc(tile_made, 1)
                if j < FT - 1:
                    ins.then_inc(y_made, 1)

            norm_turn(pe, n, ident, 0)
            for nb in range(NB):
                pe.wait_ge(n.ready, TB * (nb + 1))
                for j, k in enumerate(frows):
                    c = nb * FT + j
                    for w, bank, old, made in ((wg, g_ps, silu_out, g_made), (wu, u_ps, h_out, u_made)):
                        if c:
                            pe.wait_ge(old, c)
                        if nb == 0:
                            pe.wait_ge(w_low, piece_of["gu", j])
                        for d in range(DC):
                            cols = slice(j * P, j * P + k)
                            ins = split_product(pe, bank[0:k, :], (w[0][:, d, cols], w[1][:, d, cols]),
                                                n.parts(nb, d), d == 0, d == DC - 1)
                        ins.then_inc(made, 1)
                    if j == FT - 1 and nb < NB - 1:
                        norm_turn(pe, n, ident, nb + 1, range(0, 2))
                    if j:
                        down(nb, j - 1)
                if nb < NB - 1:
                    norm_turn(pe, n, ident, nb + 1, range(2, TB))
                down(nb, FT - 1)


def adapter_ffn(nc, sb, ps, sems, tag, x, out, ident, w_ap, b_ap, a_ap, bm_ap, p_ap):
    n, r = Norm(sb, ps, sems, tag), Residual(sb, sems, tag)
    w = Weights(sb, sems, tag, {"a": a_ap, "w": w_ap, "bm": bm_ap})
    bias = sb(f"bias{tag}", [P, D], F32)
    scores = sb(f"scores{tag}", [ER, 1], F32)
    uT = sb(f"uT{tag}", [ER, BLK], F32)
    uh = sb(f"uhT{tag}", [ER, 2, BLK], F32R)
    ul = sb(f"ulT{tag}", [ER, 2, BLK], F32R)
    z = sb(f"z{tag}", [P, 2, D], F32)
    y = sb(f"y{tag}", [P, 2, D], F32)
    square = sb(f"square{tag}", [P, 2, D], F32)
    norms = sb(f"norms{tag}", [P, 2, 2], F32)
    gamma = sb(f"gamma{tag}", [P, 3], F32)
    u_ps = ps(f"u_ps{tag}", [ER, BLK], F32)
    z_ps = ps(f"z_ps{tag}", [P, 2, D], F32)
    m_ps = ps(f"m_ps{tag}", [P, 2, D], F32)
    c_loaded, u_made, u_scaled, uh_out, u_out, z_made, m_made, z_out = (sems(k) for k in (
        "bias_loaded", "u_made", "u_scaled", "uh_ready", "uT_ready", "z_made", "m_made", "z_ready"))
    z_squared, m_squared, roots, g_steps = (sems(k) for k in (
        "z_squared", "m_squared", "norms_ready", "gamma_steps"))

    with nc.Block() as block:
        @block.sync
        def _(sp):
            load_block(sp, n, x, 0)
            w.load(sp)
            sp.dma_start(bias[:, :], b_ap).then_inc(c_loaded, 16)
            sp.dma_start(scores[:, :], p_ap).then_inc(c_loaded, 16)
            load_block(sp, n, x, 1)
            for nb in range(NB):
                store_block(sp, r, n, out, nb)
                if nb + 2 < NB:
                    load_block(sp, n, x, nb + 2, (r.stored, 16 * (nb + 1)))
            sp.wait_ge(r.stored, 16 * NB)

        @block.gpsimd
        def _(pool):
            for t in range(NT):
                residual_add(pool, r, n.x[:, t // TB % 2, t % TB, :], t)

        @block.scalar
        def _(act):
            norm_root(act, n, 0)
            w.split_high(act, ["a"])
            norm_high(act, n, 0)
            w.split_high(act, ["w", "bm"])
            act.wait_ge(c_loaded, 16 * 2)
            for nb in range(NB):
                if nb < NB - 1:
                    norm_root(act, n, nb + 1)
                act.wait_ge(u_made, nb + 1)
                if nb:
                    act.wait_ge(u_out, nb)
                act.activation(uT[:, :], u_ps[:, :], ACT.Copy, scale=scores[:, 0:1]).then_inc(u_scaled, 1)
                act.wait_ge(u_scaled, nb + 1)
                act.activation(uh[:, nb % 2, :], uT[:, :], ACT.Copy).then_inc(uh_out, 1)
                for i in range(TB):
                    t = TB * nb + i
                    par = t % 2
                    act.wait_ge(z_out, t + 1)
                    if t >= 2:
                        act.wait_ge(g_steps, 5 * (t - 1))
                    if t:
                        act.wait_ge(roots, t)
                    act.activation(square[:, 0, :], z[:, par, :], ACT.Square,
                                   accum_out=norms[:, par, 0:1]).then_inc(z_squared, 1)
                    act.wait_ge(m_made, t + 1)
                    act.activation(square[:, 1, :], m_ps[:, par, :], ACT.Square,
                                   accum_out=norms[:, par, 1:2]).then_inc(m_squared, 1)
                    act.wait_ge(z_squared, t + 1)
                    act.wait_ge(m_squared, t + 1)
                    act.activation(norms[:, par, :], norms[:, par, :], ACT.Sqrt).then_inc(roots, 1)
                    if i == 1 and nb < NB - 1:
                        norm_high(act, n, nb + 1)
                    residual_root(act, r, t)

        @block.vector
        def _(dve):
            norm_vector(dve, n, 0)
            w.split_low(dve, ["a"])
            norm_low(dve, n, 0)
            w.split_low(dve, ["w", "bm"])
            dve.wait_ge(c_loaded, 16 * 2)
            for nb in range(NB):
                if nb < NB - 1:
                    norm_vector(dve, n, nb + 1)
                dve.wait_ge(uh_out, nb + 1)
                if nb >= 2:
                    dve.wait_ge(m_made, TB * (nb - 1))
                dve.tensor_tensor(ul[:, nb % 2, :], uT[:, :], uh[:, nb % 2, :].bitcast(F32),
                                  ALU.subtract).then_inc(u_out, 1)
                for i in range(TB):
                    t = TB * nb + i
                    par = t % 2
                    dve.wait_ge(z_made, t + 1)
                    dve.tensor_tensor(z[:, par, :], z_ps[:, par, :], bias[:, :], ALU.add).then_inc(z_out, 1)
                    if i == 1 and nb < NB - 1:
                        norm_low(dve, n, nb + 1)
                    dve.wait_ge(roots, t + 1)
                    dve.tensor_scalar(gamma[:, 0:1], norms[:, par, 1:2], NORM_EPS, None, ALU.add).then_inc(g_steps, 1)
                    dve.wait_ge(g_steps, 5 * t + 1)
                    dve.reciprocal(gamma[:, 1:2], gamma[:, 0:1]).then_inc(g_steps, 1)
                    dve.wait_ge(g_steps, 5 * t + 2)
                    dve.scalar_tensor_tensor(out=gamma[:, 2:3], in0=norms[:, par, 0:1], scalar=CLAMP,
                                             in1=gamma[:, 1:2], op0=ALU.mult, op1=ALU.mult).then_inc(g_steps, 1)
                    dve.wait_ge(g_steps, 5 * t + 3)
                    dve.tensor_scalar(gamma[:, 2:3], gamma[:, 2:3], 1.0, None, ALU.min).then_inc(g_steps, 1)
                    dve.wait_ge(g_steps, 5 * t + 4)
                    dve.wait_ge(m_squared, t + 1)
                    dve.scalar_tensor_tensor(out=y[:, par, :], in0=m_ps[:, par, :], scalar=gamma[:, 2:3],
                                             in1=z[:, par, :], op0=ALU.mult, op1=ALU.add).then_inc(g_steps, 1)
                    dve.wait_ge(g_steps, 5 * t + 5)
                    residual_vector(dve, r, y[:, par, :], t)

        @block.tensor
        def _(pe):
            norm_turn(pe, n, ident, 0)
            for nb in range(NB):
                pe.wait_ge(n.ready, TB * (nb + 1))
                if nb:
                    pe.wait_ge(u_scaled, nb)
                else:
                    pe.wait_ge(w.ready, w.count("a"))
                for c in range(DC):
                    ins = split_product(pe, u_ps[:, :], w.parts("a", c, slice(0, ER)), n.parts(nb, c),
                                        c == 0, c == DC - 1)
                ins.then_inc(u_made, 1)
                if nb == 0:
                    pe.wait_ge(w.ready, w.count("bm"))
                for i in range(TB):
                    t = TB * nb + i
                    cols = slice(i * P, (i + 1) * P)
                    if t >= 2:
                        pe.wait_ge(z_out, t - 1)
                    for c in range(DC):
                        ins = split_product(pe, z_ps[:, t % 2, :], n.parts(nb, c, cols),
                                            w.parts("w", c, slice(0, D)), c == 0, c == DC - 1)
                    ins.then_inc(z_made, 1)
                    pe.wait_ge(u_out, nb + 1)
                    if t >= 2:
                        pe.wait_ge(g_steps, 5 * (t - 1))
                    split_product(pe, m_ps[:, t % 2, :], (uh[:, nb % 2, cols], ul[:, nb % 2, cols]),
                                  w.parts("bm", 0, slice(0, D)), True, True).then_inc(m_made, 1)
                    if i == 1 and nb < NB - 1:
                        norm_turn(pe, n, ident, nb + 1)


def build(nc, x, w_q, w_k, w_v, w_o, gate_w, gate_s, up_w, up_s, down_w, down_s, wqkv, wo1, w1, b1, a1, bm1,
          p1, ident_in, ident_bf_in, mask_q_in, mask_k_in, fixed_k, bias_q_in, out, stop=99):
    with ExitStack() as whole:
        xs = [x] + [nc.dram_tensor(f"x{k}", (TOK, D), F32, kind="Internal").ap() for k in range(1, 4)] + [out]
        ident = whole.enter_context(nc.sbuf_tensor("ident", [P, P], F32))
        ident_bf = whole.enter_context(nc.sbuf_tensor("ident_bf", [P, P], BF16))
        mask_q = whole.enter_context(nc.sbuf_tensor("mask_q", [P, P], BF16))
        mask_k = whole.enter_context(nc.sbuf_tensor("mask_k", [P, P], BF16))
        q_parts = [nc.dram_tensor(f"q_parts{l}", (3, ITS, GH * HD, SEQ), BF16, kind="Internal").ap() for l in range(2)]
        k_parts = [nc.dram_tensor("k_parts0", (3, ITS, GH * HD, SEQ), BF16, kind="Internal").ap(),
                   nc.dram_tensor("k_parts1", (3, BATCH, HD, SEQ), BF16, kind="Internal").ap()]
        v_rows = [nc.dram_tensor("v_rows0", (ITS, P, KT, GH * HD), F32, kind="Internal").ap(),
                  nc.dram_tensor("v_rows1", (BATCH, P, KT, HD), F32, kind="Internal").ap()]

        def one(i):
            return slice(i, i + 1) if isinstance(i, int) else bass.ds(i, 1)

        def store_parts(scratch, j):
            def to(nb, s):
                b, th = nb // 2, nb % 2
                v = scratch.rearrange("c (b i) e (h t) -> c b (i e) h t", b=BATCH, h=2)
                return v[:, one(b), j * P:(j + 1) * P, one(th), :].rearrange("c b e h t -> (b e h) c t")
            return to

        def store_k1(nb, s):
            v = k_parts[1].rearrange("c b e (h t) -> c b e h t", h=2)
            return v[:, one(nb // 2), :, one(nb % 2), :].rearrange("c b e h t -> (b e h) c t")

        def store_v0(nb, s):
            v = v_rows[0].rearrange("(b g) p (h k) c -> b h k p g c", b=BATCH, h=2)
            return v[one(nb // 2), one(nb % 2), s].rearrange("b h p g c -> (b h p) g c")

        def store_v1(nb, s):
            v = v_rows[1].rearrange("b p (h k) c -> b h p k c", h=2)
            return v[one(nb // 2), one(nb % 2)].rearrange("b h p k c -> (b h p) k c")

        phases = [0]

        def phase():
            ctx, mine = ExitStack(), []
            phases[0] += 1
            number = phases[0]

            def sb(name, shape, dt):
                return ctx.enter_context(nc.sbuf_tensor(name, shape, dt))

            def ps(name, shape, dt):
                return ctx.enter_context(nc.psum_tensor(name, shape, dt))

            def sems(name):
                mine.append(nc.alloc_semaphore(f"{name}_{number}"))
                return mine[-1]

            def give_back():
                nc.clear_and_free_semaphores(mine)
                nc.all_engine_barrier()

            ctx.callback(give_back)
            return ctx, sb, ps, sems

        out0 = [("split", "q", j * P, 0, P, SCALE, store_parts(q_parts[0], j)) for j in range(DC)]
        out0 += [("split", "k", j * P, 0, P, 1.0, store_parts(k_parts[0], j)) for j in range(DC)]
        out0 += [("v", "v", 0, D, False, store_v0)] * TB
        out0 = out0[:8] + [("v", "v", 0, D, False, store_v0) for _ in range(TB)]
        kv = HEADS * HD + 2 * HD - P
        out1 = [("split", "qkv", j * P, 0, P, SCALE, store_parts(q_parts[1], j)) for j in range(DC)]
        out1 += [("split", "qkv", kv, P - 2 * HD, HD, 1.0, store_k1),
                 ("v", "qkv", HEADS * HD + HD, HD, True, store_v1)]
        consts = [(ident[:, :], ident_in), (ident_bf[:, :], ident_bf_in), (mask_q[:, :], mask_q_in),
                  (mask_k[:, :], mask_k_in)]

        for layer in range(2):
            ctx, sb, ps, sems = phase()
            with ctx:
                if layer == 0:
                    project(nc, sb, ps, sems, "A", xs[0], ident, {"q": w_q, "k": w_k, "v": w_v}, out0, consts)
                else:
                    project(nc, sb, ps, sems, "F", xs[2], ident, {"qkv": wqkv}, out1)
            if stop <= 4 * layer + 1:
                break
            with ExitStack() as kept:
                tag = "BG"[layer]
                oT = kept.enter_context(nc.sbuf_tensor(f"oT{tag}", [P, ITS, 2, HALF], F32))

                def ot(it, half):
                    if isinstance(it, int):
                        return oT[:, it, half, :]
                    return oT[:, bass.ds(it, 1), half, :].rearrange("p a t -> p (a t)")

                def heads_q(c, it, half):
                    v = q_parts[layer].rearrange("c i (h d) (f t) -> c i f d h t", d=HD, f=2)
                    return v[c, one(it), half].rearrange("i d h t -> (i d) h t")

                def heads_k(c, it):
                    if layer:
                        return k_parts[1][c, one(it // NG)].rearrange("b d (h t) -> (b d) h t", h=1)
                    v = k_parts[0].rearrange("c i (h d) t -> c i d h t", d=HD)
                    return v[c, one(it)].rearrange("i d h t -> (i d) h t")

                def v_of(it):
                    return v_rows[layer][one(it // NG if layer else it)].rearrange("i p k c -> (i p) k c")

                def bias_q(it, half):
                    return bias_q_in[one(it % NG), :, half].rearrange("i r h t -> (i r) h t")

                ctx, sb, ps, sems = phase()
                with ctx:
                    attention(nc, sb, ps, sems, tag, layer == 1, heads_q, heads_k, v_of, ot, ident, ident_bf,
                              mask_q, mask_k, fixed_k, bias_q)
                ctx, sb, ps, sems = phase()

                def o_tile(b, g, q):
                    return oT[:, b * NG + g, q // QT, (q % QT) * P:(q % QT + 1) * P]

                with ctx:
                    output(nc, sb, ps, sems, "CH"[layer], xs[2 * layer], xs[2 * layer + 1], ident, o_tile, (w_o, wo1)[layer])
            if stop <= 4 * layer + 2:
                break
            ctx, sb, ps, sems = phase()
            with ctx:
                if layer == 0:
                    gated_ffn(nc, sb, ps, sems, "D", xs[1], xs[2], ident, gate_w, gate_s, up_w, up_s, down_w, down_s)
                else:
                    adapter_ffn(nc, sb, ps, sems, "I", xs[3], xs[4], ident, w1, b1, a1, bm1, p1)
            if stop <= 4 * layer + 3:
                break
        if stop < 99:
            dump = whole.enter_context(nc.semaphore("dump"))
            with nc.Block() as block:
                @block.sync
                def _(sp):
                    sp.dma_start(out, xs[{2: 1, 3: 2, 6: 3}[stop]]).then_inc(dump, 16)
                    sp.wait_ge(dump, 16)


def shape_constants():

    bf = np.dtype("bfloat16")

    def parts(a, n):
        a, out = a.astype(np.float32), []
        for _ in range(n):
            out.append(a.astype(bf))
            a = a - out[-1].astype(np.float32)
        return out

    later = np.arange(P)[None, :] > np.arange(P)[:, None]
    mask_q = np.where(later, np.float32(-1e30), np.float32(0)).astype(bf)
    pos = np.arange(SEQ, dtype=np.float32)
    slopes = (2.0 ** (-0.25 * np.arange(1, HEADS + 1, dtype=np.float64))).astype(np.float32)
    ones = np.ones((HEADS, SEQ), np.float32)
    slope_parts, pos_parts = parts(slopes[:, None] * ones, 3), parts(pos, 2)
    query_parts = parts(-slopes[:, None] * pos[None, :], 3)
    q_rows = np.stack([s for s in slope_parts for _ in pos_parts] + query_parts)
    k_rows = np.stack([p for _ in slope_parts for p in pos_parts] + [np.ones(SEQ, bf)] * (3 + SHIFT))
    bias_q = q_rows.reshape(ALIBI, NG, GH, 2, HALF).transpose(1, 0, 3, 2, 4)
    return {
        "ident": np.eye(P, dtype=np.float32), "ident_bf": np.eye(P).astype(bf), "mask_q": mask_q,
        "mask_k": np.ascontiguousarray(mask_q.T), "fixed_k": k_rows, "bias_q": np.ascontiguousarray(bias_q),
    }


def kernel(**inputs):
    import concourse.bacc as _bacc
    from concourse.bass_utils import run_bass_kernel_spmd as _run

    a = {k: np.asarray(v) for k, v in inputs.items()}

    def columns(v):
        return np.pad(v.reshape(FF), (0, FT * P - FF)).reshape(FT, P).T

    arrays = {
        "x": a["L0_attn_x"].reshape(TOK, D),
        "w_q": a["L0_attn_w_q"].T, "w_k": a["L0_attn_w_k"].T, "w_v": a["L0_attn_w_v"].T, "w_o": a["L0_attn_w_o"].T,
        "gate_w": a["L0_ffn_gate_w"].T, "gate_s": columns(a["L0_ffn_gate_s"]), "up_w": a["L0_ffn_up_w"].T,
        "up_s": columns(a["L0_ffn_up_s"]), "down_w": a["L0_ffn_down_w"].T,
        "down_s": np.broadcast_to(a["L0_ffn_down_s"].reshape(1, D), (P, D)),
        "wqkv": a["L1_attn_Wqkv"], "wo1": a["L1_attn_Wo"], "w1": a["L1_ffn_W"].T,
        "b1": np.broadcast_to(a["L1_ffn_b"].reshape(1, D), (P, D)),
        "a1": a["L1_ffn_A"].transpose(1, 0, 2).reshape(D, ER), "bm1": a["L1_ffn_B"].reshape(ER, D),
        "p1": np.repeat(a["L1_ffn_p_scores"], ER // 8).reshape(ER, 1),
    }
    arrays.update(shape_constants())
    nc = _bacc.Bacc("TRN2", target_bir_lowering=False, num_devices=1)
    in_map, args = {}, []
    for name, v in arrays.items():
        v = np.ascontiguousarray(v)
        in_map[f"in_{name}"] = v
        args.append(nc.dram_tensor(f"in_{name}", v.shape, mybir.dt.from_np(v.dtype), kind="ExternalInput").ap())
    args.append(nc.dram_tensor("out_0", (TOK, D), F32, kind="ExternalOutput").ap())
    build(nc, *args)
    r = _run(nc, [in_map], core_ids=[0])
    return r.results[0]["out_0"].reshape(BATCH, SEQ, D)
```

```python
from contextlib import ExitStack

import numpy as np

import concourse.bass as bass
from concourse import mybir

F32 = mybir.dt.float32
F32R = mybir.dt.float32r
BF16 = mybir.dt.bfloat16
I32 = mybir.dt.int32
ALU = mybir.AluOpType
ACT = mybir.ActivationFunctionType
AX = mybir.AxisListType

P = 128
BATCH, SEQ, D = 2, 1024, 512
TOK = BATCH * SEQ
NT = TOK // P
DC = D // P
BLK = 512
NB = TOK // BLK
TB = BLK // P
HEADS, HD = 32, 16
GH = 4
NG = HEADS // GH
ITS = BATCH * NG
HALF = 512
KT = SEQ // P
QT = HALF // P
SCALE = HD ** -0.5
FF = 1376
FT = -(-FF // P)
FLAST = FF - (FT - 1) * P
LN_EPS = 1e-5
ER = 128
CLAMP, NORM_EPS = 0.5, 1e-6

Q_PARTS = (0, 0, 0, 1, 1, 2)
K_PARTS = (0, 1, 2, 0, 1, 0)
MAIN = HD * len(Q_PARTS)
ALIBI = 9
SHIFT = 3


def widths(causal, half):
    out = []
    for kt in range(KT):
        first = kt * P - half * HALF
        if causal and first >= HALF:
            break
        diagonal = causal and first >= 0
        out.append((first if diagonal else 0, diagonal))
    return out


def settle(engine, passed):
    engine.sem_inc(passed, 1)


def split_product(pe, out, left, right, start, stop):
    pe.matmul(out, left[0], right[0], start=start, stop=False)
    pe.matmul(out, left[0], right[1], start=False, stop=False)
    return pe.matmul(out, left[1], right[0], start=False, stop=stop)


class Norm:

    def __init__(self, sb, ps, sems, tag, buffers=2, blocks=2):
        self.x = sb(f"x{tag}", [P, blocks, TB, D], F32)
        self.xn = sb(f"xn{tag}", [P, TB, D], F32)
        self.high = sb(f"xhT{tag}", [P, buffers, DC, BLK], F32R)
        self.low = sb(f"xlT{tag}", [P, buffers, DC, BLK], F32R)
        self.buffers, self.blocks = buffers, blocks
        self.stats = sb(f"stats{tag}", [P, TB, 6], F32)
        self.mv = sb(f"mv{tag}", [P, TB, 2], F32)
        self.rstd = sb(f"rstd{tag}", [P, TB], F32)
        self.tp = ps(f"tp{tag}", [P, 2, DC, P], F32)
        self.loaded = sems("x_loaded")
        self.summed, self.meaned, self.padded, self.rooted, self.inverted, self.normed = (
            sems(n) for n in ("ln_stats", "ln_mean", "ln_var_eps", "ln_root", "ln_rstd", "ln_out"))
        self.turned, self.high_out, self.ready = sems("xn_turned"), sems("xhT_ready"), sems("xT_ready")

    def parts(self, nb, c, cols=slice(0, BLK)):
        b = nb % self.buffers
        return self.high[:, b, c, cols], self.low[:, b, c, cols]


def load_block(sp, n, x, nb, free=None):
    if nb:
        sp.wait_ge(n.loaded, 16 * nb)
    if free:
        sp.wait_ge(*free)
    sp.dma_start(n.x[:, nb % n.blocks, :, :], x[BLK * nb:BLK * (nb + 1), :].rearrange("(t p) d -> p t d", p=P)
                 ).then_inc(n.loaded, 16)


def norm_stats(dve, n, nb):
    dve.wait_ge(n.loaded, 16 * (nb + 1))
    for i in range(TB):
        dve.bn_stats(n.stats[:, i, :], n.x[:, nb % n.blocks, i, :]).then_inc(n.summed, 1)
    dve.wait_ge(n.summed, TB * (nb + 1))
    for i in range(TB):
        dve.bn_aggr(n.mv[:, i, :], n.stats[:, i, :]).then_inc(n.meaned, 1)
    dve.wait_ge(n.meaned, TB * (nb + 1))
    dve.tensor_scalar(n.mv[:, :, 1], n.mv[:, :, 1], LN_EPS, None, ALU.add).then_inc(n.padded, 1)


def norm_apply(dve, n, nb):
    dve.wait_ge(n.rooted, nb + 1)
    dve.reciprocal(n.rstd[:, :], n.rstd[:, :]).then_inc(n.inverted, 1)
    dve.wait_ge(n.inverted, nb + 1)
    if nb:
        dve.wait_ge(n.turned, TB * nb)
    for i in range(TB):
        dve.tensor_scalar(n.xn[:, i, :], n.x[:, nb % n.blocks, i, :], n.mv[:, i, 0:1], n.rstd[:, i:i + 1],
                          ALU.subtract, ALU.mult).then_inc(n.normed, 1)


def norm_vector(dve, n, nb):
    norm_stats(dve, n, nb)
    norm_apply(dve, n, nb)


def norm_root(act, n, nb):
    act.wait_ge(n.padded, nb + 1)
    act.activation(n.rstd[:, :], n.mv[:, :, 1], ACT.Sqrt).then_inc(n.rooted, 1)


def norm_turn(pe, n, ident, nb, tiles=range(TB)):
    for i in tiles:
        t = TB * nb + i
        pe.wait_ge(n.normed, t + 1)
        if t >= 2:
            pe.wait_ge(n.ready, t - 1)
        for c in range(DC):
            ins = pe.transpose(n.tp[:, i % 2, c, :], n.xn[:, i, c * P:(c + 1) * P], ident[:, :])
        ins.then_inc(n.turned, 1)


def norm_high(act, n, nb, tiles=range(TB)):
    for i in tiles:
        t = TB * nb + i
        act.wait_ge(n.turned, t + 1)
        act.activation(n.high[:, nb % n.buffers, :, i * P:(i + 1) * P], n.tp[:, i % 2, :, :],
                       ACT.Copy).then_inc(n.high_out, 1)


def norm_low(dve, n, nb, tiles=range(TB)):
    for i in tiles:
        t = TB * nb + i
        dve.wait_ge(n.high_out, t + 1)
        cols = slice(i * P, (i + 1) * P)
        dve.tensor_tensor(n.low[:, nb % n.buffers, :, cols], n.tp[:, i % 2, :, :],
                          n.high[:, nb % n.buffers, :, cols].bitcast(F32), ALU.subtract).then_inc(n.ready, 1)


class Weights:

    def __init__(self, sb, sems, tag, aps):
        self.raw, self.high, self.low, self.order = {}, {}, {}, list(aps)
        self.aps = aps
        self.chunks = {k: ap.shape[0] // P for k, ap in aps.items()}
        self.loaded = {k: sems(f"{k}_loaded") for k in aps}
        self.high_out, self.ready = sems("weights_high"), sems("weights_ready")
        for k, ap in aps.items():
            shape = [P, ap.shape[0] // P, ap.shape[1]]
            self.raw[k] = sb(f"{k}_raw{tag}", shape, F32)
            self.high[k], self.low[k] = (sb(f"{k}_{x}{tag}", shape, F32R) for x in ("high", "low"))

    def load(self, sp):
        for k, ap in self.aps.items():
            sp.dma_start(self.raw[k][:, :, :], ap.rearrange("(c p) e -> p c e", p=P)).then_inc(self.loaded[k], 16)

    def split_high(self, act, keys):
        for k in keys:
            act.wait_ge(self.loaded[k], 16)
            for c in range(self.chunks[k]):
                act.activation(self.high[k][:, c, :], self.raw[k][:, c, :], ACT.Copy).then_inc(self.high_out, 1)

    def split_low(self, dve, keys):
        for k in keys:
            for c in range(self.chunks[k]):
                dve.wait_ge(self.high_out, self.count(k) - self.chunks[k] + c + 1)
                dve.tensor_tensor(self.low[k][:, c, :], self.raw[k][:, c, :], self.high[k][:, c, :].bitcast(F32),
                                  ALU.subtract).then_inc(self.ready, 1)

    def count(self, k):
        return sum(self.chunks[o] for o in self.order[:self.order.index(k) + 1])

    def parts(self, k, c, cols):
        return self.high[k][:, c, cols], self.low[k][:, c, cols]


class Residual:

    def __init__(self, sb, sems, tag):
        self.stats = sb(f"ystats{tag}", [P, 6], F32)
        self.mv = sb(f"ymv{tag}", [P, 2], F32)
        self.rstd = sb(f"yrstd{tag}", [P, 1], F32)
        self.yn = sb(f"yn{tag}", [P, 2, D], F32)
        self.summed, self.meaned, self.padded, self.rooted, self.inverted, self.normed, self.added = (
            sems(n) for n in ("y_stats", "y_mean", "y_var_eps", "y_root", "y_rstd", "y_normed", "x_added"))
        self.stored = sems("x_stored")


def residual_vector(dve, r, y, t):
    dve.bn_stats(r.stats[:, :], y).then_inc(r.summed, 1)
    dve.wait_ge(r.summed, t + 1)
    dve.bn_aggr(r.mv[:, :], r.stats[:, :]).then_inc(r.meaned, 1)
    dve.wait_ge(r.meaned, t + 1)
    dve.tensor_scalar(r.mv[:, 1:2], r.mv[:, 1:2], LN_EPS, None, ALU.add).then_inc(r.padded, 1)
    dve.wait_ge(r.rooted, t + 1)
    dve.reciprocal(r.rstd[:, :], r.rstd[:, :]).then_inc(r.inverted, 1)
    dve.wait_ge(r.inverted, t + 1)
    if t >= 2:
        dve.wait_ge(r.added, t - 1)
    dve.tensor_scalar(r.yn[:, t % 2, :], y, r.mv[:, 0:1], r.rstd[:, :], ALU.subtract,
                      ALU.mult).then_inc(r.normed, 1)


def residual_root(act, r, t):
    act.wait_ge(r.padded, t + 1)
    act.activation(r.rstd[:, :], r.mv[:, 1:2], ACT.Sqrt).then_inc(r.rooted, 1)


def residual_add(pool, r, x, t):
    pool.wait_ge(r.normed, t + 1)
    pool.tensor_tensor(x, x, r.yn[:, t % 2, :], ALU.add).then_inc(r.added, 1)


def store_block(sp, r, n, out, nb):
    sp.wait_ge(r.added, TB * (nb + 1))
    if nb:
        sp.wait_ge(r.stored, 16 * nb)
    sp.dma_start(out[BLK * nb:BLK * (nb + 1), :].rearrange("(t p) d -> p t d", p=P), n.x[:, nb % n.blocks, :, :]
                 ).then_inc(r.stored, 16)


def store_last(sp, r, n, out):
    nb = NB - 1
    sp.wait_ge(r.stored, 16 * nb)
    for i in range(TB):
        sp.wait_ge(r.added, TB * nb + i + 1)
        sp.dma_start(out[BLK * nb + P * i:BLK * nb + P * (i + 1), :], n.x[:, nb % n.blocks, i, :]).then_inc(r.stored, 16)
    sp.wait_ge(r.stored, 16 * (nb + TB))


class BlockResidual:

    def __init__(self, sb, sems, tag, buffers=1):
        self.y = sb(f"y{tag}", [P, buffers, TB, D], F32)
        self.stats = sb(f"ystats{tag}", [P, TB, 6], F32)
        self.mv = sb(f"ymv{tag}", [P, TB, 2], F32)
        self.rstd = sb(f"yrstd{tag}", [P, TB], F32)
        self.buffers = buffers
        self.summed, self.meaned, self.padded, self.rooted, self.inverted, self.normed, self.added = (
            sems(n) for n in ("y_stats", "y_mean", "y_var_eps", "y_root", "y_rstd", "y_normed", "x_added"))
        self.stored = sems("x_stored")

    def tile(self, nb, i):
        return self.y[:, nb % self.buffers, i, :]


def block_residual_stats(dve, r, nb, y_ready):
    for i in range(TB):
        y_ready(i)
        dve.bn_stats(r.stats[:, i, :], r.tile(nb, i)).then_inc(r.summed, 1)
    dve.wait_ge(r.summed, TB * (nb + 1))
    for i in range(TB):
        dve.bn_aggr(r.mv[:, i, :], r.stats[:, i, :]).then_inc(r.meaned, 1)
    dve.wait_ge(r.meaned, TB * (nb + 1))
    dve.tensor_scalar(r.mv[:, :, 1], r.mv[:, :, 1], LN_EPS, None, ALU.add).then_inc(r.padded, 1)


def block_residual_root(act, r, nb):
    act.wait_ge(r.padded, nb + 1)
    act.activation(r.rstd[:, :], r.mv[:, :, 1], ACT.Sqrt).then_inc(r.rooted, 1)


def block_residual_apply(dve, r, nb):
    dve.wait_ge(r.rooted, nb + 1)
    dve.reciprocal(r.rstd[:, :], r.rstd[:, :]).then_inc(r.inverted, 1)
    dve.wait_ge(r.inverted, nb + 1)
    for i in range(TB):
        dve.tensor_scalar(r.tile(nb, i), r.tile(nb, i), r.mv[:, i, 0:1], r.rstd[:, i:i + 1],
                          ALU.subtract, ALU.mult).then_inc(r.normed, 1)


def block_residual_add(pool, r, n, nb):
    for i in range(TB):
        pool.wait_ge(r.normed, TB * nb + i + 1)
        x = n.x[:, nb % n.blocks, i, :]
        pool.tensor_tensor(x, x, r.tile(nb, i), ALU.add).then_inc(r.added, 1)


def project(nc, sb, ps, sems, tag, x, ident, w_aps, outputs, constants=()):
    n_out = len(outputs)
    splits = [u for u, o in enumerate(outputs) if o[0] == "split"]
    vs = [u for u, o in enumerate(outputs) if o[0] == "v"]
    ns, nv = len(splits), len(vs)
    assert splits == list(range(ns)) and vs
    n = Norm(sb, ps, sems, tag)
    parts = sb(f"parts{tag}", [P, ns, 3, BLK], BF16)
    rest = sb(f"rest{tag}", [P, ns, BLK], F32)
    turned_v = outputs[vs[0]][4]
    vrows = slice(outputs[vs[0]][2], P)
    vwide = outputs[vs[0]][3] if turned_v else D
    vout = sb(f"vout{tag}", [P, TB, vwide // 2 if turned_v else D], F32)
    vt = sb(f"vt{tag}", [P, BLK], F32) if turned_v else None
    vt_out = sems("v_rows_ready")
    w = Weights(sb, sems, tag, w_aps)
    acc = ps(f"acc_ps{tag}", [P, 6, BLK], F32)
    made = sems("product_made")
    passed = sems("pool_passed")
    hi_out, rest_out, mid_out, low_out = (sems(k) for k in (
        "part0_ready", "rest_ready", "part1_ready", "parts_ready"))
    v_out, const_loaded = sems("v_ready"), sems("constants_loaded")
    stored = [sems(f"stored{i}") for i in range(3)]
    assert n_out % 3 == 0

    def stores(u, nb):
        return stored[u % 3], 16 * (nb * (n_out // 3) + u // 3 + 1)

    def bank_free(u, nb, first):
        if u < 6 and first:
            return None
        q, b = (u - 6, nb) if u >= 6 else (n_out + u - 6, nb - 1)
        return (rest_out, b * ns + splits.index(q) + 1) if q in splits else (v_out, b * nv + vs.index(q) + 1)

    with nc.Block() as block:
        @block.sync
        def _(sp):
            load_block(sp, n, x, 0)
            for dst, src in constants:
                sp.dma_start(dst, src).then_inc(const_loaded, 16)
            w.load(sp)
            load_block(sp, n, x, 1)

            def store(nb, first):
                for u, o in enumerate(outputs):
                    if u in splits:
                        s = splits.index(u)
                        sp.wait_ge(low_out, nb * ns + s + 1)
                        src = parts[o[3]:o[3] + o[4], s, :, :]
                    else:
                        s = vs.index(u)
                        sp.wait_ge(v_out, nb * nv + s + 1)
                        src = vout[:, :, :] if o[4] else vout[:, s, :].rearrange("p (g c) -> p g c", g=NG)
                    if not (first and u < 3):
                        sp.wait_ge(*(stores(u - 3, nb) if u >= 3 else stores(n_out + u - 3, nb - 1)))
                    sp.dma_start(o[-1](nb, s), src).then_inc(stored[u % 3], 16)

            for nb in range(NB):
                if nb + 2 < NB:
                    load_block(sp, n, x, nb + 2, (n.normed, TB * (nb + 1)))
                store(nb, nb == 0)
            for u in range(n_out - 3, n_out):
                sp.wait_ge(*stores(u, NB - 1))

        @block.vector
        def _(dve):
            def rests(nb, which):
                for s in which:
                    u = splits[s]
                    o = outputs[u]
                    rows = slice(o[3], o[3] + o[4])
                    dve.wait_ge(hi_out, nb * ns + s + 1)
                    if nb:
                        dve.wait_ge(low_out, (nb - 1) * ns + s + 1)
                    dve.scalar_tensor_tensor(out=rest[rows, s, :], in0=acc[rows, u % 6, :], scalar=o[5],
                                             in1=parts[rows, s, 0, :], op0=ALU.mult, op1=ALU.subtract
                                             ).then_inc(rest_out, 1)

            norm_vector(dve, n, 0)
            w.split_low(dve, w.order[:1])
            norm_low(dve, n, 0)
            w.split_low(dve, w.order[1:])
            for nb in range(NB):
                if nb < NB - 1:
                    norm_vector(dve, n, nb + 1)
                rests(nb, range(0, 4))
                if nb < NB - 1:
                    norm_low(dve, n, nb + 1)
                rests(nb, range(4, ns))

        @block.gpsimd
        def _(pool):
            with pool.Fori(0, NB) as nb:
                for s, u in enumerate(splits):
                    o = outputs[u]
                    rows = slice(o[3], o[3] + o[4])
                    if o[4] < P and s:
                        pool.wait_ge(low_out, nb * ns + s)
                        settle(pool, passed)
                    pool.wait_ge(mid_out, nb * ns + s + 1)
                    pool.tensor_tensor(parts[rows, s, 2, :], rest[rows, s, :], parts[rows, s, 1, :],
                                       ALU.subtract).then_inc(low_out, 1)
                    if o[4] < P:
                        pool.wait_ge(low_out, nb * ns + s + 1)
                        settle(pool, passed)
                if outputs[splits[0]][4] < P:
                    pool.wait_ge(low_out, nb * ns + ns)
                    settle(pool, passed)

        @block.scalar
        def _(act):
            def copies(nb, us, first):
                for u in us:
                    o = outputs[u]
                    act.wait_ge(made, nb * n_out + u + 1)
                    if not first:
                        act.wait_ge(*stores(u, nb - 1))
                    if turned_v and u == 0:
                        if not first:
                            act.wait_ge(made, nb * n_out)
                        act.activation(vt[vrows, :], acc[vrows, u % 6, :], ACT.Copy).then_inc(vt_out, 1)
                    if u in splits:
                        rows = slice(o[3], o[3] + o[4])
                        act.activation(parts[rows, splits.index(u), 0, :], acc[rows, u % 6, :], ACT.Copy,
                                       scale=o[5]).then_inc(hi_out, 1)
                    elif o[4]:
                        act.activation(vout[:, :, :], acc[:, u % 6, 0:TB * vwide].rearrange(
                            "p (t c) -> p t c", t=TB)[:, :, vwide // 2:], ACT.Copy).then_inc(v_out, 1)
                    else:
                        act.activation(vout[:, vs.index(u), :], acc[:, u % 6, :], ACT.Copy).then_inc(v_out, 1)
                    if 0 < u <= ns:
                        rows = slice(outputs[u - 1][3], outputs[u - 1][3] + outputs[u - 1][4])
                        act.wait_ge(rest_out, nb * ns + u)
                        act.activation(parts[rows, u - 1, 1, :], rest[rows, u - 1, :], ACT.Copy).then_inc(mid_out, 1)

            norm_root(act, n, 0)
            w.split_high(act, w.order[:1])
            norm_high(act, n, 0)
            w.split_high(act, w.order[1:])
            for nb in range(NB):
                if nb < NB - 1:
                    norm_root(act, n, nb + 1)
                copies(nb, range(0, 4), nb == 0)
                if nb < NB - 1:
                    norm_high(act, n, nb + 1)
                copies(nb, range(4, n_out), nb == 0)

        @block.tensor
        def _(pe):
            def products(nb, us, first):
                for u in us:
                    o = outputs[u]
                    if first:
                        pe.wait_ge(w.ready, w.count(o[1]))
                    old = bank_free(u, nb, first)
                    if old:
                        pe.wait_ge(*old)
                    bank = acc[:, u % 6, :]
                    if turned_v and u == 0 and not first:
                        pe.wait_ge(vt_out, nb)
                    if o[4] and u in vs:
                        pe.wait_ge(vt_out, nb + 1)
                        for t in range(TB):
                            ins = pe.transpose(bank[:, t * vwide:(t + 1) * vwide], vt[vrows, t * P:(t + 1) * P],
                                               ident[vrows, vrows])
                    elif u in splits:
                        for c in range(DC):
                            ins = split_product(pe, bank, w.parts(o[1], c, slice(o[2], o[2] + P)), n.parts(nb, c),
                                                c == 0, c == DC - 1)
                    else:
                        t = vs.index(u)
                        for c in range(DC):
                            ins = split_product(pe, bank, n.parts(nb, c, slice(t * P, (t + 1) * P)),
                                                w.parts(o[1], c, slice(o[2], o[2] + o[3])), c == 0, c == DC - 1)
                    ins.then_inc(made, 1)

            if constants:
                pe.wait_ge(const_loaded, 16 * len(constants))
            norm_turn(pe, n, ident, 0)
            for nb in range(NB):
                pe.wait_ge(n.ready, TB * (nb + 1))
                products(nb, range(0, 4), nb == 0)
                if nb < NB - 1:
                    norm_turn(pe, n, ident, nb + 1)
                products(nb, range(4, n_out), nb == 0)


def attention(nc, sb, ps, sems, tag, causal, qparts, kparts, vrows, ot, ident, ident_bf, mask_q, mask_k, fixed_k, bias_q):
    bias_rows = ALIBI if causal else 0
    top = MAIN + bias_rows
    rows = top + SHIFT
    kh = 1 if causal else GH
    qst = sb(f"q_stack{tag}", [rows, 3, 2, GH, HALF], BF16)
    kst = sb(f"k_stack{tag}", [rows, 3, kh, SEQ], BF16)
    vload = sb(f"v_load{tag}", [P, KT, kh, HD], F32)
    vone = sb(f"v_ones{tag}", [P, KT, kh, 2 * HD], F32)
    probs = sb(f"probs{tag}", [P, 16, HALF], F32)
    maxes = sb(f"maxes{tag}", [P, 2, GH * QT], F32)
    mrow = sb(f"mrow{tag}", [GH * QT, P], F32)
    mneg = sb(f"mneg{tag}", [GH * QT, P], F32)
    mrest = sb(f"mrest{tag}", [GH * QT, P], F32)
    mparts = sb(f"mparts{tag}", [GH * QT, 3, P], BF16)
    s_ps = ps(f"s_ps{tag}", [P, 2, SEQ], F32)
    st_ps = ps(f"st_ps{tag}", [P, 3, HALF], F32)
    o_ps = ps(f"o_ps{tag}", [P, HALF], F32)

    stacks, v_in, v_set, fixed = sems("stacks_loaded"), sems("v_loaded"), sems("v_spread"), sems("fixed_rows")
    scored, maxed = sems("row_scores_ready"), sems("row_max_ready")
    st_made, st_used = sems("key_scores_ready"), sems("key_scores_used")
    m_neg, m_part0, m_rest, m_part1, m_parts, m_rows = (sems(n) for n in (
        "max_negated", "max_part0", "max_rest", "max_part1", "max_parts_ready", "max_rows_ready"))
    pv_done, o_out = sems("probs_used"), sems("o_copied")
    passed, sp_passed = sems("pool_passed"), sems("sp_passed")

    steps = [(half, kt, *w) for half in range(2) for kt, w in enumerate(widths(causal, half))]
    n_steps = len(steps)
    first_of = [next(i for i, s in enumerate(steps) if s[0] == half) for half in range(2)]
    row_units = [[(half, qt, h) for qt in range(QT) for h in range(GH)] for half in range(2)]
    units_at = [[] for _ in steps]
    for half in range(2):
        mine = [i for i, s in enumerate(steps) if s[0] == half]
        mine = mine[:-1] if causal and half else mine
        for n, unit in enumerate(row_units[half]):
            units_at[mine[n * len(mine) // len(row_units[half])]].append((half * GH * QT + n, *unit))
    turn_at = [f + (0 if causal else 1) for f in first_of]
    takes = []
    for i, s in enumerate(steps):
        takes += [("exp", i, h) for h in range(GH)]
        if i == turn_at[s[0]]:
            takes.append(("max", s[0], 0))
    where = {t: n for n, t in enumerate(takes)}
    n_takes = len(takes)

    def is_last(it, k=1):
        return isinstance(it, int) and it >= ITS - k

    def bank_of(n):
        return n % 3

    skipped = where[("max", 1, 0)]

    def taken(it, n):
        return 1 + n_takes * it + n + 1 - (1 if is_last(it) and n >= skipped else 0)

    def used_before(it, n):
        m = max(x for x in range(-n_takes, n) if bank_of(x % n_takes) == bank_of(n)
                and not (is_last(it) and x == skipped))
        if m < 0:
            return max(1 + n_takes * it + m + 1, 1) if isinstance(it, int) else 1 + n_takes * it + m + 1
        return taken(it, m)

    def max_take(n):
        group, half = n
        if half == 1:
            return taken(group, where[("max", 0, 0)])
        if isinstance(group, int) and group == 0:
            return 1
        return taken(group - 1, where[("max", 1, 0)])

    ring = 4
    n_loads = 16 * (3 * len(Q_PARTS) + (2 if causal else 0))
    loop = range(1, ITS - 3)
    assert len(loop) % 3 == 0 and n_steps % ring == 0

    def run(engine, body):
        body(0, 0, False)
        with engine.Fori(0, len(loop) // 3) as i:
            for r in range(3):
                body(3 * i + 1 + r, (1 + r) % 3, True)
        for it in range(ITS - 3, ITS):
            body(it, it % 3, True)

    def key_width(half, qt):
        return (half * QT + qt + 1) * P if causal else SEQ

    with nc.Block() as block:
        def load_stacks(engine, it, buf, which=range(len(Q_PARTS))):
            for r in which:
                a, b, dst = Q_PARTS[r], K_PARTS[r], slice(HD * r, HD * r + HD)
                for half in range(2):
                    engine.dma_start(qst[dst, buf, half, :, :], qparts(a, it, half)).then_inc(stacks, 16)
                engine.dma_start(kst[dst, buf, :, :], kparts(b, it)).then_inc(stacks, 16)
            if causal and which[0] == 0:
                for half in range(2):
                    engine.dma_start(qst[MAIN:top, buf, half, :, :], bias_q(it, half)).then_inc(stacks, 16)

        @block.sync
        def _(sp):
            def load_v(it):
                sp.dma_start(vload[:, :, :, :].rearrange("p k h d -> p k (h d)"), vrows(it)).then_inc(v_in, 16)

            def max_rows(n, half, buf):
                sp.wait_ge(m_parts, n + 1)
                for p in range(SHIFT):
                    sp.dma_start(qst[top + p:top + p + 1, buf, half, :, :].rearrange(
                        "r h (q c) -> r (h q) c", c=P), mparts[:, p, :]).then_inc(m_rows, 16)

            def body(it, buf, before):
                if before:
                    sp.wait_ge(st_made, 1 + n_takes * it)
                max_rows(2 * it + 1, 1, buf)
                if not is_last(it, 2):
                    sp.wait_ge(stacks, n_loads * (it + 2))
                    settle(sp, sp_passed)
                    load_stacks(sp, it + 2, (buf + 2) % 3)
                if not is_last(it):
                    sp.wait_ge(v_set, it + 2)
                    settle(sp, sp_passed)
                    load_v(it + 1)
                if not is_last(it):
                    max_rows(2 * it + 2, 0, (buf + 1) % 3)

            load_stacks(sp, 0, 0, range(0, 3))
            load_v(0)
            sp.wait_ge(stacks, n_loads)
            load_stacks(sp, 1, 1)
            max_rows(0, 0, 0)
            run(sp, body)
            sp.wait_ge(m_rows, 16 * SHIFT * 2 * ITS)

        @block.gpsimd
        def _(pool):
            def spread(it, before):
                pool.wait_ge(v_in, 16 * (it + 1))
                if before:
                    pool.wait_ge(pv_done, n_steps * it)
                    settle(pool, passed)
                pool.tensor_copy(vone[:, :, :, 0:HD], vload[:, :, :, :]).then_inc(v_set, 1)

            def split_max(n, turned, before):
                pool.wait_ge(st_used, max_take(turned))
                settle(pool, passed)
                pool.tensor_scalar(mneg[:, :], mrow[:, :], -1.0, None, ALU.mult).then_inc(m_neg, 1)
                pool.wait_ge(m_neg, n + 1)
                if before:
                    pool.wait_ge(m_rows, 16 * SHIFT * n)
                    settle(pool, passed)
                pool.tensor_copy(mparts[:, 0, :], mneg[:, :]).then_inc(m_part0, 1)
                pool.wait_ge(m_part0, n + 1)
                pool.tensor_tensor(mrest[:, :], mneg[:, :], mparts[:, 0, :], ALU.subtract).then_inc(m_rest, 1)
                pool.wait_ge(m_rest, n + 1)
                settle(pool, passed)
                pool.tensor_copy(mparts[:, 1, :], mrest[:, :]).then_inc(m_part1, 1)
                pool.wait_ge(m_part1, n + 1)
                pool.tensor_tensor(mparts[:, 2, :], mrest[:, :], mparts[:, 1, :], ALU.subtract).then_inc(m_parts, 1)

            def body(it, before, last):
                spread(it, before)
                split_max(2 * it + 1, (it, 1), True)
                if not last:
                    split_max(2 * it + 2, (it + 1, 0), True)

            pool.dma_start(kst[MAIN:rows, :, :, :].rearrange("r b h t -> r (b h) t"), fixed_k[
                ALIBI - bias_rows:, :].rearrange("r (b t) -> r b t", b=1).broadcast_to([rows - MAIN, 3 * kh, SEQ])
                ).then_inc(fixed, 16)
            pool.memset(vone[:, :, :, :], 1.0).then_inc(v_set, 1)
            pool.wait_ge(v_set, 1)
            split_max(0, (0, 0), False)
            body(0, False, False)
            with pool.Fori(1, ITS - 1) as it:
                body(it, True, False)
            body(ITS - 1, True, True)

        @block.scalar
        def _(act):
            def body(it, before, last):
                for n, (kind, i, h) in enumerate(takes):
                    if kind == "max" and last and i == 1:
                        continue
                    act.wait_ge(st_made, taken(it, n))
                    if kind == "max":
                        act.wait_ge(m_neg, 2 * it + 1 + i)
                        act.activation(mrow[:, :], st_ps[0:GH * QT, bank_of(n), 0:P],
                                       ACT.Copy).then_inc(st_used, 1)
                        continue
                    first = steps[i][2]
                    if h == 0 and (before or i >= ring):
                        act.wait_ge(pv_done, n_steps * it + i - ring + 1)
                    act.activation(probs[:, (i % ring) * GH + h, first:HALF], st_ps[:, bank_of(n), first:HALF],
                                   ACT.Exp).then_inc(st_used, 1)

            load_stacks(act, 0, 0, range(3, len(Q_PARTS)))
            act.wait_ge(st_made, 1)
            act.activation(mrow[:, :], st_ps[0:GH * QT, 2, 0:P], ACT.Copy).then_inc(st_used, 1)
            body(0, False, False)
            with act.Fori(1, ITS - 1) as it:
                body(it, True, False)
            body(ITS - 1, True, True)

        @block.vector
        def _(dve):
            def maximum(group, n, half, qt, h):
                dve.wait_ge(scored, 2 * GH * QT * group + n + 1)
                dve.reduce_max(maxes[:, half, h * QT + qt:h * QT + qt + 1],
                               s_ps[:, n % 2, 0:key_width(half, qt)], AX.X).then_inc(maxed, 1)

            def copy_o(it, half):
                dve.wait_ge(pv_done, n_steps * it + (first_of[1] if half == 0 else n_steps))
                dve.tensor_copy(ot(it, half), o_ps[:, :]).then_inc(o_out, 1)

            def body(it, before, last):
                for i in range(n_steps):
                    for n, half, qt, h in units_at[i] if not last else ():
                        if n == half * GH * QT:
                            dve.wait_ge(st_made, max_take((it, half)))
                        maximum(it + 1, n, half, qt, h)
                    if i == 0 and before:
                        copy_o(it - 1, 1)
                    if i == first_of[1]:
                        copy_o(it, 0)

            for half in range(2):
                for n, (_, qt, h) in enumerate(row_units[half]):
                    maximum(0, half * GH * QT + n, half, qt, h)
            body(0, False, False)
            with dve.Fori(1, ITS - 1) as it:
                body(it, True, False)
            body(ITS - 1, True, True)
            copy_o(ITS - 1, 1)

        @block.tensor
        def _(pe):
            def row_scores(group, buf, n, half, qt, h):
                if not (isinstance(group, int) and group == 0 and n < 2):
                    pe.wait_ge(maxed, 2 * GH * QT * group + n - 1)
                q = qst[0:top, buf, half, h, qt * P:(qt + 1) * P]
                width = key_width(half, qt)
                for a in range(0, width, HALF):
                    b = min(a + HALF, width)
                    masked = causal and b == width
                    ins = pe.matmul(s_ps[:, n % 2, a:b], q, kst[0:top, buf, h % kh, a:b],
                                    start=True, stop=not masked)
                    if masked:
                        ins = pe.matmul(s_ps[:, n % 2, width - P:width], ident_bf[:, :], mask_q[:, :],
                                        start=False, stop=True)
                ins.then_inc(scored, 1)

            def turn_max(group, half, bank):
                pe.wait_ge(maxed, 2 * GH * QT * group + (half + 1) * GH * QT)
                pe.matmul(st_ps[0:GH * QT, bank, 0:P], maxes[:, half, :], ident[:, :],
                          start=True, stop=True).then_inc(st_made, 1)

            def values(it, i):
                half, kt, first, _ = steps[i]
                if i == 0:
                    pe.wait_ge(v_set, it + 2)
                if kt == 0 and not (isinstance(it, int) and it == 0 and half == 0):
                    pe.wait_ge(o_out, 2 * it + half)
                last = i == n_steps - 1 or steps[i + 1][0] != half
                pe.wait_ge(st_used, taken(it, where[("exp", i, GH - 1)]))
                for h in range(GH):
                    ins = pe.matmul(o_ps[32 * h:32 * h + 32, first:HALF], vone[:, kt, h % kh, :],
                                    probs[:, (i % ring) * GH + h, first:HALF], start=kt == 0, stop=last)
                ins.then_inc(pv_done, 1)

            def body(it, buf, before):
                last = is_last(it)
                if not last:
                    pe.wait_ge(stacks, n_loads * (it + 2))
                for i, (half, kt, first, diagonal) in enumerate(steps):
                    if i == first_of[half]:
                        pe.wait_ge(m_rows, 16 * SHIFT * (2 * it + half + 1))
                    units = [] if last else list(units_at[i])
                    spacing = -(-len(units) // 2)
                    for h in range(GH):
                        n = where[("exp", i, h)]
                        pe.wait_ge(st_used, used_before(it, n))
                        bank = st_ps[:, bank_of(n), :]
                        ins = pe.matmul(bank[:, first:HALF], kst[0:rows, buf, h % kh, kt * P:(kt + 1) * P],
                                        qst[0:rows, buf, half, h, first:HALF], start=True, stop=not diagonal)
                        if diagonal:
                            ins = pe.matmul(bank[:, first:first + P], ident_bf[:, :], mask_k[:, :],
                                            start=False, stop=True)
                        ins.then_inc(st_made, 1)
                        if h % 2:
                            for unit in units[:spacing]:
                                row_scores(it + 1, (buf + 1) % 3, *unit)
                            units = units[spacing:]
                    if i == 0 and before:
                        values(it - 1, n_steps - 1)
                    if i > 0:
                        values(it, i - 1)
                    if i == turn_at[half] and not (last and half == 1):
                        n = where[("max", half, 0)]
                        pe.wait_ge(st_used, used_before(it, n))
                        turn_max(it + half, 1 - half, bank_of(n))

            pe.wait_ge(stacks, n_loads)
            pe.wait_ge(v_set, 1)
            pe.wait_ge(fixed, 16)
            for half in range(2):
                for n, (_, qt, h) in enumerate(row_units[half]):
                    row_scores(0, 0, half * GH * QT + n, half, qt, h)
                if half == 0:
                    turn_max(0, 0, 2)
            run(pe, body)
            values(ITS - 1, n_steps - 1)


def output(nc, sb, ps, sems, tag, x, x_out, ident, ot, wo_ap):
    w = Weights(sb, sems, tag, {"wo": wo_ap})
    xt = sb(f"xt{tag}", [P, 2, TB, D], F32)
    recip = sb(f"recip{tag}", [P, HEADS], F32)
    on = sb(f"on{tag}", [P, D], F32)
    onh = sb(f"onhT{tag}", [P, 2, DC, P], F32R)
    onl = sb(f"onlT{tag}", [P, 2, DC, P], F32R)
    r = Residual(sb, sems, tag)
    a_ps = ps(f"a_ps{tag}", [P, 2, NG, P], F32)
    b_ps = ps(f"b_ps{tag}", [P, 2, DC, P], F32)
    y_ps = ps(f"y_ps{tag}", [P, 2, D], F32)
    x_loaded, turned, inverted, scaled = sems("x_loaded"), sems("o_turned"), sems("sums_inverted"), sems("o_scaled")
    back, high_out, ready, made = sems("o_turned_back"), sems("ohT_ready"), sems("oT_ready"), sems("y_made")

    with nc.Block() as block:
        @block.sync
        def _(sp):
            w.load(sp)
            for nb in range(NB + 1):
                if nb < NB:
                    if nb:
                        sp.wait_ge(x_loaded, 16 * nb)
                    if nb >= 2:
                        sp.wait_ge(r.stored, 16 * (nb - 1))
                    sp.dma_start(xt[:, nb % 2, :, :], x[BLK * nb:BLK * (nb + 1), :].rearrange(
                        "(t p) d -> p t d", p=P)).then_inc(x_loaded, 16)
                if nb:
                    sp.wait_ge(r.added, TB * nb)
                    if nb > 1:
                        sp.wait_ge(r.stored, 16 * (nb - 1))
                    sp.dma_start(x_out[BLK * (nb - 1):BLK * nb, :].rearrange("(t p) d -> p t d", p=P),
                                 xt[:, (nb - 1) % 2, :, :]).then_inc(r.stored, 16)
            sp.wait_ge(r.stored, 16 * NB)

        @block.tensor
        def _(pe):
            def turn(t):
                if t >= 2:
                    pe.wait_ge(scaled, t - 1)
                for g in range(NG):
                    ins = pe.transpose(a_ps[:, t % 2, g, :], ot(t // (SEQ // P), g, t % (SEQ // P)), ident[:, :])
                ins.then_inc(turned, 1)

            def turn_back(t):
                pe.wait_ge(scaled, t + 1)
                if t >= 2:
                    pe.wait_ge(ready, t - 1)
                for c in range(DC):
                    ins = pe.transpose(b_ps[:, t % 2, c, :], on[:, c * P:(c + 1) * P], ident[:, :])
                ins.then_inc(back, 1)

            turn(0)
            turn(1)
            turn_back(0)
            for t in range(NT):
                if t < NT - 2:
                    turn(t + 2)
                if t < NT - 1:
                    turn_back(t + 1)
                if t == 0:
                    pe.wait_ge(w.ready, w.count("wo"))
                pe.wait_ge(ready, t + 1)
                if t >= 2:
                    pe.wait_ge(r.normed, t - 1)
                for c in range(DC):
                    ins = split_product(pe, y_ps[:, t % 2, :], (onh[:, t % 2, c, :], onl[:, t % 2, c, :]),
                                        w.parts("wo", c, slice(0, D)), c == 0, c == DC - 1)
                ins.then_inc(made, 1)

        @block.vector
        def _(dve):
            def scale(t):
                dve.wait_ge(turned, t + 1)
                if t:
                    dve.wait_ge(scaled, t)
                sums = a_ps[:, t % 2, :, :].rearrange("p g (h c) -> p (g h) c", h=GH)
                dve.reciprocal(recip[:, :], sums[:, :, HD]).then_inc(inverted, 1)
                dve.wait_ge(inverted, t + 1)
                if t:
                    dve.wait_ge(back, t)
                dve.tensor_tensor(on[:, :].rearrange("p (h c) -> p h c", c=HD), sums[:, :, 0:HD],
                                  recip[:, :].rearrange("p (h a) -> p h a", a=1).broadcast_to([P, HEADS, HD]),
                                  ALU.mult).then_inc(scaled, 1)

            def low(t):
                dve.wait_ge(high_out, t + 1)
                if t >= 2:
                    dve.wait_ge(made, t - 1)
                dve.tensor_tensor(onl[:, t % 2, :, :], b_ps[:, t % 2, :, :], onh[:, t % 2, :, :].bitcast(F32),
                                  ALU.subtract).then_inc(ready, 1)

            scale(0)
            w.split_low(dve, w.order)
            low(0)
            scale(1)
            for t in range(NT):
                if t < NT - 2:
                    scale(t + 2)
                if t < NT - 1:
                    low(t + 1)
                if t:
                    dve.wait_ge(made, t)
                    residual_vector(dve, r, y_ps[:, (t - 1) % 2, :], t - 1)
            dve.wait_ge(made, NT)
            residual_vector(dve, r, y_ps[:, (NT - 1) % 2, :], NT - 1)

        @block.scalar
        def _(act):
            def high(t):
                act.wait_ge(back, t + 1)
                if t >= 2:
                    act.wait_ge(made, t - 1)
                act.activation(onh[:, t % 2, :, :], b_ps[:, t % 2, :, :], ACT.Copy).then_inc(high_out, 1)

            w.split_high(act, w.order)
            high(0)
            for t in range(NT):
                if t < NT - 1:
                    high(t + 1)
                if t:
                    residual_root(act, r, t - 1)
            residual_root(act, r, NT - 1)

        @block.gpsimd
        def _(pool):
            for t in range(NT):
                if t % TB == 0:
                    pool.wait_ge(x_loaded, 16 * (t // TB + 1))
                residual_add(pool, r, xt[:, t // TB % 2, t % TB, :], t)


def gated_ffn(nc, sb, ps, sems, tag, x, x_out, ident, gate_w, gate_s, up_w, up_s, down_w, down_s):
    n, r = Norm(sb, ps, sems, tag, buffers=1), BlockResidual(sb, sems, tag)
    wg, wu = ([sb(f"w{k}_{x_}{tag}", [P, DC, FF], F32R) for x_ in ("high", "low")] for k in "gu")
    wd = [sb(f"wd_{x_}{tag}", [P, FT, D], F32R) for x_ in ("high", "low")]
    sg = sb(f"sg{tag}", [P, FT], F32)
    su = sb(f"su{tag}", [P, FT], F32)
    ds = sb(f"ds{tag}", [P, D], F32)
    silu = sb(f"silu{tag}", [P, BLK], F32)
    h = sb(f"h{tag}", [P, BLK], F32)
    hh = sb(f"hh{tag}", [P, 2, BLK], F32R)
    hl = sb(f"hl{tag}", [P, 2, BLK], F32R)
    g_ps = ps(f"g_ps{tag}", [P, BLK], F32)
    u_ps = ps(f"u_ps{tag}", [P, BLK], F32)
    y_ps = ps(f"y_ps{tag}", [P, TB, D], F32)
    s_loaded, w_high, w_low = sems("scales_loaded"), sems("w_high"), sems("w_low")
    g_made, u_made, silu_out, h_out, hh_out, hl_out, y_made, y_scaled = (sems(k) for k in (
        "gate", "up", "silu_ready", "h_ready", "h_high", "h_low", "y_made", "y_scaled"))
    tile_made = sems("y_tile_made")
    frows = [P] * (FT - 1) + [FLAST]

    pieces, piece_of = [], {}

    def gate_up_piece(j0, j1):
        cols = slice(j0 * P, min(j1 * P, FF))
        for k, w_ap in ((wg, gate_w), (wu, up_w)):
            pieces.append((w_ap.rearrange("(c p) f -> p c f", p=P)[:, :, cols], k[0][:, :, cols], k[1][:, :, cols]))
        piece_of.update({("gu", j): len(pieces) for j in range(j0, j1)})

    def down_piece(j0, j1):
        k = frows[j0]
        src = down_w[j0 * P:min(j1 * P, FF), :].rearrange("(j p) d -> p j d", p=k)
        pieces.append((src, wd[0][0:k, j0:j1, :], wd[1][0:k, j0:j1, :]))
        piece_of.update({("d", j): len(pieces) for j in range(j0, j1)})

    gate_up_piece(0, 1)
    gate_up_piece(1, 3)
    down_piece(0, 1)
    for j in range(1, 9, 2):
        down_piece(j, j + 2)
        gate_up_piece(j + 2, j + 4)
    down_piece(9, 10)
    down_piece(10, FT)
    first, second = (0, 1), (2, 3)
    later = {0: (4, 5), 1: (6, 7), 2: (8,), 3: (9, 10), 4: (11,), 5: (12, 13), 6: (14,), 7: (15, 16), 8: (17,), 9: (18,)}
    assert len(pieces) == 19
    land = sb(f"land{tag}", [P, 2, 2 * D], I32)
    landed = [sems(f"w_landed{i}") for i in range(4)]

    def landing(i):
        rows, middle, cols = pieces[i][1].shape
        slot = i % 4
        room = land[0:rows, slot, :] if slot < 2 else r.y[0:rows, 0, 2 * slot - 4:2 * slot - 2, :].rearrange(
            "p a c -> p (a c)").bitcast(I32)
        return room[:, 0:middle * cols].rearrange("p (m c) -> p m c", m=middle)

    with nc.Block() as block:
        @block.sync
        def _(sp):
            load_block(sp, n, x, 0)
            for i, piece in enumerate(pieces):
                if i >= 4:
                    sp.wait_ge(w_low, i - 3)
                sp.dma_start(landing(i), piece[0]).then_inc(landed[i % 4], 16)
                if i == 1:
                    for dst, src in ((sg, gate_s), (su, up_s), (ds, down_s)):
                        sp.dma_start(dst[:, :], src).then_inc(s_loaded, 16)
                if i == 3:
                    load_block(sp, n, x, 1)
            for nb in range(NB - 1):
                store_block(sp, r, n, x_out, nb)
                if nb + 2 < NB:
                    load_block(sp, n, x, nb + 2, (r.stored, 16 * (nb + 1)))
            store_last(sp, r, n, x_out)

        @block.gpsimd
        def _(pool):
            for nb in range(NB):
                block_residual_add(pool, r, n, nb)

        @block.scalar
        def _(act):
            def high(which):
                for i in which:
                    act.wait_ge(landed[i % 4], 16 * (i // 4 + 1))
                    act.activation(pieces[i][1], landing(i), ACT.Copy).then_inc(w_high, 1)

            norm_root(act, n, 0)
            high(first)
            norm_high(act, n, 0)
            high(second)
            act.wait_ge(s_loaded, 16 * 3)
            for nb in range(NB):
                for j, k in enumerate(frows):
                    c = nb * FT + j
                    act.wait_ge(g_made, c + 1)
                    if c:
                        act.wait_ge(h_out, c)
                    act.activation(silu[0:k, :], g_ps[0:k, :], ACT.Silu, scale=sg[0:k, j:j + 1]).then_inc(silu_out, 1)
                    act.wait_ge(h_out, c + 1)
                    if c >= 2:
                        old_nb, old_j = divmod(c - 2, FT)
                        if old_j == FT - 1:
                            act.wait_ge(tile_made, TB * (old_nb + 1))
                        else:
                            act.wait_ge(y_made, (FT - 1) * old_nb + old_j + 1)
                    act.activation(hh[0:k, c % 2, :], h[0:k, :], ACT.Copy).then_inc(hh_out, 1)
                    if nb == 0:
                        high(later.get(j, ()))
                    if nb and j == 1:
                        block_residual_root(act, r, nb - 1)
                    if nb < NB - 1 and j == 6:
                        norm_root(act, n, nb + 1)
                if nb < NB - 1:
                    norm_high(act, n, nb + 1)
            block_residual_root(act, r, NB - 1)

        @block.vector
        def _(dve):
            def low(which):
                for i in which:
                    dve.wait_ge(w_high, i + 1)
                    dve.tensor_tensor(pieces[i][2], landing(i), pieces[i][1].bitcast(F32),
                                      ALU.subtract).then_inc(w_low, 1)

            norm_stats(dve, n, 0)
            norm_apply(dve, n, 0)
            low(first)
            norm_low(dve, n, 0)
            low(second)
            dve.wait_ge(s_loaded, 16 * 3)
            for nb in range(NB):
                for j, k in enumerate(frows):
                    c = nb * FT + j
                    dve.wait_ge(u_made, c + 1)
                    dve.wait_ge(silu_out, c + 1)
                    if c:
                        dve.wait_ge(hl_out, c)
                    dve.scalar_tensor_tensor(out=h[0:k, :], in0=u_ps[0:k, :], scalar=su[0:k, j:j + 1],
                                             in1=silu[0:k, :], op0=ALU.mult, op1=ALU.mult).then_inc(h_out, 1)
                    dve.wait_ge(hh_out, c + 1)
                    dve.tensor_tensor(hl[0:k, c % 2, :], h[0:k, :], hh[0:k, c % 2, :].bitcast(F32),
                                      ALU.subtract).then_inc(hl_out, 1)
                    if nb == 0:
                        low(later.get(j, ()))
                    if nb and j == 1:
                        block_residual_stats(dve, r, nb - 1, lambda i: None)
                    if nb and j == 2:
                        block_residual_apply(dve, r, nb - 1)
                    if nb < NB - 1 and j == 6:
                        norm_stats(dve, n, nb + 1)
                    if nb < NB - 1 and j == 8:
                        norm_apply(dve, n, nb + 1)
                if nb < NB - 1:
                    norm_low(dve, n, nb + 1)
                if nb:
                    dve.wait_ge(r.added, TB * nb)
                for i in range(TB):
                    dve.wait_ge(tile_made, TB * nb + i + 1)
                    dve.tensor_tensor(r.tile(nb, i), y_ps[:, i, :], ds[:, :], ALU.mult).then_inc(y_scaled, 1)
                dve.wait_ge(y_scaled, TB * (nb + 1))
            block_residual_stats(dve, r, NB - 1, lambda i: None)
            block_residual_apply(dve, r, NB - 1)

        @block.tensor
        def _(pe):
            def down(nb, j):
                k, c = frows[j], nb * FT + j
                if nb == 0:
                    pe.wait_ge(w_low, piece_of["d", j])
                pe.wait_ge(hl_out, c + 1)
                if nb and j == 0:
                    pe.wait_ge(y_scaled, TB * nb)
                for i in range(TB):
                    cols = slice(i * P, (i + 1) * P)
                    ins = split_product(pe, y_ps[:, i, :], (hh[0:k, c % 2, cols], hl[0:k, c % 2, cols]),
                                        (wd[0][0:k, j, :], wd[1][0:k, j, :]), j == 0, j == FT - 1)
                    if j == FT - 1:
                        ins.then_inc(tile_made, 1)
                if j < FT - 1:
                    ins.then_inc(y_made, 1)

            norm_turn(pe, n, ident, 0)
            for nb in range(NB):
                pe.wait_ge(n.ready, TB * (nb + 1))
                for j, k in enumerate(frows):
                    c = nb * FT + j
                    for w, bank, old, made in ((wg, g_ps, silu_out, g_made), (wu, u_ps, h_out, u_made)):
                        if c:
                            pe.wait_ge(old, c)
                        if nb == 0:
                            pe.wait_ge(w_low, piece_of["gu", j])
                        for d in range(DC):
                            cols = slice(j * P, j * P + k)
                            ins = split_product(pe, bank[0:k, :], (w[0][:, d, cols], w[1][:, d, cols]),
                                                n.parts(nb, d), d == 0, d == DC - 1)
                        ins.then_inc(made, 1)
                    if j == FT - 1 and nb < NB - 1:
                        norm_turn(pe, n, ident, nb + 1, range(0, 2))
                    if j:
                        down(nb, j - 1)
                if nb < NB - 1:
                    norm_turn(pe, n, ident, nb + 1, range(2, TB))
                down(nb, FT - 1)


def adapter_ffn(nc, sb, ps, sems, tag, x, out, ident, w_ap, b_ap, a_ap, bm_ap, p_ap):
    n, r = Norm(sb, ps, sems, tag, blocks=NB), BlockResidual(sb, sems, tag, buffers=2)
    w = Weights(sb, sems, tag, {"a": a_ap, "w": w_ap, "bm": bm_ap})
    bias = sb(f"bias{tag}", [P, D], F32)
    scores = sb(f"scores{tag}", [ER, 1], F32)
    uT = sb(f"uT{tag}", [ER, BLK], F32)
    uh = sb(f"uhT{tag}", [ER, 2, BLK], F32R)
    ul = sb(f"ulT{tag}", [ER, 2, BLK], F32R)
    m = sb(f"m{tag}", [P, 2, TB, D], F32)
    square = sb(f"square{tag}", [P, 2, D], F32)
    norms = sb(f"norms{tag}", [P, 2, 2, TB], F32)
    gamma = sb(f"gamma{tag}", [P, 3, TB], F32)
    u_ps = ps(f"u_ps{tag}", [ER, BLK], F32)
    z_ps = ps(f"z_ps{tag}", [P, 2, D], F32)
    m_ps = ps(f"m_ps{tag}", [P, 2, D], F32)
    c_loaded, u_made, u_scaled, uh_out, u_out, z_made, m_made, z_out, m_out = (sems(k) for k in (
        "bias_loaded", "u_made", "u_scaled", "uh_ready", "uT_ready", "z_made", "m_made", "z_ready", "m_ready"))
    z_squared, m_squared, roots, g_steps, joined = (sems(k) for k in (
        "z_squared", "m_squared", "norms_ready", "gamma_steps", "y_ready"))

    with nc.Block() as block:
        @block.sync
        def _(sp):
            load_block(sp, n, x, 0)
            w.load(sp)
            sp.dma_start(bias[:, :], b_ap).then_inc(c_loaded, 16)
            sp.dma_start(scores[:, :], p_ap).then_inc(c_loaded, 16)
            load_block(sp, n, x, 1)
            load_block(sp, n, x, 2)
            load_block(sp, n, x, 3)
            for nb in range(NB - 1):
                store_block(sp, r, n, out, nb)
            store_last(sp, r, n, out)

        @block.gpsimd
        def _(pool):
            for nb in range(NB):
                block_residual_add(pool, r, n, nb)

        @block.scalar
        def _(act):
            norm_root(act, n, 0)
            w.split_high(act, ["a"])
            norm_high(act, n, 0)
            w.split_high(act, ["w", "bm"])
            act.wait_ge(c_loaded, 16 * 2)
            for nb in range(NB):
                act.wait_ge(u_made, nb + 1)
                if nb:
                    act.wait_ge(u_out, nb)
                act.activation(uT[:, :], u_ps[:, :], ACT.Copy, scale=scores[:, 0:1]).then_inc(u_scaled, 1)
                act.wait_ge(u_scaled, nb + 1)
                if nb >= 2:
                    act.wait_ge(m_made, TB * (nb - 1))
                act.activation(uh[:, nb % 2, :], uT[:, :], ACT.Copy).then_inc(uh_out, 1)
                if nb < NB - 1:
                    norm_root(act, n, nb + 1)
                if nb >= 2:
                    act.wait_ge(g_steps, 4 * (nb - 1))
                for i in range(TB):
                    t = TB * nb + i
                    act.wait_ge(z_out, t + 1)
                    if t:
                        act.wait_ge(z_squared, t)
                    act.activation(square[:, 0, :], r.tile(nb, i), ACT.Square,
                                   accum_out=norms[:, nb % 2, 0, i:i + 1]).then_inc(z_squared, 1)
                    act.wait_ge(m_made, t + 1)
                    if nb >= 2 and i == 0:
                        act.wait_ge(joined, TB * (nb - 1))
                    act.activation(m[:, nb % 2, i, :], m_ps[:, t % 2, :], ACT.Copy).then_inc(m_out, 1)
                    act.wait_ge(m_out, t + 1)
                    if t:
                        act.wait_ge(m_squared, t)
                    act.activation(square[:, 1, :], m[:, nb % 2, i, :], ACT.Square,
                                   accum_out=norms[:, nb % 2, 1, i:i + 1]).then_inc(m_squared, 1)
                    if i in (1, 2) and nb < NB - 1:
                        norm_high(act, n, nb + 1, range(2 * i - 2, 2 * i))
                    if i == 2 and nb:
                        block_residual_root(act, r, nb - 1)
                act.wait_ge(z_squared, TB * (nb + 1))
                act.wait_ge(m_squared, TB * (nb + 1))
                act.activation(norms[:, nb % 2, :, :], norms[:, nb % 2, :, :], ACT.Sqrt).then_inc(roots, 1)
            block_residual_root(act, r, NB - 1)

        @block.vector
        def _(dve):
            def join(nb):
                dve.wait_ge(roots, nb + 1)
                dve.tensor_scalar(gamma[:, 0, :], norms[:, nb % 2, 1, :], NORM_EPS, None, ALU.add).then_inc(g_steps, 1)
                dve.wait_ge(g_steps, 4 * nb + 1)
                dve.reciprocal(gamma[:, 1, :], gamma[:, 0, :]).then_inc(g_steps, 1)
                dve.wait_ge(g_steps, 4 * nb + 2)
                dve.scalar_tensor_tensor(out=gamma[:, 2, :], in0=norms[:, nb % 2, 0, :], scalar=CLAMP,
                                         in1=gamma[:, 1, :], op0=ALU.mult, op1=ALU.mult).then_inc(g_steps, 1)
                dve.wait_ge(g_steps, 4 * nb + 3)
                dve.tensor_scalar(gamma[:, 2, :], gamma[:, 2, :], 1.0, None, ALU.min).then_inc(g_steps, 1)
                dve.wait_ge(g_steps, 4 * nb + 4)
                for i in range(TB):
                    dve.scalar_tensor_tensor(out=r.tile(nb, i), in0=m[:, nb % 2, i, :], scalar=gamma[:, 2, i:i + 1],
                                             in1=r.tile(nb, i), op0=ALU.mult, op1=ALU.add).then_inc(joined, 1)

            def stats(nb):
                block_residual_stats(dve, r, nb, lambda i: dve.wait_ge(joined, TB * nb + i + 1))

            norm_vector(dve, n, 0)
            w.split_low(dve, ["a"])
            norm_low(dve, n, 0)
            w.split_low(dve, ["w", "bm"])
            dve.wait_ge(c_loaded, 16 * 2)
            for nb in range(NB):
                if nb < NB - 1:
                    norm_stats(dve, n, nb + 1)
                dve.wait_ge(uh_out, nb + 1)
                if nb >= 2:
                    dve.wait_ge(m_made, TB * (nb - 1))
                dve.tensor_tensor(ul[:, nb % 2, :], uT[:, :], uh[:, nb % 2, :].bitcast(F32),
                                  ALU.subtract).then_inc(u_out, 1)
                if nb < NB - 1:
                    norm_apply(dve, n, nb + 1)
                for i in range(TB):
                    t = TB * nb + i
                    dve.wait_ge(z_made, t + 1)
                    if nb >= 2 and i == 0:
                        dve.wait_ge(r.added, TB * (nb - 1))
                    dve.tensor_tensor(r.tile(nb, i), z_ps[:, t % 2, :], bias[:, :], ALU.add).then_inc(z_out, 1)
                    if i == 0 and nb:
                        join(nb - 1)
                    if i == 1 and nb:
                        stats(nb - 1)
                    if i >= 2 and nb < NB - 1:
                        norm_low(dve, n, nb + 1, range(2 * i - 4, 2 * i - 2))
                    if i == 3 and nb:
                        block_residual_apply(dve, r, nb - 1)
            join(NB - 1)
            stats(NB - 1)
            block_residual_apply(dve, r, NB - 1)

        @block.tensor
        def _(pe):
            norm_turn(pe, n, ident, 0)
            for nb in range(NB):
                pe.wait_ge(n.ready, TB * (nb + 1))
                if nb:
                    pe.wait_ge(u_scaled, nb)
                else:
                    pe.wait_ge(w.ready, w.count("a"))
                for c in range(DC):
                    ins = split_product(pe, u_ps[:, :], w.parts("a", c, slice(0, ER)), n.parts(nb, c),
                                        c == 0, c == DC - 1)
                ins.then_inc(u_made, 1)
                if nb == 0:
                    pe.wait_ge(w.ready, w.count("bm"))
                for i in range(TB):
                    t = TB * nb + i
                    cols = slice(i * P, (i + 1) * P)
                    if t >= 2:
                        pe.wait_ge(z_out, t - 1)
                    for c in range(DC):
                        ins = split_product(pe, z_ps[:, t % 2, :], n.parts(nb, c, cols),
                                            w.parts("w", c, slice(0, D)), c == 0, c == DC - 1)
                    ins.then_inc(z_made, 1)
                    pe.wait_ge(u_out, nb + 1)
                    if t >= 2:
                        pe.wait_ge(m_out, t - 1)
                    split_product(pe, m_ps[:, t % 2, :], (uh[:, nb % 2, cols], ul[:, nb % 2, cols]),
                                  w.parts("bm", 0, slice(0, D)), True, True).then_inc(m_made, 1)
                    if i in (1, 2) and nb < NB - 1:
                        norm_turn(pe, n, ident, nb + 1, range(2 * i - 2, 2 * i))


def build(nc, x, w_q, w_k, w_v, w_o, gate_w, gate_s, up_w, up_s, down_w, down_s, wqkv, wo1, w1, b1, a1, bm1,
          p1, ident_in, ident_bf_in, mask_q_in, mask_k_in, fixed_k, bias_q_in, out):
    with ExitStack() as whole:
        xs = [x] + [nc.dram_tensor(f"x{k}", (TOK, D), F32, kind="Internal").ap() for k in range(1, 4)] + [out]
        ident = whole.enter_context(nc.sbuf_tensor("ident", [P, P], F32))
        ident_bf = whole.enter_context(nc.sbuf_tensor("ident_bf", [P, P], BF16))
        mask_q = whole.enter_context(nc.sbuf_tensor("mask_q", [P, P], BF16))
        mask_k = whole.enter_context(nc.sbuf_tensor("mask_k", [P, P], BF16))
        q_parts = [nc.dram_tensor(f"q_parts{l}", (3, ITS, GH * HD, SEQ), BF16, kind="Internal").ap() for l in range(2)]
        k_parts = [nc.dram_tensor("k_parts0", (3, ITS, GH * HD, SEQ), BF16, kind="Internal").ap(),
                   nc.dram_tensor("k_parts1", (3, BATCH, HD, SEQ), BF16, kind="Internal").ap()]
        v_rows = [nc.dram_tensor("v_rows0", (ITS, P, KT, GH * HD), F32, kind="Internal").ap(),
                  nc.dram_tensor("v_rows1", (BATCH, P, KT, HD), F32, kind="Internal").ap()]

        def one(i):
            return slice(i, i + 1) if isinstance(i, int) else bass.ds(i, 1)

        def store_parts(scratch, j):
            def to(nb, s):
                b, th = nb // 2, nb % 2
                v = scratch.rearrange("c (b i) e (h t) -> c b (i e) h t", b=BATCH, h=2)
                return v[:, one(b), j * P:(j + 1) * P, one(th), :].rearrange("c b e h t -> (b e h) c t")
            return to

        def store_k1(nb, s):
            v = k_parts[1].rearrange("c b e (h t) -> c b e h t", h=2)
            return v[:, one(nb // 2), :, one(nb % 2), :].rearrange("c b e h t -> (b e h) c t")

        def store_v0(nb, s):
            v = v_rows[0].rearrange("(b g) p (h k) c -> b h k p g c", b=BATCH, h=2)
            return v[one(nb // 2), one(nb % 2), s].rearrange("b h p g c -> (b h p) g c")

        def store_v1(nb, s):
            v = v_rows[1].rearrange("b p (h k) c -> b h p k c", h=2)
            return v[one(nb // 2), one(nb % 2)].rearrange("b h p k c -> (b h p) k c")

        phases = [0]

        def phase():
            ctx, mine = ExitStack(), []
            phases[0] += 1
            number = phases[0]

            def sb(name, shape, dt):
                return ctx.enter_context(nc.sbuf_tensor(name, shape, dt))

            def ps(name, shape, dt):
                return ctx.enter_context(nc.psum_tensor(name, shape, dt))

            def sems(name):
                mine.append(nc.alloc_semaphore(f"{name}_{number}"))
                return mine[-1]

            def give_back():
                nc.clear_and_free_semaphores(mine)
                nc.all_engine_barrier()

            ctx.callback(give_back)
            return ctx, sb, ps, sems

        out0 = [("split", "q", j * P, 0, P, SCALE, store_parts(q_parts[0], j)) for j in range(DC)]
        out0 += [("split", "k", j * P, 0, P, 1.0, store_parts(k_parts[0], j)) for j in range(DC)]
        out0 += [("v", "v", 0, D, False, store_v0) for _ in range(TB)]
        kv = HEADS * HD + 2 * HD - P
        out1 = [("split", "qkv", kv, P - 2 * HD, HD, 1.0, store_k1)]
        out1 += [("split", "qkv", j * P, 0, P, SCALE, store_parts(q_parts[1], j)) for j in range(DC)]
        out1 += [("v", "qkv", P - 2 * HD, 2 * HD, True, store_v1)]
        consts = [(ident[:, :], ident_in), (ident_bf[:, :], ident_bf_in), (mask_q[:, :], mask_q_in),
                  (mask_k[:, :], mask_k_in)]

        for layer in range(2):
            ctx, sb, ps, sems = phase()
            with ctx:
                if layer == 0:
                    project(nc, sb, ps, sems, "A", xs[0], ident, {"q": w_q, "k": w_k, "v": w_v}, out0, consts)
                else:
                    project(nc, sb, ps, sems, "F", xs[2], ident, {"qkv": wqkv}, out1)
            with ExitStack() as kept:
                tag = "BG"[layer]
                oT = kept.enter_context(nc.sbuf_tensor(f"oT{tag}", [P, ITS, 2, HALF], F32))

                def ot(it, half):
                    if isinstance(it, int):
                        return oT[:, it, half, :]
                    return oT[:, bass.ds(it, 1), half, :].rearrange("p a t -> p (a t)")

                def heads_q(c, it, half):
                    v = q_parts[layer].rearrange("c i (h d) (f t) -> c i f d h t", d=HD, f=2)
                    return v[c, one(it), half].rearrange("i d h t -> (i d) h t")

                def heads_k(c, it):
                    if layer:
                        return k_parts[1][c, one(it // NG)].rearrange("b d (h t) -> (b d) h t", h=1)
                    v = k_parts[0].rearrange("c i (h d) t -> c i d h t", d=HD)
                    return v[c, one(it)].rearrange("i d h t -> (i d) h t")

                def v_of(it):
                    return v_rows[layer][one(it // NG if layer else it)].rearrange("i p k c -> (i p) k c")

                def bias_q(it, half):
                    return bias_q_in[one(it % NG), :, half].rearrange("i r h t -> (i r) h t")

                ctx, sb, ps, sems = phase()
                with ctx:
                    attention(nc, sb, ps, sems, tag, layer == 1, heads_q, heads_k, v_of, ot, ident, ident_bf,
                              mask_q, mask_k, fixed_k, bias_q)
                ctx, sb, ps, sems = phase()

                def o_tile(b, g, q):
                    return oT[:, b * NG + g, q // QT, (q % QT) * P:(q % QT + 1) * P]

                with ctx:
                    output(nc, sb, ps, sems, "CH"[layer], xs[2 * layer], xs[2 * layer + 1], ident, o_tile, (w_o, wo1)[layer])
            ctx, sb, ps, sems = phase()
            with ctx:
                if layer == 0:
                    gated_ffn(nc, sb, ps, sems, "D", xs[1], xs[2], ident, gate_w, gate_s, up_w, up_s, down_w, down_s)
                else:
                    adapter_ffn(nc, sb, ps, sems, "I", xs[3], xs[4], ident, w1, b1, a1, bm1, p1)


def shape_constants():

    bf = np.dtype("bfloat16")

    def parts(a, n):
        a, out = a.astype(np.float32), []
        for _ in range(n):
            out.append(a.astype(bf))
            a = a - out[-1].astype(np.float32)
        return out

    later = np.arange(P)[None, :] > np.arange(P)[:, None]
    mask_q = np.where(later, np.float32(-1e30), np.float32(0)).astype(bf)
    pos = np.arange(SEQ, dtype=np.float32)
    slopes = (2.0 ** (-0.25 * np.arange(1, HEADS + 1, dtype=np.float64))).astype(np.float32)
    ones = np.ones((HEADS, SEQ), np.float32)
    slope_parts, pos_parts = parts(slopes[:, None] * ones, 3), parts(pos, 2)
    query_parts = parts(-slopes[:, None] * pos[None, :], 3)
    q_rows = np.stack([s for s in slope_parts for _ in pos_parts] + query_parts)
    k_rows = np.stack([p for _ in slope_parts for p in pos_parts] + [np.ones(SEQ, bf)] * (3 + SHIFT))
    bias_q = q_rows.reshape(ALIBI, NG, GH, 2, HALF).transpose(1, 0, 3, 2, 4)
    return {
        "ident": np.eye(P, dtype=np.float32), "ident_bf": np.eye(P).astype(bf), "mask_q": mask_q,
        "mask_k": np.ascontiguousarray(mask_q.T), "fixed_k": k_rows, "bias_q": np.ascontiguousarray(bias_q),
    }


def kernel(**inputs):
    import concourse.bacc as _bacc
    from concourse.bass_utils import run_bass_kernel_spmd as _run

    a = {k: np.asarray(v) for k, v in inputs.items()}

    def columns(v):
        return np.pad(v.reshape(FF), (0, FT * P - FF)).reshape(FT, P).T

    arrays = {
        "x": a["L0_attn_x"].reshape(TOK, D),
        "w_q": a["L0_attn_w_q"].T, "w_k": a["L0_attn_w_k"].T, "w_v": a["L0_attn_w_v"].T, "w_o": a["L0_attn_w_o"].T,
        "gate_w": a["L0_ffn_gate_w"].T, "gate_s": columns(a["L0_ffn_gate_s"]), "up_w": a["L0_ffn_up_w"].T,
        "up_s": columns(a["L0_ffn_up_s"]), "down_w": a["L0_ffn_down_w"].T,
        "down_s": np.broadcast_to(a["L0_ffn_down_s"].reshape(1, D), (P, D)),
        "wqkv": a["L1_attn_Wqkv"], "wo1": a["L1_attn_Wo"], "w1": a["L1_ffn_W"].T,
        "b1": np.broadcast_to(a["L1_ffn_b"].reshape(1, D), (P, D)),
        "a1": a["L1_ffn_A"].transpose(1, 0, 2).reshape(D, ER), "bm1": a["L1_ffn_B"].reshape(ER, D),
        "p1": np.repeat(a["L1_ffn_p_scores"], ER // 8).reshape(ER, 1),
    }
    arrays.update(shape_constants())
    nc = _bacc.Bacc("TRN2", target_bir_lowering=False, num_devices=1)
    in_map, args = {}, []
    for name, v in arrays.items():
        v = np.ascontiguousarray(v)
        in_map[f"in_{name}"] = v
        args.append(nc.dram_tensor(f"in_{name}", v.shape, mybir.dt.from_np(v.dtype), kind="ExternalInput").ap())
    args.append(nc.dram_tensor("out_0", (TOK, D), F32, kind="ExternalOutput").ap())
    build(nc, *args)
    r = _run(nc, [in_map], core_ids=[0])
    return r.results[0]["out_0"].reshape(BATCH, SEQ, D)
```
